# Optimizing a Trainium2 kernel written in Bass

```python
import numpy as np
import jax
import jax.numpy as jnp

def _softmax(x, axis=-1):
    return jax.nn.softmax(x, axis=axis)

def _gelu(x):
    return jax.nn.gelu(x, approximate=True)

def _silu(x):
    return jax.nn.silu(x)

def _sigmoid(x):
    return jax.nn.sigmoid(x)

def _layernorm(x, axis=-1, eps=1e-05):
    m = jnp.mean(x, axis=axis, keepdims=True)
    v = jnp.var(x, axis=axis, keepdims=True)
    return (x - m) / jnp.sqrt(v + eps)

def _scatter_add(tgt, idx, src, axis=0):
    return tgt.at[idx].add(src)

def _segment_sum(src, seg, n):
    return jax.ops.segment_sum(src, seg, n)
kernel_name = 'mk_seq_preln_d1_jaxref_r2_e58ca8'

def setup_inputs(seed: int=0):
    np.random.seed(seed)
    _w = jnp.asarray

    def _L0_attn_setup():
        import jax, jax.numpy as jnp
        import numpy as np
        D_MODEL = 512
        D_STATE = 16
        DT_RANK = 64
        DT_MIN, DT_MAX = (0.001, 0.1)

        def _s6(x, A_log, D, x_proj_w, dt_proj_w, dt_proj_b):
            A = -jnp.exp(A_log)
            xp = jnp.einsum('bld,ed->ble', x, x_proj_w)
            d_rank = xp[..., :DT_RANK]
            Bm = xp[..., DT_RANK:DT_RANK + D_STATE]
            Cm = xp[..., DT_RANK + D_STATE:]
            delta = jax.nn.softplus(jnp.einsum('blr,dr->bld', d_rank, dt_proj_w) + dt_proj_b)
            deltaA = jnp.exp(jnp.einsum('bld,dn->bldn', delta, A))
            deltaB_u = jnp.einsum('bld,bln,bld->bldn', delta, Bm, x)

            def step(h, inp):
                dA_t, dBu_t, C_t = inp
                h = dA_t * h + dBu_t
                y = jnp.einsum('bdn,bn->bd', h, C_t)
                return (h, y)
            b, l, d = x.shape
            h0 = jnp.zeros((b, d, D_STATE), x.dtype)
            _, ys = jax.lax.scan(step, h0, (deltaA.transpose(1, 0, 2, 3), deltaB_u.transpose(1, 0, 2, 3), Cm.transpose(1, 0, 2)))
            y = ys.transpose(1, 0, 2) + x * D
            return y
        key = jax.random.key(seed)
        ks = jax.random.split(key, 6)
        x = jax.random.normal(ks[0], (2, 1024, D_MODEL), jnp.float32)
        A_log = jax.random.normal(ks[1], (D_MODEL, D_STATE), jnp.float32)
        D = jax.random.normal(ks[2], (D_MODEL,), jnp.float32)
        x_proj_w = jax.random.normal(ks[3], (DT_RANK + 2 * D_STATE, D_MODEL), jnp.float32) * D_MODEL ** (-0.5)
        dt_init_std = DT_RANK ** (-0.5)
        dt_proj_w = jax.random.uniform(ks[4], (D_MODEL, DT_RANK), jnp.float32, -dt_init_std, dt_init_std)
        dt = jnp.exp(jax.random.uniform(ks[5], (D_MODEL,), jnp.float32) * (np.log(DT_MAX) - np.log(DT_MIN)) + np.log(DT_MIN))
        dt_proj_b = dt + jnp.log(-jnp.expm1(-dt))
        return {'x': x, 'A_log': A_log, 'D': D, 'x_proj_w': x_proj_w, 'dt_proj_w': dt_proj_w, 'dt_proj_b': dt_proj_b}
    _L0_attn_in = _L0_attn_setup()

    def _L0_ffn_setup():
        import jax, jax.numpy as jnp
        import numpy as np
        B, S, D, H, F = (4, 2048, 512, 16, 2048)
        CAP = 0.125
        ROPE_BASE = 10000.0

        def rmsnorm(x, g):
            return x * jax.lax.rsqrt(jnp.mean(x * x, -1, keepdims=True) + 1e-06) * g

        def rope(t, pos):
            hd = t.shape[-1]
            inv = 1.0 / ROPE_BASE ** (jnp.arange(0, hd, 2, dtype=jnp.float32) / hd)
            f = pos[:, None, :, None].astype(jnp.float32) * inv
            emb = jnp.concatenate([f, f], axis=-1)
            cos, sin = (jnp.cos(emb), jnp.sin(emb))
            rot = jnp.concatenate([-t[..., hd // 2:], t[..., :hd // 2]], axis=-1)
            return t * cos + rot * sin
        key = jax.random.key(seed)
        ks = jax.random.split(key, 9)
        scale = 0.02
        x = jax.random.normal(ks[0], (B, S, D), jnp.float32)
        causal = jnp.where(jnp.tril(jnp.ones((S, S), bool)), 0.0, -1000000000.0).astype(jnp.float32)
        attention_mask = jnp.broadcast_to(causal[None, None], (B, 1, S, S))
        position_ids = jnp.broadcast_to(jnp.arange(S, dtype=jnp.int32), (B, S))
        return {'x': x, 'attention_mask': attention_mask, 'position_ids': position_ids, 'router_w': jax.random.normal(ks[1], (D, 1), jnp.float32) * scale, 'router_b': jnp.zeros((1,), jnp.float32), 'wq': jax.random.normal(ks[2], (D, D), jnp.float32) * scale, 'wk': jax.random.normal(ks[3], (D, D), jnp.float32) * scale, 'wv': jax.random.normal(ks[4], (D, D), jnp.float32) * scale, 'wo': jax.random.normal(ks[5], (D, D), jnp.float32) * scale, 'w1': jax.random.normal(ks[6], (D, F), jnp.float32) * scale, 'w2': jax.random.normal(ks[7], (F, D), jnp.float32) * scale, 'ln1': jnp.ones((D,), jnp.float32), 'ln2': jnp.ones((D,), jnp.float32)}
    _L0_ffn_in = _L0_ffn_setup()
    _d = {'L0_attn_x': _L0_attn_in['x'], 'L0_attn_A_log': _L0_attn_in['A_log'], 'L0_attn_D': _L0_attn_in['D'], 'L0_attn_x_proj_w': _L0_attn_in['x_proj_w'], 'L0_attn_dt_proj_w': _L0_attn_in['dt_proj_w'], 'L0_attn_dt_proj_b': _L0_attn_in['dt_proj_b'], 'L0_ffn_attention_mask': _L0_ffn_in['attention_mask'], 'L0_ffn_position_ids': _L0_ffn_in['position_ids'], 'L0_ffn_router_w': _L0_ffn_in['router_w'], 'L0_ffn_router_b': _L0_ffn_in['router_b'], 'L0_ffn_wq': _L0_ffn_in['wq'], 'L0_ffn_wk': _L0_ffn_in['wk'], 'L0_ffn_wv': _L0_ffn_in['wv'], 'L0_ffn_wo': _L0_ffn_in['wo'], 'L0_ffn_w1': _L0_ffn_in['w1'], 'L0_ffn_w2': _L0_ffn_in['w2'], 'L0_ffn_ln1': _L0_ffn_in['ln1'], 'L0_ffn_ln2': _L0_ffn_in['ln2']}
    _x0 = _d['L0_attn_x']
    _d['L0_attn_x'] = jax.random.normal(jax.random.fold_in(jax.random.key(seed), 1), (16, 1024, 512), dtype=_x0.dtype)
    del _x0
    return _d

def reference(L0_attn_x, L0_attn_A_log, L0_attn_D, L0_attn_x_proj_w, L0_attn_dt_proj_w, L0_attn_dt_proj_b, L0_ffn_attention_mask, L0_ffn_position_ids, L0_ffn_router_w, L0_ffn_router_b, L0_ffn_wq, L0_ffn_wk, L0_ffn_wv, L0_ffn_wo, L0_ffn_w1, L0_ffn_w2, L0_ffn_ln1, L0_ffn_ln2):

    def _L0_attn_ref(x, A_log, D, x_proj_w, dt_proj_w, dt_proj_b):
        import jax, jax.numpy as jnp
        import numpy as np
        D_MODEL = 512
        D_STATE = 16
        DT_RANK = 64
        DT_MIN, DT_MAX = (0.001, 0.1)

        def _s6(x, A_log, D, x_proj_w, dt_proj_w, dt_proj_b):
            A = -jnp.exp(A_log)
            xp = jnp.einsum('bld,ed->ble', x, x_proj_w)
            d_rank = xp[..., :DT_RANK]
            Bm = xp[..., DT_RANK:DT_RANK + D_STATE]
            Cm = xp[..., DT_RANK + D_STATE:]
            delta = jax.nn.softplus(jnp.einsum('blr,dr->bld', d_rank, dt_proj_w) + dt_proj_b)
            deltaA = jnp.exp(jnp.einsum('bld,dn->bldn', delta, A))
            deltaB_u = jnp.einsum('bld,bln,bld->bldn', delta, Bm, x)

            def step(h, inp):
                dA_t, dBu_t, C_t = inp
                h = dA_t * h + dBu_t
                y = jnp.einsum('bdn,bn->bd', h, C_t)
                return (h, y)
            b, l, d = x.shape
            h0 = jnp.zeros((b, d, D_STATE), x.dtype)
            _, ys = jax.lax.scan(step, h0, (deltaA.transpose(1, 0, 2, 3), deltaB_u.transpose(1, 0, 2, 3), Cm.transpose(1, 0, 2)))
            y = ys.transpose(1, 0, 2) + x * D
            return y
        return _s6(x, A_log, D, x_proj_w, dt_proj_w, dt_proj_b)

    def _L0_ffn_ref(x, attention_mask, position_ids, router_w, router_b, wq, wk, wv, wo, w1, w2, ln1, ln2):
        import jax, jax.numpy as jnp
        import numpy as np
        B, S, D, H, F = (4, 2048, 512, 16, 2048)
        CAP = 0.125
        ROPE_BASE = 10000.0

        def rmsnorm(x, g):
            return x * jax.lax.rsqrt(jnp.mean(x * x, -1, keepdims=True) + 1e-06) * g

        def rope(t, pos):
            hd = t.shape[-1]
            inv = 1.0 / ROPE_BASE ** (jnp.arange(0, hd, 2, dtype=jnp.float32) / hd)
            f = pos[:, None, :, None].astype(jnp.float32) * inv
            emb = jnp.concatenate([f, f], axis=-1)
            cos, sin = (jnp.cos(emb), jnp.sin(emb))
            rot = jnp.concatenate([-t[..., hd // 2:], t[..., :hd // 2]], axis=-1)
            return t * cos + rot * sin
        b, s, d = x.shape
        hd = d // H
        weights = (x @ router_w)[..., 0] + router_b[0]
        k = int(CAP * s)
        topv, topi = jax.lax.top_k(weights, k)
        thr = topv[:, -1]
        sel_mask = (weights > thr[:, None]).astype(x.dtype)
        kc = k - 1
        sel_idx = jnp.sort(topi[:, :kc], axis=1)
        bidx = jnp.arange(b)[:, None]
        x_sel = x[bidx, sel_idx]
        pos_sel = position_ids[bidx, sel_idx]
        w_sel = weights[bidx, sel_idx]
        m = attention_mask[:, 0]
        m_sel = m[bidx[:, :, None], sel_idx[:, :, None], sel_idx[:, None, :]]
        hn = rmsnorm(x_sel, ln1)

        def heads(t):
            return t.reshape(b, kc, H, hd).transpose(0, 2, 1, 3)
        q = rope(heads(hn @ wq), pos_sel)
        kk = rope(heads(hn @ wk), pos_sel)
        v = heads(hn @ wv)
        sc = jnp.einsum('bhqd,bhkd->bhqk', q, kk) / np.sqrt(hd).astype(np.float32)
        sc = sc + m_sel[:, None]
        a = jax.nn.softmax(sc, axis=-1)
        o = jnp.einsum('bhqk,bhkd->bhqd', a, v).transpose(0, 2, 1, 3).reshape(b, kc, d) @ wo
        x1 = x_sel + o
        x2 = x1 + jax.nn.gelu(rmsnorm(x1, ln2) @ w1) @ w2
        proc = x2 * w_sel[..., None]
        out = jnp.zeros_like(x).at[bidx, sel_idx].set(proc)
        return out + x * (1.0 - sel_mask)[..., None]
    x = L0_attn_x
    x = x + _L0_attn_ref(_layernorm(x, axis=-1), L0_attn_A_log, L0_attn_D, L0_attn_x_proj_w, L0_attn_dt_proj_w, L0_attn_dt_proj_b)
    x = x + _L0_ffn_ref(_layernorm(x, axis=-1), L0_ffn_attention_mask, L0_ffn_position_ids, L0_ffn_router_w, L0_ffn_router_b, L0_ffn_wq, L0_ffn_wk, L0_ffn_wv, L0_ffn_wo, L0_ffn_w1, L0_ffn_w2, L0_ffn_ln1, L0_ffn_ln2)
    return x

_drawn_inputs = setup_inputs


def setup_inputs(seed=0):
    import zlib

    import numpy as np

    out = dict(_drawn_inputs(seed))
    spreads = {'L0_ffn_ln1': (1.0, 0.6), 'L0_ffn_ln2': (1.0, 0.6)}
    factors = {'L0_ffn_wq': 8.0,
     'L0_ffn_wk': 8.0,
     'L0_ffn_wv': 7.455,
     'L0_ffn_wo': 7.682,
     'L0_ffn_w1': 3.451,
     'L0_ffn_w2': 3.202}
    for name, (base, spread) in spreads.items():
        noise = np.random.default_rng([zlib.crc32(name.encode()), seed]).standard_normal(out[name].shape)
        drawn = base * np.exp(spread * noise) if base else spread * noise
        out[name] = jnp.asarray(drawn.astype(out[name].dtype))
    for name, factor in factors.items():
        out[name] = (out[name] * factor).astype(out[name].dtype)
    return out
```

```python
from contextlib import ExitStack

import numpy as np

import concourse.bass as bass
from concourse import mybir

ALU = mybir.AluOpType
ACT = mybir.ActivationFunctionType
F32 = mybir.dt.float32
BF16 = mybir.dt.bfloat16
I32 = mybir.dt.int32
U32 = mybir.dt.uint32
AX = mybir.AxisListType

P = 128
EPS = 1e-5

B, L, D, N, R = 16, 1024, 512, 16, 64
CH = 32
NT = P // CH
CHUNKS = D // CH
GROUPS = N // NT
TILES = CHUNKS * GROUPS
TC = L // P
KD = D // P
HALF = 512
RING = 4

BC_ORDER = (0, 2, 1, 4, 3, 6, 5, 7)

USES = ([("xhat", t) for t in range(TC)] + [("proj", 0), ("proj", 1)]
        + [("z0", 0), ("z0", 1)] + [("skip", t) for t in range(4)]
        + [("z1", 0), ("z1", 1)] + [("skip", t) for t in range(4, 8)]
        + [("z2", 0), ("z2", 1)]
        + [(f"bc{i}", h) for i in BC_ORDER for h in range(2)]
        + [("z3", 0), ("z3", 1)])
USE = {key: u for u, key in enumerate(USES)}
NUSE = len(USES)
EMPTIED = {("xhat", t): t + 1 for t in range(TC)}
for i, name in enumerate(["proj", "z0", "z1", "z2"] + [f"bc{i}" for i in BC_ORDER] + ["z3"]):
    EMPTIED[(name, 0)] = EMPTIED[(name, 1)] = TC + 1 + i
NEMPTIED = TC + 5 + 2 * GROUPS
LN_VAR = TC + 7
LN1 = LN_VAR + 4
LN2 = LN1 + 2

BC_MADE = (53, 59, 61, 62, 63, 64, 65, 66)
BC_COPIED = (63, 65, 66, 67, 68, 69, 70, 71)


def scan_phase(nc, semaphores, x, A_log, w_xproj, w_dt, dt_b, D_col, router_w, router_b, ident_c, nsum_c, rep_c, bc_c,
               x1_dram, w_dram, out, nb_run=B):
    with ExitStack() as ctx:
        def sb(name, shape, dt=F32):
            return ctx.enter_context(nc.sbuf_tensor(name, shape, dt))

        def ps(name, shape, dt=F32):
            return ctx.enter_context(nc.psum_tensor(name, shape, dt))

        def sem(name):
            return semaphores.enter_context(nc.semaphore(name))

        ps_delta = ps("ps_delta", [P, 2, HALF])
        ps_dx = ps("ps_dx", [P, 2, HALF])
        ps_y = ps("ps_y", [P, 2, HALF])
        ps_aux = ps("ps_aux", [P, 2, HALF])

        ident = sb("ident", [P, P])
        nsum = sb("nsum", [P, CH])
        rep = sb("rep", [P, P])
        bc_sel = sb("bc_sel", [P, 2 * GROUPS, P])
        xproj = sb("xproj", [P, KD, R + 2 * N])
        dtw = sb("dtw", [R, D])
        dtb = sb("dtb", [P, KD])
        dcol = sb("dcol", [P, KD])
        ddiag = sb("ddiag", [P, KD, P])
        a_neg = sb("a_neg", [P, CHUNKS * GROUPS])
        rw = sb("rw", [P, D])
        rb = sb("rb", [P, 1])

        xr = sb("xr", [P, 2, TC, D])
        xh = sb("xh", [P, 2, D])
        xhT = sb("xhT", [P, KD, L])
        xpT = sb("xpT", [P, L])
        delT = sb("delT", [P, KD, L])
        dxT = sb("dxT", [P, KD, L])
        te = sb("te", [P, L])
        tu = sb("tu", [P, L])
        bmat = sb("bmat", [P, GROUPS, L])
        cmat = sb("cmat", [P, GROUPS, L])
        stage = sb("stage", [P, 2, D])
        junk = sb("junk", [P, 2, D], BF16)
        wcol = sb("wcol", [P, B * TC])
        wrow = sb("wrow", [P, P])
        st1 = sb("st1", [P, TC, 6])
        mean1 = sb("mean1", [P, TC])
        r1 = sb("r1", [P, 6, TC])
        st2 = sb("st2", [P, TC, 6])
        mean2 = sb("mean2", [P, TC])
        r2 = sb("r2", [P, 9, TC])

        decay = sb("decay", [P, RING, L])
        inp = sb("inp", [P, RING, L])
        hid = sb("hid", [P, 2, L])
        ch = sb("ch", [P, 2, L])
        dxr = sb("dxr", [P, 2, L])
        ysb = sb("ysb", [P, 2, 2 * P])

        consts_in = sem("consts_in")
        x_in = [sem("x_in_even"), sem("x_in_odd")]
        x1_out = sem("x1_out")
        out_even, out_odd = sem("out_even"), sem("out_odd")
        w_out = sem("w_out")
        a_exp = sem("a_exp")
        a_ready = sem("a_ready")
        ddiag_ready = sem("ddiag_ready")
        decay_ready = sem("decay_ready")
        inp_ready = sem("inp_ready")
        hid_ready = sem("hid_ready")
        ch_ready = sem("ch_ready")
        ch_summed = sem("ch_summed")
        delta_rep = sem("delta_rep")
        dx_rep = sem("dx_rep")
        dxr_ready = sem("dxr_ready")
        ysb_ready = sem("ysb_ready")
        yt_ready = sem("yt_ready")
        y_added = sem("y_added")
        aux_full = sem("aux_full")
        aux_emptied = sem("aux_emptied")
        skip_added = sem("skip_added")
        z_act = sem("z_act")
        z_dve = sem("z_dve")
        ln1 = sem("ln1")
        ln1_act = sem("ln1_act")
        ln2 = sem("ln2")
        ln2_act = sem("ln2_act")
        xh_ready = sem("xh_ready")
        router_sum = sem("router_sum")
        stage_ready = sem("stage_ready")
        wt_ready = sem("wt_ready")
        wrow_ready = sem("wrow_ready")
        NCONST = 11

        def tile(b, c, g):
            return b * TILES + c * GROUPS + g

        def has(b, least):
            return not isinstance(b, int) or b >= least

        def batches(eng, body):
            body(0, 0)
            if nb_run > 2:
                with eng.Fori(1, nb_run - 2, 2) as i:
                    body(i, 1)
                    body(i + 1, 0)
            body(nb_run - 1, 1)

        block = ctx.enter_context(nc.Block())

        @block.sync
        def _(sp):
            for dst, src in ((ident[:], ident_c), (nsum[:], nsum_c), (rep[:], rep_c),
                             (bc_sel[R:R + 2 * N], bc_c), (xproj[:], w_xproj), (dtw[:], w_dt), (dtb[:], dt_b),
                             (dcol[:], D_col), (a_neg[:], A_log), (rw[:], router_w), (rb[:], router_b)):
                sp.dma_start(dst, src).then_inc(consts_in, 16)

            def load_x(b, par):
                if has(b, 2):
                    sp.wait_ge(x1_out, b * 16 - 16)
                    sp.wait_ge(stage_ready, b * TC - TC)
                sp.dma_start(xr[:, par], x[b].rearrange("(t p) d -> p t d", p=P)).then_inc(x_in[par], 16)

            def stores(b, par):
                sp.wait_ge(y_added, b * CHUNKS + CHUNKS)
                sp.dma_start(x1_dram[b].rearrange("(t p) d -> p t d", p=P), xr[:, par]).then_inc(x1_out, 16)
                for t in range(TC):
                    sp.wait_ge(stage_ready, b * TC + t + 1)
                    sp.dma_start(out[b, P * t:P * (t + 1)], stage[:, t % 2]).then_inc((out_even, out_odd)[t % 2], 16)

            load_x(0, 0)

            def body(b, par):
                if has(b, 1):
                    stores(b - 1, 1 - par)
                if not (isinstance(b, int) and b == nb_run - 1):
                    load_x(b + 1, 1 - par)

            batches(sp, body)
            stores(nb_run - 1, 1)
            sp.wait_ge(wrow_ready, 1)
            sp.dma_start(w_dram.rearrange("b (t p) -> (b t) p", p=P)[0:nb_run * TC], wrow[0:nb_run * TC]).then_inc(w_out, 16)
            sp.wait_ge(w_out, 16)
            sp.wait_ge(x1_out, 16 * nb_run)
            sp.wait_ge(out_even, 64 * nb_run)
            sp.wait_ge(out_odd, 64 * nb_run)

        @block.tensor
        def _(pe):
            def aux_bank(b, key):
                u = USE[key] - 2
                before = b
                if u < 0:
                    u += NUSE
                    before = b - 1
                if has(before, 0):
                    old = USES[u]
                    if old[0] == "skip":
                        pe.wait_ge(skip_added, before * TC + old[1] + 1)
                    else:
                        pe.wait_ge(aux_emptied, before * NEMPTIED + EMPTIED[old])
                return ps_aux[:, USE[key] % 2, :]

            def turn_xhat(b, t):
                bank = aux_bank(b, ("xhat", t))
                pe.wait_ge(xh_ready, b * TC + t + 1)
                for k in range(KD):
                    last = pe.transpose(bank[:, k * P:(k + 1) * P], xh[:, t % 2, k * P:(k + 1) * P], ident[:])
                last.then_inc(aux_full, 1)

            def project(b, h):
                bank = aux_bank(b, ("proj", h))
                pe.wait_ge(aux_emptied, b * NEMPTIED + TC)
                for k in range(KD):
                    last = pe.matmul(bank[0:R + 2 * N, :], xproj[:, k, :], xhT[:, k, h * HALF:(h + 1) * HALF],
                                     start=(k == 0), stop=(k == KD - 1))
                last.then_inc(aux_full, 1)

            def step_size(b, k, h):
                bank = aux_bank(b, (f"z{k}", h))
                pe.wait_ge(aux_emptied, b * NEMPTIED + EMPTIED[("proj", 0)])
                pe.matmul(bank, dtw[:, k * P:(k + 1) * P], xpT[0:R, h * HALF:(h + 1) * HALF],
                          start=True, stop=True).then_inc(aux_full, 1)

            def skip_term(b, t):
                bank = aux_bank(b, ("skip", t))
                for k in range(KD):
                    last = pe.matmul(bank[:, k * P:(k + 1) * P], xhT[:, k, t * P:(t + 1) * P], ddiag[:, k, :],
                                     start=True, stop=True)
                last.then_inc(aux_full, 1)

            def spread_bc(b, i, h):
                bank = aux_bank(b, (f"bc{i}", h))
                pe.matmul(bank, bc_sel[R:R + 2 * N, i, :], xpT[R:R + 2 * N, h * HALF:(h + 1) * HALF],
                          start=True, stop=True).then_inc(aux_full, 1)

            def repeat_dx(b, c):
                k, r = c // NT, CH * (c % NT)
                pe.wait_ge(z_dve, b * 20 + 5 * k + 5)
                if has(b, 1) or c > 0:
                    pe.wait_ge(dxr_ready, b * CHUNKS + c)
                for h in range(2):
                    last = pe.matmul(ps_dx[:, h, :], rep[r:r + CH, :], dxT[r:r + CH, k, h * HALF:(h + 1) * HALF],
                                     start=True, stop=True)
                last.then_inc(dx_rep, 1)

            def repeat_delta(b, c):
                k, r = c // NT, CH * (c % NT)
                if has(b, 1) or c > 0:
                    pe.wait_ge(decay_ready, tile(b, c, 0))
                for h in range(2):
                    last = pe.matmul(ps_delta[:, h, :], rep[r:r + CH, :], delT[r:r + CH, k, h * HALF:(h + 1) * HALF],
                                     start=True, stop=True)
                last.then_inc(delta_rep, 1)

            def sum_states(b, c, g):
                pe.wait_ge(ch_ready, tile(b, c, g) + 1)
                if g == 0 and (has(b, 1) or c >= 2):
                    pe.wait_ge(y_added, b * CHUNKS + c - 1)
                for q in range(4):
                    last = pe.matmul(ps_y[q * CH:(q + 1) * CH, c % 2, 0:2 * P], nsum[:],
                                     ch[:, g % 2, q * 2 * P:(q + 1) * 2 * P],
                                     start=(g == 0), stop=(g == GROUPS - 1))
                last.then_inc(ch_summed, 1)

            def turn_y(b, c):
                pe.wait_ge(ysb_ready, b * CHUNKS + c + 1)
                for t in range(2):
                    last = pe.transpose(ps_y[:, c % 2, (2 + t) * P:(3 + t) * P], ysb[:, c % 2, t * P:(t + 1) * P],
                                        ident[:])
                last.then_inc(yt_ready, 1)

            pe.wait_ge(consts_in, 16 * NCONST)
            for t in range(TC):
                turn_xhat(0, t)
            for h in range(2):
                project(0, h)
            for h in range(2):
                step_size(0, 0, h)
            pe.wait_ge(ddiag_ready, KD)
            for t in range(4):
                skip_term(0, t)
            for h in range(2):
                step_size(0, 1, h)
            for t in range(4, 8):
                skip_term(0, t)
            for h in range(2):
                step_size(0, 2, h)
            for i in BC_ORDER:
                for h in range(2):
                    spread_bc(0, i, h)
            repeat_dx(0, 0)
            repeat_delta(0, 0)

            def body(b, par):
                final = isinstance(b, int) and b == nb_run - 1
                for c in range(CHUNKS):
                    if c < CHUNKS - 1:
                        repeat_dx(b, c + 1)
                        repeat_delta(b, c + 1)
                    elif not final:
                        repeat_dx(b + 1, 0)
                        repeat_delta(b + 1, 0)
                    for g in range(GROUPS):
                        s = c * GROUPS + g
                        sum_states(b, c, g)
                        if g == 0 and c > 0:
                            turn_y(b, c - 1)
                        if s == 0 and has(b, 1):
                            turn_y(b - 1, CHUNKS - 1)
                        if s + TILES in BC_MADE and has(b, 1):
                            for h in range(2):
                                spread_bc(b, BC_ORDER[BC_MADE.index(s + TILES)], h)
                        if s == 8:
                            for h in range(2):
                                step_size(b, 3, h)
                        if final:
                            continue
                        if 24 <= s < 24 + TC:
                            turn_xhat(b + 1, s - 24)
                        if s in (33, 34):
                            project(b + 1, s - 33)
                        if s in (37, 44, 51):
                            for h in range(2):
                                step_size(b + 1, (s - 37) // 7, h)
                        if 40 <= s < 44:
                            skip_term(b + 1, s - 40)
                        if 47 <= s < 51:
                            skip_term(b + 1, s - 43)
                        if s in BC_MADE:
                            for h in range(2):
                                spread_bc(b + 1, BC_ORDER[BC_MADE.index(s)], h)

            batches(pe, body)
            turn_y(nb_run - 1, CHUNKS - 1)
            pe.wait_ge(router_sum, 10 * nb_run)
            pe.transpose(ps_aux[0:nb_run * TC, 0, 0:P], wcol[:, 0:nb_run * TC], ident[:]).then_inc(wt_ready, 1)

        @block.scalar
        def _(act):
            def aux_filled(b, key):
                act.wait_ge(aux_full, b * NUSE + USE[key] + 1)
                return ps_aux[:, USE[key] % 2, :]

            def copy_xhat(b, t):
                bank = aux_filled(b, ("xhat", t))
                if t == 0 and has(b, 1):
                    act.wait_ge(z_dve, b * 20)
                nc.scalar.activation(xhT[:, :, t * P:(t + 1) * P], bank.rearrange("p (k t) -> p k t", k=KD),
                                     ACT.Copy).then_inc(aux_emptied, 1)

            def copy_proj(b):
                aux_filled(b, ("proj", 1))
                nc.scalar.activation(xpT[0:R + 2 * N, :], ps_aux[0:R + 2 * N].rearrange("p h t -> p (h t)"),
                                     ACT.Copy).then_inc(aux_emptied, 1)

            def softplus_a(b, k):
                aux_filled(b, (f"z{k}", 1))
                z = ps_aux[:].rearrange("p h t -> p (h t)")
                if has(b, 1) or k > 0:
                    act.wait_ge(z_dve, b * 20 + 5 * k)
                nc.scalar.activation(te[:], z, ACT.Abs, bias=dtb[:, k:k + 1]).then_inc(z_act, 1)
                if has(b, 1):
                    act.wait_ge(dx_rep, b * CHUNKS - CHUNKS + 4 * k + 4)
                    act.wait_ge(delta_rep, b * CHUNKS - CHUNKS + 4 * k + 4)
                nc.scalar.activation(dxT[:, k, :], z, ACT.Relu, bias=dtb[:, k:k + 1]).then_inc(aux_emptied, 1)

            def softplus_b(b, k):
                act.wait_ge(z_act, b * 12 + 3 * k + 1)
                nc.scalar.activation(te[:], te[:], ACT.Exp, scale=-1.0).then_inc(z_act, 1)

            def softplus_c(b, k):
                act.wait_ge(z_act, b * 12 + 3 * k + 2)
                nc.scalar.activation(delT[:, k, :], te[:], ACT.Ln, bias=1.0).then_inc(z_act, 1)

            def copy_bc(b, i):
                aux_filled(b, (f"bc{i}", 1))
                g = i // 2
                if has(b, 1):
                    act.wait_ge((inp_ready, ch_ready)[i % 2], tile(b, 0, 0) - GROUPS + g + 1)
                nc.scalar.activation((bmat, cmat)[i % 2][:, g, :], ps_aux[:].rearrange("p h t -> p (h t)"),
                                     ACT.Copy).then_inc(aux_emptied, 1)

            def rstd(b, chain, chain_act, r, at, per):
                act.wait_ge(chain, b * per + at)
                nc.scalar.activation(r[:, 1, :], r[:, 0, :], ACT.Ln).then_inc(chain_act, 1)
                act.wait_ge(chain_act, b * 2 + 1)
                nc.scalar.activation(r[:, 2, :], r[:, 1, :], ACT.Exp, scale=-0.5).then_inc(chain_act, 1)

            def exp_decay(b, c, g):
                if has(b, 1) or c > 0:
                    act.wait_ge(hid_ready, tile(b, c, g) - RING + 1)
                if g == 0:
                    act.wait_ge(delta_rep, b * CHUNKS + c + 1)
                i = c * GROUPS + g
                nc.scalar.activation(decay[:, g, :], ps_delta[:].rearrange("p h t -> p (h t)"),
                                     ACT.Exp, scale=a_neg[:, i:i + 1]).then_inc(decay_ready, 1)

            def copy_dx(b, c):
                act.wait_ge(dx_rep, b * CHUNKS + c + 1)
                if has(b, 1) or c >= 2:
                    act.wait_ge(inp_ready, tile(b, c - 1, 0))
                nc.scalar.activation(dxr[:, c % 2, :], ps_dx[:].rearrange("p h t -> p (h t)"),
                                     ACT.Copy).then_inc(dxr_ready, 1)

            def copy_y(b, c):
                act.wait_ge(ch_summed, tile(b, c, GROUPS - 1) + 1)
                if has(b, 1) or c >= 2:
                    act.wait_ge(yt_ready, b * CHUNKS + c - 1)
                nc.scalar.activation(ysb[:, c % 2, :], ps_y[:, c % 2, 0:2 * P], ACT.Copy).then_inc(ysb_ready, 1)

            act.wait_ge(consts_in, 16 * NCONST)
            nc.scalar.activation(a_neg[:], a_neg[:], ACT.Exp).then_inc(a_exp, 1)
            act.wait_ge(a_exp, 1)
            nc.scalar.mul(a_neg[:], a_neg[:], -1.0).then_inc(a_ready, 1)
            act.wait_ge(a_ready, 1)
            rstd(0, ln1, ln1_act, r1, LN_VAR, LN1)
            for t in range(TC):
                copy_xhat(0, t)
            copy_proj(0)
            for k in range(3):
                softplus_a(0, k)
                softplus_b(0, k)
                softplus_c(0, k)
            for i in BC_ORDER:
                copy_bc(0, i)

            def body(b, par):
                final = isinstance(b, int) and b == nb_run - 1
                for c in range(CHUNKS):
                    for g in range(GROUPS):
                        s = c * GROUPS + g
                        exp_decay(b, c, g)
                        if g == 0 and c >= 2:
                            copy_y(b, c - 2)
                        if g == 0 and c < 2 and has(b, 1):
                            copy_y(b - 1, CHUNKS + c - 2)
                        if g == 1:
                            copy_dx(b, c)
                        if s + TILES in BC_COPIED and has(b, 1):
                            copy_bc(b, BC_ORDER[BC_COPIED.index(s + TILES)])
                        if s == 12 and has(b, 1):
                            rstd(b - 1, ln2, ln2_act, r2, LN_VAR, LN2)
                        if s == 14:
                            softplus_a(b, 3)
                        if s == 15:
                            softplus_b(b, 3)
                        if s == 16:
                            softplus_c(b, 3)
                        if final:
                            continue
                        if s == 27:
                            rstd(b + 1, ln1, ln1_act, r1, LN_VAR, LN1)
                        if 30 <= s < 30 + TC:
                            copy_xhat(b + 1, s - 30)
                        if s == 42:
                            copy_proj(b + 1)
                        if s in (43, 50, 57):
                            softplus_a(b + 1, (s - 43) // 7)
                        if s in (44, 51, 58):
                            softplus_b(b + 1, (s - 44) // 7)
                        if s in (45, 52, 59):
                            softplus_c(b + 1, (s - 45) // 7)
                        if s in BC_COPIED:
                            copy_bc(b + 1, BC_ORDER[BC_COPIED.index(s)])

            batches(act, body)
            copy_y(nb_run - 1, CHUNKS - 2)
            copy_y(nb_run - 1, CHUNKS - 1)
            rstd(nb_run - 1, ln2, ln2_act, r2, LN_VAR, LN2)

        @block.vector
        def _(dve):
            def stats(par, t, s, chain):
                nc.vector.bn_stats(s[:, t, :], xr[:, par, t, :]).then_inc(chain, 1)

            def moments(b, s, mean, r, chain, per):
                n = b * per + TC
                dve.wait_ge(chain, n)
                nc.vector.tensor_tensor(r[:, 3, :], s[:, :, 1], s[:, :, 4], ALU.add).then_inc(chain, 1)
                nc.vector.tensor_tensor(r[:, 4, :], s[:, :, 1], s[:, :, 4], ALU.subtract).then_inc(chain, 1)
                nc.vector.tensor_tensor(r[:, 5, :], s[:, :, 2], s[:, :, 5], ALU.add).then_inc(chain, 1)
                dve.wait_ge(chain, n + 3)
                nc.vector.tensor_scalar(mean[:], r[:, 3, :], 0.5, None, ALU.mult).then_inc(chain, 1)
                nc.vector.tensor_tensor(r[:, 2, :], r[:, 4, :], r[:, 4, :], ALU.mult).then_inc(chain, 1)
                nc.vector.tensor_scalar(r[:, 1, :], r[:, 5, :], 1.0 / D, EPS, ALU.mult, ALU.add).then_inc(chain, 1)
                dve.wait_ge(chain, n + 6)
                nc.vector.scalar_tensor_tensor(r[:, 0, :], r[:, 2, :], 0.25, r[:, 1, :], ALU.mult, ALU.add)\
                    .then_inc(chain, 1)

            def newton(b, r, chain, chain_act, per):
                dve.wait_ge(chain_act, b * 2 + 2)
                n = b * per + TC + 7
                nc.vector.tensor_tensor(r[:, 3, :], r[:, 2, :], r[:, 2, :], ALU.mult).then_inc(chain, 1)
                dve.wait_ge(chain, n + 1)
                nc.vector.tensor_tensor(r[:, 5, :], r[:, 3, :], r[:, 0, :], ALU.mult).then_inc(chain, 1)
                dve.wait_ge(chain, n + 2)
                nc.vector.tensor_scalar(r[:, 3, :], r[:, 5, :], -0.5, 1.5, ALU.mult, ALU.add).then_inc(chain, 1)
                dve.wait_ge(chain, n + 3)
                nc.vector.tensor_tensor(r[:, 4, :], r[:, 2, :], r[:, 3, :], ALU.mult).then_inc(chain, 1)
                dve.wait_ge(chain, n + 4)

            def ln1_stats(b, par, ts):
                dve.wait_ge(x_in[par], (b - par) * 8 + 16)
                for t in ts:
                    stats(par, t, st1, ln1)

            def normalise(b, par, t):
                if has(b, 1) or t >= 2:
                    if t >= 2:
                        dve.wait_ge(aux_full, b * NUSE + t - 1)
                    else:
                        dve.wait_ge(aux_full, b * NUSE - NUSE + TC - 1 + t)
                nc.vector.tensor_scalar(xh[:, t % 2, :], xr[:, par, t, :], mean1[:, t:t + 1], r1[:, 4, t:t + 1],
                                        ALU.subtract, ALU.mult).then_inc(xh_ready, 1)

            def add_skip(b, par, t):
                u = USE[("skip", t)]
                dve.wait_ge(aux_full, b * NUSE + u + 1)
                dve.wait_ge(xh_ready, b * TC + TC)
                nc.vector.tensor_tensor(xr[:, par, t, :], xr[:, par, t, :], ps_aux[:, u % 2, :],
                                        ALU.add).then_inc(skip_added, 1)

            def softplus(b, k):
                dve.wait_ge(z_act, b * 12 + 3 * k + 2)
                n = b * 20 + 5 * k
                if has(b, 1) or k > 0:
                    dve.wait_ge(z_dve, n)
                nc.vector.tensor_scalar(tu[:], te[:], 1.0, None, ALU.add).then_inc(z_dve, 1)
                dve.wait_ge(z_dve, n + 1)
                nc.vector.scalar_tensor_tensor(tu[:], tu[:], 1.0, te[:], ALU.subtract, ALU.subtract)\
                    .then_inc(z_dve, 1)
                dve.wait_ge(z_act, b * 12 + 3 * k + 3)
                dve.wait_ge(z_dve, n + 2)
                nc.vector.tensor_tensor(delT[:, k, :], delT[:, k, :], tu[:], ALU.subtract).then_inc(z_dve, 1)
                dve.wait_ge(aux_emptied, b * NEMPTIED + EMPTIED[(f"z{k}", 0)])
                dve.wait_ge(z_dve, n + 3)
                nc.vector.tensor_tensor(delT[:, k, :], delT[:, k, :], dxT[:, k, :], ALU.add).then_inc(z_dve, 1)
                dve.wait_ge(z_dve, n + 4)
                nc.vector.tensor_tensor(dxT[:, k, :], delT[:, k, :], xhT[:, k, :], ALU.mult).then_inc(z_dve, 1)

            def make_input(b, c, g):
                if g == 0:
                    dve.wait_ge(dxr_ready, b * CHUNKS + c + 1)
                if c == 0:
                    dve.wait_ge(aux_emptied, b * NEMPTIED + EMPTIED[(f"bc{2 * g}", 0)])
                if has(b, 1) or c > 0:
                    dve.wait_ge(hid_ready, tile(b, c, g) - RING + 1)
                nc.vector.tensor_tensor(inp[:, g, :], dxr[:, c % 2, :], bmat[:, g, :],
                                        ALU.mult).then_inc(inp_ready, 1)

            def scan(b, c, g):
                dve.wait_ge(decay_ready, tile(b, c, g) + 1)
                dve.wait_ge(inp_ready, tile(b, c, g) + 1)
                if has(b, 1) or c * GROUPS + g >= 2:
                    dve.wait_ge(ch_ready, tile(b, c, g) - 1)
                nc.vector.tensor_tensor_scan(hid[:, g % 2, :], decay[:, g, :], inp[:, g, :],
                                             0.0, ALU.mult, ALU.add).then_inc(hid_ready, 1)

            def add_y(b, par, c):
                dve.wait_ge(yt_ready, b * CHUNKS + c + 1)
                if c == 0:
                    dve.wait_ge(skip_added, b * TC + TC)
                x1 = xr[:, par, :, c * CH:(c + 1) * CH].rearrange("p (q t) d -> p t q d", t=2)
                y = ps_y[:, c % 2, 2 * P:4 * P].rearrange("p (t q d) -> p t q d", t=2, q=4)
                nc.vector.tensor_tensor(x1, x1, y, ALU.add).then_inc(y_added, 1)

            def ln2_stats(b, par):
                dve.wait_ge(y_added, b * CHUNKS + CHUNKS)
                for t in range(TC):
                    stats(par, t, st2, ln2)
                moments(b, st2, mean2, r2, ln2, LN2)

            def ln2_finish(b, par):
                newton(b, r2, ln2, ln2_act, LN2)
                nc.vector.scalar_tensor_tensor(r2[:, 6, :], mean2[:], -1.0, r2[:, 4, :], ALU.mult, ALU.mult)\
                    .then_inc(ln2, 1)
                nc.vector.tensor_scalar(r2[:, 7, :], r2[:, 4, :], 1.0, None, ALU.add).then_inc(ln2, 1)

            def router(b, par):
                for t in range(TC):
                    if t >= 2:
                        dve.wait_ge(router_sum, b * 10 + t - 1)
                    elif has(b, 1):
                        dve.wait_ge(router_sum, b * 10)
                    nc.vector.scalar_tensor_tensor(junk[:, t % 2, :], xr[:, par, t, :], mean2[:, t:t + 1], rw[:],
                                                   ALU.subtract, ALU.mult, accum_out=r2[:, 8, t:t + 1])\
                        .then_inc(router_sum, 1)
                dve.wait_ge(router_sum, b * 10 + TC)
                nc.vector.tensor_tensor(r2[:, 3, :], r2[:, 8, :], r2[:, 4, :], ALU.mult).then_inc(router_sum, 1)
                dve.wait_ge(router_sum, b * 10 + TC + 1)
                nc.vector.tensor_scalar(wcol[:, bass.ds(b * TC, TC)], r2[:, 3, :], rb[:, 0:1], None, ALU.add)\
                    .then_inc(router_sum, 1)

            def make_out(b, par):
                dve.wait_ge(ln2, b * LN2 + LN2)
                for t in range(TC):
                    if has(b, 1) or t >= 2:
                        dve.wait_ge((out_even, out_odd)[t % 2], b * 64 + 16 * (t // 2))
                    nc.vector.tensor_scalar(stage[:, t % 2, :], xr[:, par, t, :], r2[:, 7, t:t + 1],
                                            r2[:, 6, t:t + 1], ALU.mult, ALU.add).then_inc(stage_ready, 1)

            dve.wait_ge(consts_in, 16 * NCONST)
            for k in range(KD):
                nc.vector.tensor_scalar(ddiag[:, k, :], ident[:], dcol[:, k:k + 1], None, ALU.mult)\
                    .then_inc(ddiag_ready, 1)
            ln1_stats(0, 0, range(TC))
            moments(0, st1, mean1, r1, ln1, LN1)
            newton(0, r1, ln1, ln1_act, LN1)
            for t in range(TC):
                normalise(0, 0, t)
            softplus(0, 0)
            for t in range(4):
                add_skip(0, 0, t)
            softplus(0, 1)
            for t in range(4, 8):
                add_skip(0, 0, t)
            softplus(0, 2)
            make_input(0, 0, 0)

            def body(b, par):
                final = isinstance(b, int) and b == nb_run - 1
                other = 1 - par
                for c in range(CHUNKS):
                    for g in range(GROUPS):
                        s = c * GROUPS + g
                        if g < GROUPS - 1:
                            make_input(b, c, g + 1)
                        elif c < CHUNKS - 1:
                            make_input(b, c + 1, 0)
                        elif not final:
                            make_input(b + 1, 0, 0)
                        scan(b, c, g)
                        if g == 2:
                            if c >= 1:
                                add_y(b, par, c - 1)
                            elif has(b, 1):
                                add_y(b - 1, other, CHUNKS - 1)
                        if s == 13:
                            softplus(b, 3)
                        if has(b, 1):
                            if s == 4:
                                ln2_stats(b - 1, other)
                            if s == 9:
                                ln2_finish(b - 1, other)
                            if s == 10:
                                router(b - 1, other)
                            if s == 12:
                                make_out(b - 1, other)
                        if final:
                            continue
                        if s == 21:
                            ln1_stats(b + 1, other, range(0, 4))
                        if s == 22:
                            ln1_stats(b + 1, other, range(4, TC))
                            moments(b + 1, st1, mean1, r1, ln1, LN1)
                        if s == 24:
                            newton(b + 1, r1, ln1, ln1_act, LN1)
                        if 24 <= s < 24 + TC:
                            normalise(b + 1, other, s - 24)
                        if 42 <= s < 46:
                            add_skip(b + 1, other, s - 42)
                        if 49 <= s < 53:
                            add_skip(b + 1, other, s - 45)
                        if s in (43, 50, 57):
                            softplus(b + 1, (s - 43) // 7)

            batches(dve, body)
            last = nb_run - 1
            add_y(last, 1, CHUNKS - 1)
            ln2_stats(last, 1)
            ln2_finish(last, 1)
            router(last, 1)
            make_out(last, 1)
            dve.wait_ge(wt_ready, 1)
            nc.vector.tensor_copy(wrow[0:nb_run * TC], ps_aux[0:nb_run * TC, 0, 0:P]).then_inc(wrow_ready, 1)

        @block.gpsimd
        def _(pool):
            def body(b, par):
                for c in range(CHUNKS):
                    for g in range(GROUPS):
                        pool.wait_ge(hid_ready, tile(b, c, g) + 1)
                        if c == 0:
                            pool.wait_ge(aux_emptied, b * NEMPTIED + EMPTIED[(f"bc{2 * g + 1}", 0)])
                        if has(b, 1) or c * GROUPS + g >= 2:
                            pool.wait_ge(ch_summed, tile(b, c, g) - 1)
                        nc.gpsimd.tensor_tensor(ch[:, g % 2, :], hid[:, g % 2, :], cmat[:, g, :],
                                                ALU.mult).then_inc(ch_ready, 1)

            batches(pool, body)


K = 128
KS = K - 1
H, HD, F = 16, 32, 2048
BM, SM = 4, 2048
LOWEST = -3.0e38
MAGIC = 12582912.0
TWO_PI_HI = 6.28125
TWO_PI_LO = 2 * np.pi - TWO_PI_HI

MLP = {"h2T", "up0", "up1", "up2", "up3", "gT0", "gT1", "gT2", "gT3", "down"}
BANK_USES = {
    "t0": ["hnT", "v", "up1", "up3", "GT1", "gT1", "gT3"],
    "t1": ["h2T", "up0", "up2", "GT0", "gT0", "gT2", "oT"],
    "m0": ["q", "qT", "mask", "o"],
    "m1": ["k", "kT", "down", "attn"],
    "s": ["scores", "aT"],
}
BANK_OF = {use: bank for bank, uses in BANK_USES.items() for use in uses}


def use_number(i, use):
    uses = BANK_USES[BANK_OF[use]]
    skipped = sum(u in MLP for u in uses)
    if isinstance(i, int) and i == 0:
        return [u for u in uses if u not in MLP].index(use)
    at = uses.index(use)
    if isinstance(i, int) and i == B:
        at = [u for u in uses if u in MLP].index(use)
    return i * len(uses) - skipped + at


def ffn_phase(nc, semaphores, w_dram, x1_dram, out, mask, pos, wq, wk, wv, wo, w1, w2, ln1, ln2, ident_c, sel16_c, token_c,
              batch_c, inv_c):
    with ExitStack() as ctx:
        def sb(name, shape, dt=F32):
            return ctx.enter_context(nc.sbuf_tensor(name, shape, dt))

        def sem(name):
            return semaphores.enter_context(nc.semaphore(name))

        banks = {name: ctx.enter_context(nc.psum_tensor(f"ps_{name}", [P, n, HALF], F32))
                 for name, n in (("s", 4), ("t0", 1), ("t1", 1), ("m0", 1), ("m1", 1))}
        one = {name: banks[name][:, 0, :] for name in ("t0", "t1", "m0", "m1")}

        ident = sb("identf", [P, P])
        token = sb("token", [P, TC])
        batch = sb("batch", [B, 3])
        inv = sb("inv", [P, HD // 2])
        w_qkv = sb("w_qkv", [P, 3, KD, D])
        w_o = sb("w_o", [P, KD, D])
        w_1 = sb("w_1", [P, KD, F])
        w_2 = sb("w_2", [P, F // P, D])
        g1 = sb("g1", [P, KD])
        g2 = sb("g2", [P, KD])

        top = sb("top", [B, K])
        topi = sb("topi", [B, K], U32)
        rows_f = sb("rows_f", [B, 5, K])
        cols_i = sb("cols_i", [P, 3, B], U32)
        wsel = sb("wsel", [P, B])
        notsel = sb("notsel", [P, B])
        idx_bc = sb("idx_bc", [P, B, K])
        pos_i = sb("pos_i", [P, B], I32)
        pos_f = sb("pos_f", [P, B])
        ang = sb("ang", [P, 4, B, HD // 2])
        cos = sb("cos", [P, B, HD // 2])
        sin = sb("sin", [P, B, HD // 2])

        idx_now = sb("idx_now", [P, 2, 3], U32)
        xg = sb("xg", [P, 2, D])
        rows_m = sb("rows_m", [P, L])
        xn = sb("xn", [P, D])
        base = sb("base", [P, 2, D])
        hn = sb("hn", [P, D])
        hnT = sb("hnT", [P, KD, P])
        qk = sb("qk", [P, 2, D])
        rot = sb("rot", [P, 2, D])
        vsb = sb("vsb", [P, D])
        qkT = sb("qkT", [P, 2, KD, P])
        onehot = sb("onehot", [P, TC, K])
        GT = sb("GT", [P, TC, P])
        msel = sb("msel", [P, K])
        prob = sb("prob", [P, H, K])
        probT = sb("probT", [P, H, P])
        osb = sb("osb", [P, D])
        oT = sb("oT", [P, KD, P])
        x1f = sb("x1f", [P, 2, D])
        h2 = sb("h2", [P, 2, D])
        h2T = sb("h2T", [P, KD, P])
        act_up = sb("act_up", [P, F])
        gT = sb("gT", [P, F // P, P])
        row = sb("row", [P, 2, D])
        wts = act_up[0:B].rearrange("p (e t) -> p e t", e=2)
        sel16 = gT[0:B]
        sq = sb("sq", [P, D], BF16)
        st = sb("st", [P, 6])
        v1 = sb("v1", [P, 2, 24])
        mx = sb("mx", [P, 3, H])

        loaded = sem("loaded")
        wts_in = sem("wts_in")
        folded = sem("folded")
        topk = sem("topk")
        cols_full = sem("cols_full")
        cols_done = sem("cols_done")
        idxbc_full = sem("idxbc_full")
        pos_in = sem("pos_in")
        angle = sem("angle")
        full = {b: sem(f"full_{b}") for b in banks}
        free = {b: sem(f"free_{b}") for b in banks}
        idx_copied = sem("idx_copied")
        x_in = [sem("xg_even"), sem("xg_odd")]
        m_in = sem("m_in")
        scattered = [sem("scattered_even"), sem("scattered_odd")]
        norm = sem("norm")
        norm_act = sem("norm_act")
        norm2 = sem("norm2")
        norm2_act = sem("norm2_act")
        rope = sem("rope")
        onehot_ready = sem("onehot_ready")
        soft = sem("soft")
        exp_ready = sem("exp_ready")
        o_ready = sem("o_ready")
        row_ready = sem("row_ready")
        gathering = sem("gathering")
        scattering = sem("scattering")

        SETUP_DMAS = 5
        WEIGHT_DMAS = 8

        def steps(eng, body):
            body(0, 0)
            body(1, 1)
            with eng.Fori(2, B - 3, 2) as i:
                body(i, 0)
                body(i + 1, 1)
            body(B - 2, 0)
            body(B - 1, 1)
            body(B, 0)

        def attention(i):
            return not (isinstance(i, int) and i == B)

        def mlp(i):
            return not (isinstance(i, int) and i == 0)

        def fill(pe, i, use):
            n = use_number(i, use)
            if not (isinstance(n, int) and n == 0):
                pe.wait_ge(free[BANK_OF[use]], n)

        def filled(eng, i, use):
            eng.wait_ge(full[BANK_OF[use]], use_number(i, use) + 1)
            return BANK_OF[use]

        block = ctx.enter_context(nc.Block())

        @block.sync
        def _(sp):
            sp.dma_start(wts[:, 0, :], w_dram).then_inc(wts_in, 16)
            for dst, src in ((ident[:], ident_c), (sel16[:], sel16_c), (token[:], token_c), (batch[:], batch_c),
                             (inv[:], inv_c)):
                sp.dma_start(dst, src).then_inc(loaded, 16)
            for dst, src in ((w_qkv[:, 0], wq), (w_qkv[:, 1], wk), (w_qkv[:, 2], wv), (g1[:], ln1), (w_o[:], wo),
                             (g2[:], ln2), (w_1[:], w1), (w_2[:], w2)):
                sp.dma_start(dst, src).then_inc(loaded, 16)

        @block.gpsimd
        def _(pool):
            pool.wait_ge(cols_done, 5)
            for b in range(B):
                pool.indirect_dma_start(
                    out=pos_i[:, b:b + 1], out_offset=None, in_=pos,
                    in_offset=bass.IndirectOffsetOnAxis(ap=cols_i[:, 1, b:b + 1], axis=0),
                ).then_inc(pos_in, 16)

            def gather(a, par):
                if has_batch(a, 2):
                    pool.wait_ge(x_in[par], (a - par) * 8)
                    pool.wait_ge(scattered[par], (a - par) * 8)
                    pool.wait_ge(norm, (a - 1) * NORM)
                if has_batch(a, 1):
                    pool.wait_ge(m_in, a * 16)
                    pool.wait_ge(full["t0"], use_number(a - 1, "GT1") + 1)
                nc.gpsimd.tensor_copy(idx_now[:, par, :], cols_i[:, :, bass.ds(a, 1)].rearrange("p k b -> p (k b)"))\
                    .then_inc(idx_copied, 1)
                pool.wait_ge(idx_copied, a + 1)
                pool.sem_inc(gathering, 1)
                pool.indirect_dma_start(
                    out=xg[:, par, :], out_offset=None, in_=x1_dram,
                    in_offset=bass.IndirectOffsetOnAxis(ap=idx_now[:, par, 0:1], axis=0)).then_inc(x_in[par], 16)
                pool.indirect_dma_start(
                    out=rows_m[:], out_offset=None, in_=mask,
                    in_offset=bass.IndirectOffsetOnAxis(ap=idx_now[:, par, 2:3], axis=0)).then_inc(m_in, 16)

            def has_batch(a, least):
                return not isinstance(a, int) or a >= least

            def body(i, par):
                if mlp(i):
                    m, pm = i - 1, 1 - par
                    pool.wait_ge(row_ready, m + 1)
                    pool.sem_inc(scattering, 1)
                    pool.indirect_dma_start(
                        out=out, out_offset=bass.IndirectOffsetOnAxis(ap=idx_now[0:KS, pm, 0:1], axis=0),
                        in_=row[0:KS, pm, :], in_offset=None).then_inc(scattered[pm], 16)
                    pool.wait_ge(scattered[pm], (m - pm) * 8 + 16)
                if not (isinstance(i, int) and i >= B - 1):
                    gather(i + 1, 1 - par)

            gather(0, 0)
            steps(pool, body)

        @block.tensor
        def _(pe):
            pe.wait_ge(loaded, 16 * (SETUP_DMAS + WEIGHT_DMAS))
            pe.wait_ge(topk, TOPK)
            for j in range(4):
                last = pe.transpose(one["t0"][:, j * B:(j + 1) * B], rows_f[:, j, :], ident[0:B, 0:B])
            last = pe.transpose(one["t0"][:, 4 * B:5 * B], top[:], ident[0:B, 0:B])
            last.then_inc(cols_full, 1)
            for b in range(B):
                last = pe.matmul(banks["s"][:, b // 4, (b % 4) * K:(b % 4 + 1) * K], sel16[:, b, :],
                                 rows_f[:, 4, :], start=True, stop=True)
            last.then_inc(idxbc_full, 1)
            pe.wait_ge(folded, FOLDED)
            pe.wait_ge(cols_done, 6)

            def turn(bank, src, n=KD):
                for k in range(n):
                    last = pe.transpose(one[bank][:, k * P:(k + 1) * P], src[:, k * P:(k + 1) * P], ident[:])
                last.then_inc(full[bank], 1)

            def product(bank, xT, w, n):
                for k in range(n):
                    last = pe.matmul(one[bank], xT[:, k, :], w(k), start=(k == 0), stop=(k == n - 1))
                last.then_inc(full[bank], 1)

            def body(i, par):
                a, m, pm = i, i - 1, 1 - par
                if attention(i):
                    pe.wait_ge(norm, a * NORM + NORM)
                    fill(pe, i, "hnT")
                    turn("t0", hn)
                if mlp(i):
                    pe.wait_ge(norm2, m * NORM2 + NORM2)
                    fill(pe, i, "h2T")
                    turn("t1", h2[:, pm, :])
                if attention(i):
                    pe.wait_ge(free["t0"], use_number(i, "hnT") + 1)
                    for j, use in enumerate(("q", "k", "v")):
                        fill(pe, i, use)
                        product(BANK_OF[use], hnT, lambda k, j=j: w_qkv[:, j, k, :], KD)
                if mlp(i):
                    pe.wait_ge(free["t1"], use_number(i, "h2T") + 1)
                    for j in range(4):
                        fill(pe, i, f"up{j}")
                        product(BANK_OF[f"up{j}"], h2T, lambda k, j=j: w_1[:, k, j * HALF:(j + 1) * HALF], KD)
                if attention(i):
                    pe.wait_ge(m_in, a * 16 + 16)
                    for n in range(2):
                        fill(pe, i, f"GT{n}")
                        turn(BANK_OF[f"GT{n}"], rows_m[:, n * HALF:(n + 1) * HALF])
                    for j, use in enumerate(("qT", "kT")):
                        pe.wait_ge(rope, a * ROPE + 6 * (j + 1))
                        fill(pe, i, use)
                        turn(BANK_OF[use], qk[:, j, :])
                    pe.wait_ge(free["m0"], use_number(i, "qT") + 1)
                    pe.wait_ge(free["m1"], use_number(i, "kT") + 1)
                    fill(pe, i, "scores")
                    for k in range(KD):
                        for j in range(4):
                            last = pe.matmul(banks["s"][:, j, k * K:k * K + KS], qkT[j * HD:(j + 1) * HD, 0, k, :],
                                             qkT[j * HD:(j + 1) * HD, 1, k, 0:KS], start=True, stop=True)
                    last.then_inc(full["s"], 1)
                    pe.wait_ge(free["t0"], use_number(i, "GT1") + 1)
                    pe.wait_ge(free["t1"], use_number(i, "GT0") + 1)
                    pe.wait_ge(onehot_ready, a + 1)
                    fill(pe, i, "mask")
                    for t in range(TC):
                        last = pe.matmul(one["m0"][:, 0:K], GT[:, t, :], onehot[:, t, :],
                                         start=(t == 0), stop=(t == TC - 1))
                    last.then_inc(full["m0"], 1)
                if mlp(i):
                    for j in range(4):
                        bank = BANK_OF[f"up{j}"]
                        pe.wait_ge(free[bank], use_number(i, f"up{j}") + 1)
                        fill(pe, i, f"gT{j}")
                        turn(BANK_OF[f"gT{j}"], act_up[:, j * HALF:(j + 1) * HALF])
                    fill(pe, i, "down")
                    for j in range(4):
                        pe.wait_ge(free[BANK_OF[f"gT{j}"]], use_number(i, f"gT{j}") + 1)
                        for k in range(4 * j, 4 * j + 4):
                            last = pe.matmul(one["m1"], gT[:, k, :], w_2[:, k, :], start=(k == 0),
                                             stop=(k == F // P - 1))
                    last.then_inc(full["m1"], 1)
                if attention(i):
                    pe.wait_ge(exp_ready, a + 1)
                    fill(pe, i, "aT")
                    for h in range(H):
                        last = pe.transpose(banks["s"][0:KS, h // 4, (h % 4) * P:(h % 4 + 1) * P], prob[:, h, 0:KS],
                                            ident[:])
                    last.then_inc(full["s"], 1)
                    pe.wait_ge(free["s"], use_number(i, "aT") + 1)
                    pe.wait_ge(o_ready, a * 2 + 1)
                    fill(pe, i, "o")
                    for h in range(H):
                        hd = 4 * (h % 4) + h // 4
                        last = pe.matmul(one["m0"][:, hd * HD:(hd + 1) * HD], probT[0:KS, h, :],
                                         vsb[0:KS, hd * HD:(hd + 1) * HD], start=True, stop=True)
                    last.then_inc(full["m0"], 1)
                    pe.wait_ge(o_ready, a * 2 + 2)
                    fill(pe, i, "oT")
                    turn("t1", osb)
                    pe.wait_ge(free["t1"], use_number(i, "oT") + 1)
                    fill(pe, i, "attn")
                    product("m1", oT, lambda k: w_o[:, k, :], KD)

            steps(pe, body)

        @block.scalar
        def _(act):
            def copy(i, use, dst, rows=P):
                bank = filled(act, i, use)
                nc.scalar.activation(dst, one[bank][0:rows].rearrange("p (k t) -> p k t", t=P) if dst.ndim == 3
                                     else one[bank][0:rows], ACT.Copy).then_inc(free[bank], 1)

            act.wait_ge(angle, ANGLE)
            nc.scalar.activation(sin[:], ang[:, 0], ACT.Sin).then_inc(angle, 1)
            nc.scalar.activation(cos[:], ang[:, 1], ACT.Sin).then_inc(angle, 1)

            def inverse_root(chain, n, chain_act, na, var, spare, root):
                act.wait_ge(chain, n)
                nc.scalar.activation(spare, var, ACT.Ln).then_inc(chain_act, 1)
                act.wait_ge(chain_act, na + 1)
                nc.scalar.activation(root, spare, ACT.Exp, scale=-0.5).then_inc(chain_act, 1)

            def prepare(a, par):
                v = v1[:, par, :]
                inverse_root(norm, a * NORM + 8, norm_act, a * 5, v[:, 0:1], v[:, 7:8], v[:, 2:3])
                act.wait_ge(norm, a * NORM + 13)
                if not (isinstance(a, int) and a == 0):
                    act.wait_ge(norm_act, a * 5)
                nc.scalar.activation(sq[:], xn[:], ACT.Square, accum_out=v[:, 8:9]).then_inc(norm_act, 1)
                inverse_root(norm, a * NORM + 14, norm_act, a * 5 + 3, v[:, 9:10], v[:, 10:11], v[:, 11:12])

            prepare(0, 0)

            def body(i, par):
                a, m, pm = i, i - 1, 1 - par
                if attention(i):
                    copy(i, "hnT", hnT[:])
                if mlp(i):
                    copy(i, "h2T", h2T[:])
                if attention(i):
                    copy(i, "v", vsb[:])
                if mlp(i):
                    for j in range(4):
                        bank = filled(act, i, f"up{j}")
                        nc.scalar.activation(act_up[:, j * HALF:(j + 1) * HALF], one[bank],
                                             ACT.Gelu_apprx_tanh).then_inc(free[bank], 1)
                if attention(i):
                    copy(i, "qT", qkT[:, 0])
                    copy(i, "kT", qkT[:, 1])
                if mlp(i):
                    for j in range(4):
                        copy(i, f"gT{j}", gT[:, 4 * j:4 * j + 4, :])
                if attention(i):
                    act.wait_ge(soft, a * SOFT + 2)
                    nc.scalar.activation(prob[:, :, 0:KS], prob[:, :, 0:KS], ACT.Exp).then_inc(exp_ready, 1)
                    act.wait_ge(full["s"], use_number(i, "aT") + 1)
                    nc.scalar.activation(probT[0:KS, 0:8, :],
                                         banks["s"][0:KS, 0:2, :].rearrange("p j (k t) -> p (j k) t", t=P),
                                         ACT.Copy).then_inc(free["s"], 1)
                    copy(i, "oT", oT[:])
                    v = v1[:, par, :]
                    act.wait_ge(norm2, a * NORM2 + 1)
                    nc.scalar.activation(sq[:], x1f[:, par, :], ACT.Square, accum_out=v[:, 16:17])\
                        .then_inc(norm2_act, 1)
                    inverse_root(norm2, a * NORM2 + 2, norm2_act, a * 3 + 1, v[:, 17:18], v[:, 18:19], v[:, 19:20])
                    if not (isinstance(i, int) and i == B - 1):
                        prepare(i + 1, pm)

            steps(act, body)

        @block.vector
        def _(dve):
            V = nc.vector
            chain = [0]

            def link(ins):
                chain[0] += 1
                ins.then_inc(topk, 1)
                dve.wait_ge(topk, chain[0])

            dve.wait_ge(wts_in, 16)
            for r in range(K // 8):
                now, then = wts[:, r % 2, :], wts[:, 1 - r % 2, :]
                eight = slice(8 * r, 8 * r + 8)
                link(V.max(top[:, eight], now))
                link(V.max_index(topi[:, eight], top[:, eight], now))
                link(V.match_replace(then, top[:, eight], now, LOWEST))
            link(V.tensor_copy(rows_f[:, 4, :], topi[:]))
            dve.wait_ge(loaded, 16 * (SETUP_DMAS + WEIGHT_DMAS))
            for j, scale in enumerate((1.0, 1.0, 2.0)):
                link(V.tensor_scalar(rows_f[:, j, :], rows_f[:, 4, :], scale, batch[:, j:j + 1], ALU.mult, ALU.add))
            link(V.tensor_scalar(rows_f[:, 3, :], top[:], top[:, K - 1:K], None, ALU.is_le))
            assert chain[0] == TOPK
            dve.wait_ge(cols_full, 1)
            t0 = one["t0"]
            for j in range(3):
                V.tensor_copy(cols_i[:, j, :], t0[:, j * B:(j + 1) * B]).then_inc(cols_done, 1)
            V.tensor_copy(notsel[:], t0[:, 3 * B:4 * B]).then_inc(cols_done, 1)
            V.tensor_copy(wsel[:], t0[:, 4 * B:5 * B]).then_inc(cols_done, 1)
            dve.wait_ge(idxbc_full, 1)
            V.tensor_copy(idx_bc[:].rearrange("p b k -> p (b k)"),
                          banks["s"][:].rearrange("p j k -> p (j k)")).then_inc(cols_done, 1)
            for j in range(3):
                for k in range(KD):
                    V.tensor_scalar(w_qkv[:, j, k, :], w_qkv[:, j, k, :], g1[:, k:k + 1], None, ALU.mult)\
                     .then_inc(folded, 1)
            for k in range(KD):
                V.tensor_scalar(w_1[:, k, :], w_1[:, k, :], g2[:, k:k + 1], None, ALU.mult).then_inc(folded, 1)

            n = [0]

            def angle_step(ins):
                n[0] += 1
                ins.then_inc(angle, 1)
                dve.wait_ge(angle, n[0])

            dve.wait_ge(pos_in, 16 * B)
            angle_step(V.tensor_copy(pos_f[:], pos_i[:]))
            f3 = [P, B, HD // 2]
            angle_step(V.tensor_tensor(ang[:, 2], pos_f[:].unsqueeze(2).to_broadcast(f3),
                                       inv[:].unsqueeze(1).to_broadcast(f3), ALU.mult))
            angle_step(V.tensor_scalar(ang[:, 3], ang[:, 2], float(1 / (2 * np.pi)), MAGIC, ALU.mult, ALU.add))
            angle_step(V.tensor_scalar(ang[:, 1], ang[:, 3], MAGIC, None, ALU.subtract))
            angle_step(V.scalar_tensor_tensor(ang[:, 3], ang[:, 1], -TWO_PI_HI, ang[:, 2], ALU.mult, ALU.add))
            angle_step(V.scalar_tensor_tensor(ang[:, 2], ang[:, 1], -TWO_PI_LO, ang[:, 3], ALU.mult, ALU.add))
            angle_step(V.tensor_scalar(ang[:, 0], ang[:, 2], 3.1415925, -3.1415925, ALU.min, ALU.max))
            angle_step(V.scalar_tensor_tensor(ang[:, 3], ang[:, 0], -1.0, ang[:, 0], ALU.mult, ALU.max))
            angle_step(V.tensor_scalar(ang[:, 1], ang[:, 3], -1.0, float(np.pi / 2), ALU.mult, ALU.add))
            assert n[0] == ANGLE

            def newton(sem_, at, r0, v, t, u, r):
                V.tensor_tensor(t, r0, r0, ALU.mult).then_inc(sem_, 1)
                dve.wait_ge(sem_, at + 1)
                V.tensor_tensor(u, t, v, ALU.mult).then_inc(sem_, 1)
                dve.wait_ge(sem_, at + 2)
                V.tensor_scalar(t, u, -0.5, 1.5, ALU.mult, ALU.add).then_inc(sem_, 1)
                dve.wait_ge(sem_, at + 3)
                V.tensor_tensor(r, r0, t, ALU.mult).then_inc(sem_, 1)
                dve.wait_ge(sem_, at + 4)

            def prepare(a, par):
                v = v1[:, par, :]
                at = a * NORM
                c = lambda j: v[:, j:j + 1]
                dve.wait_ge(x_in[par], (a - par) * 8 + 16)
                if not (isinstance(a, int) and a == 0):
                    dve.wait_ge(full["t0"], use_number(a - 1, "hnT") + 1)
                    dve.wait_ge(norm2, (a - 1) * NORM2 + 1)
                V.bn_stats(st[:], xg[:, par, :]).then_inc(norm, 1)
                dve.wait_ge(norm, at + 1)
                V.tensor_tensor(c(3), st[:, 1:2], st[:, 4:5], ALU.add).then_inc(norm, 1)
                V.tensor_tensor(c(4), st[:, 1:2], st[:, 4:5], ALU.subtract).then_inc(norm, 1)
                V.tensor_tensor(c(5), st[:, 2:3], st[:, 5:6], ALU.add).then_inc(norm, 1)
                dve.wait_ge(norm, at + 4)
                V.tensor_scalar(c(1), c(3), 0.5, None, ALU.mult).then_inc(norm, 1)
                V.tensor_tensor(c(6), c(4), c(4), ALU.mult).then_inc(norm, 1)
                V.tensor_scalar(c(5), c(5), 1.0 / D, EPS, ALU.mult, ALU.add).then_inc(norm, 1)
                dve.wait_ge(norm, at + 7)
                V.scalar_tensor_tensor(c(0), c(6), 0.25, c(5), ALU.mult, ALU.add).then_inc(norm, 1)
                dve.wait_ge(norm_act, a * 5 + 2)
                newton(norm, at + 8, c(2), c(0), c(3), c(4), c(6))
                V.tensor_scalar(xn[:], xg[:, par, :], c(1), c(6), ALU.subtract, ALU.mult).then_inc(norm, 1)
                dve.wait_ge(norm_act, a * 5 + 3)
                V.tensor_scalar(c(9), c(8), 1.0 / D, 1e-6, ALU.mult, ALU.add).then_inc(norm, 1)
                dve.wait_ge(norm_act, a * 5 + 5)
                dve.wait_ge(norm, at + 14)
                newton(norm, at + 14, c(11), c(9), c(12), c(13), c(14))
                V.tensor_scalar(hn[:], xn[:], c(14), None, ALU.mult).then_inc(norm, 1)
                V.scalar_tensor_tensor(base[:, par, :], xn[:], notsel[:, bass.ds(a, 1)], xg[:, par, :],
                                       ALU.mult, ALU.add).then_inc(norm, 1)

            dve.wait_ge(cols_done, 6)
            prepare(0, 0)
            dve.wait_ge(angle, ANGLE + 2)

            def one_hot(a):
                if not (isinstance(a, int) and a == 0):
                    dve.wait_ge(full["m0"], use_number(a - 1, "mask") + 1)
                V.tensor_tensor(onehot[:], idx_bc[:, bass.ds(a, 1), :].to_broadcast([P, TC, K]),
                                token[:].unsqueeze(2).to_broadcast([P, TC, K]), ALU.is_equal)\
                 .then_inc(onehot_ready, 1)

            def rotate(i, j):
                bank = filled(dve, i, ("q", "k")[j])
                at = i * ROPE + 6 * j
                x = one[bank].rearrange("p (h e f) -> p h e f", h=H, e=2)
                r = rot[:, j, :].rearrange("p (h e f) -> p h e f", h=H, e=2)
                y = qk[:, j, :].rearrange("p (h e f) -> p h e f", h=H, e=2)
                s3 = [P, H, HD // 2]
                c = cos[:, bass.ds(i, 1), :].to_broadcast(s3)
                s = sin[:, bass.ds(i, 1), :].to_broadcast(s3)
                if not (isinstance(i, int) and i == 0):
                    dve.wait_ge(full[("m0", "m1")[j]], use_number(i - 1, ("qT", "kT")[j]) + 1)
                    dve.wait_ge(rope, at)
                V.tensor_tensor(y[:, :, 0, :], x[:, :, 0, :], c, ALU.mult).then_inc(rope, 1)
                V.tensor_tensor(r[:, :, 0, :], x[:, :, 1, :], s, ALU.mult).then_inc(rope, 1)
                V.tensor_tensor(y[:, :, 1, :], x[:, :, 1, :], c, ALU.mult).then_inc(rope, 1)
                V.tensor_tensor(r[:, :, 1, :], x[:, :, 0, :], s, ALU.mult).then_inc(rope, 1)
                dve.wait_ge(rope, at + 4)
                V.tensor_tensor(y[:, :, 0, :], y[:, :, 0, :], r[:, :, 0, :], ALU.subtract).then_inc(rope, 1)
                V.tensor_tensor(y[:, :, 1, :], y[:, :, 1, :], r[:, :, 1, :], ALU.add).then_inc(rope, 1)

            def body(i, par):
                a, m, pm = i, i - 1, 1 - par
                if attention(i):
                    for j, use in enumerate(("q", "k")):
                        rotate(i, j)
                        dve.wait_ge(rope, i * ROPE + 6 * j + 4)
                        dve.sem_inc(free[BANK_OF[use]], 1)
                    one_hot(a)
                    for n in range(2):
                        bank = filled(dve, i, f"GT{n}")
                        V.tensor_scalar(GT[:, 4 * n:4 * n + 4, :], one[bank].rearrange("p (k t) -> p k t", t=P),
                                        LOWEST, None, ALU.max).then_inc(free[bank], 1)
                    bank = filled(dve, i, "mask")
                    if not (isinstance(i, int) and i == 0):
                        dve.wait_ge(soft, a * SOFT)
                    V.tensor_copy(msel[:], one[bank][:, 0:K]).then_inc(free[bank], 1)
                    filled(dve, i, "scores")
                    dve.wait_ge(free[bank], use_number(i, "mask") + 1)
                    if not (isinstance(i, int) and i == 0):
                        dve.wait_ge(full["s"], use_number(i - 1, "aT") + 1)
                    at = a * SOFT
                    p3 = prob[:, :, 0:KS]
                    s3 = banks["s"][:].rearrange("p j (k t) -> p (j k) t", t=K)[:, :, 0:KS]
                    V.scalar_tensor_tensor(p3, s3, float(1 / np.sqrt(np.float32(HD))),
                                           msel[:, 0:KS].unsqueeze(1).to_broadcast([P, H, KS]), ALU.mult, ALU.add)\
                     .then_inc(free["s"], 1)
                    dve.wait_ge(free["s"], use_number(i, "scores") + 1)
                    V.tensor_reduce(mx[:, 0, :], p3, AX.X, ALU.max).then_inc(soft, 1)
                    dve.wait_ge(soft, at + 1)
                    V.tensor_tensor(p3, p3, mx[:, 0, :].unsqueeze(2).to_broadcast([P, H, KS]), ALU.subtract)\
                     .then_inc(soft, 1)
                if mlp(i):
                    bank = filled(dve, i, "down")
                    V.tensor_tensor(x1f[:, pm, :], one[bank], x1f[:, pm, :], ALU.add).then_inc(free[bank], 1)
                    dve.wait_ge(free[bank], use_number(i, "down") + 1)
                    if not (isinstance(i, int) and i < 3):
                        dve.wait_ge(scattered[pm], (m - pm) * 8)
                    V.scalar_tensor_tensor(row[:, pm, :], x1f[:, pm, :], wsel[:, bass.ds(m, 1)], base[:, pm, :],
                                           ALU.mult, ALU.add).then_inc(row_ready, 1)
                if attention(i):
                    at = a * SOFT
                    dve.wait_ge(exp_ready, a + 1)
                    V.tensor_reduce(mx[:, 1, :], prob[:, :, 0:KS], AX.X, ALU.add).then_inc(soft, 1)
                    dve.wait_ge(soft, at + 3)
                    V.reciprocal(mx[:, 2, :], mx[:, 1, :]).then_inc(soft, 1)
                    dve.wait_ge(full["s"], use_number(i, "aT") + 1)
                    V.tensor_copy(probT[0:KS, 8:16, :],
                                  banks["s"][0:KS, 2:4, :].rearrange("p j (k t) -> p (j k) t", t=P))\
                     .then_inc(o_ready, 1)
                    bank = filled(dve, i, "o")
                    dve.wait_ge(soft, at + 4)
                    V.tensor_tensor(osb[:].rearrange("p (k j e) -> p k j e", k=4, j=4),
                                    one[bank].rearrange("p (k j e) -> p k j e", k=4, j=4),
                                    mx[:, 2, :].rearrange("p (j k) -> p k j", j=4).unsqueeze(3)
                                    .to_broadcast([P, 4, 4, HD]), ALU.mult).then_inc(o_ready, 1)
                    dve.wait_ge(o_ready, a * 2 + 2)
                    dve.sem_inc(free[bank], 1)
                    bank = filled(dve, i, "attn")
                    v = v1[:, par, :]
                    n2 = a * NORM2
                    V.tensor_tensor(x1f[:, par, :], one[bank], xn[:], ALU.add).then_inc(norm2, 1)
                    dve.wait_ge(norm2, n2 + 1)
                    dve.sem_inc(free[bank], 1)
                    dve.wait_ge(norm2_act, a * 3 + 1)
                    V.tensor_scalar(v[:, 17:18], v[:, 16:17], 1.0 / D, 1e-6, ALU.mult, ALU.add).then_inc(norm2, 1)
                    dve.wait_ge(norm2_act, a * 3 + 3)
                    newton(norm2, n2 + 2, v[:, 19:20], v[:, 17:18], v[:, 20:21], v[:, 21:22], v[:, 22:23])
                    V.tensor_scalar(h2[:, par, :], x1f[:, par, :], v[:, 22:23], None, ALU.mult).then_inc(norm2, 1)
                    if not (isinstance(i, int) and i == B - 1):
                        prepare(i + 1, pm)

            steps(dve, body)


NORM = 20
NORM2 = 7
ROPE = 12
SOFT = 4
TOPK = 3 * (K // 8) + 5
ANGLE = 9
FOLDED = 3 * KD + KD


def layernorm_scan_and_chosen_tokens(nc, a, out, x1_dram, w_dram):
    with ExitStack() as semaphores:
        scan_phase(nc, semaphores, a["x"], a["A_log"], a["w_xproj"], a["w_dt"], a["dt_b"], a["D_col"],
                   a["router_w"], a["router_b"], a["ident"], a["state_sum"], a["repeat"], a["bc_rows"],
                   x1_dram, w_dram, out)
        ffn_phase(nc, semaphores, w_dram, x1_dram.rearrange("b l d -> (b l) d"), out.rearrange("b l d -> (b l) d"),
                  a["mask"], a["pos"], a["wq"], a["wk"], a["wv"], a["wo"], a["w1"], a["w2"], a["ln1"], a["ln2"],
                  a["ident"], a["batch_rows"], a["token"], a["batch_first"], a["inv_freq"])


def shape_constants(np):
    m = np.arange(P)
    bc_rows = np.zeros((2 * N, 2 * GROUPS, P), np.float32)
    for i in range(2 * GROUPS):
        bc_rows[N * (i % 2) + NT * (i // 2) + m // CH, i, m] = 1
    batch_rows = np.zeros((B, B, P), np.float32)
    batch_rows[np.arange(B), np.arange(B)] = 1
    b = np.arange(B)
    bm = np.minimum(b, BM - 1)
    inv = 1.0 / np.float32(10000.0) ** (np.arange(0, HD, 2, dtype=np.float32) / np.float32(HD))
    return {
        "ident": np.eye(P, dtype=np.float32),
        "state_sum": (m[:, None] % CH == np.arange(CH)[None]).astype(np.float32),
        "repeat": (m[:, None] % CH == m[None] % CH).astype(np.float32),
        "bc_rows": bc_rows,
        "batch_rows": batch_rows,
        "token": (m[:, None] + P * np.arange(TC)[None]).astype(np.float32),
        "batch_first": np.stack([b * L, bm * SM, bm * SM * (SM // L)], 1).astype(np.float32),
        "inv_freq": np.broadcast_to(inv.astype(np.float32), (P, HD // 2)),
    }


def kernel(**inputs):
    import numpy as np
    import concourse.bacc as bacc
    from concourse import mybir
    from concourse.bass_utils import run_bass_kernel_spmd

    i = {k: np.asarray(v) for k, v in inputs.items()}

    def rows(w):
        return w.reshape(-1, P, w.shape[1]).transpose(1, 0, 2)

    arrays = {
        "x": i["L0_attn_x"],
        "A_log": i["L0_attn_A_log"].reshape(CHUNKS, CH, GROUPS, NT).transpose(3, 1, 0, 2).reshape(P, TILES),
        "w_xproj": rows(i["L0_attn_x_proj_w"].T),
        "w_dt": i["L0_attn_dt_proj_w"].T,
        "dt_b": i["L0_attn_dt_proj_b"].reshape(KD, P).T,
        "D_col": i["L0_attn_D"].reshape(KD, P).T,
        "router_w": np.broadcast_to(i["L0_ffn_router_w"].reshape(1, D), (P, D)),
        "router_b": np.broadcast_to(i["L0_ffn_router_b"].reshape(1, 1), (P, 1)),
        "mask": i["L0_ffn_attention_mask"].reshape(-1, L),
        "pos": i["L0_ffn_position_ids"].reshape(-1, 1),
        "ln1": i["L0_ffn_ln1"].reshape(KD, P).T,
        "ln2": i["L0_ffn_ln2"].reshape(KD, P).T,
    }
    for name in ("wq", "wk", "wv", "wo", "w1", "w2"):
        arrays[name] = rows(i[f"L0_ffn_{name}"])
    arrays.update(shape_constants(np))
    arrays = {k: np.ascontiguousarray(v) for k, v in arrays.items()}

    nc = bacc.Bacc("TRN2", target_bir_lowering=False, num_devices=1)
    a = {k: nc.dram_tensor(f"in_{k}", v.shape, mybir.dt.from_np(v.dtype), kind="ExternalInput").ap()
         for k, v in arrays.items()}
    out = nc.dram_tensor("out_rows", (B, L, D), mybir.dt.float32, kind="ExternalOutput").ap()
    x1 = nc.dram_tensor("x1_rows", (B, L, D), mybir.dt.float32, kind="Internal").ap()
    w = nc.dram_tensor("router_weights", (B, L), mybir.dt.float32, kind="Internal").ap()
    layernorm_scan_and_chosen_tokens(nc, a, out, x1, w)
    r = run_bass_kernel_spmd(nc, [{f"in_{k}": v for k, v in arrays.items()}], core_ids=[0])
    return r.results[0]["out_rows"]
```

```python
from contextlib import ExitStack

import numpy as np

import concourse.bass as bass
from concourse import mybir

ALU = mybir.AluOpType
ACT = mybir.ActivationFunctionType
F32 = mybir.dt.float32
BF16 = mybir.dt.bfloat16
I32 = mybir.dt.int32
U32 = mybir.dt.uint32
AX = mybir.AxisListType

P = 128
EPS = 1e-5

B, L, D, N, R = 16, 1024, 512, 16, 64
CH = 32
NT = P // CH
CHUNKS = D // CH
GROUPS = N // NT
TILES = CHUNKS * GROUPS
TC = L // P
KD = D // P
HALF = 512

YADD = 2
TURN = ((7, 1), (7, 2), (7, 3), (8, 1), (8, 2), (8, 3), (9, 1), (9, 2))
COPY_XHAT = (7, 7, 8, 8, 8, 9, 9, 9)
PROJECT = (((9, 3),), ((10, 1), (10, 2)))
NORM1 = 7
ZSLOT = (0, 1)
Z = (11, 12, 13)
SKIP = (9, 10, 11, 12, 13, 13, 14, 15)
Z3 = 1
SOFTPLUS_NEXT = {12: ((0, 0), (0, 1)), 13: ((0, 2), (1, 0)), 14: ((1, 1),), 15: ((1, 2), (2, 0),)}
SOFTPLUS_NOW = {0: ((2, 1),), 4: ((2, 2), (3, 0),), 5: ((3, 1),), 7: ((3, 2),)}

USES = [("xhat", t) for t in range(TC)] + [("proj", 0), ("proj", 1)] + [("z", k, h) for k in range(KD) for h in range(2)]
USE = {key: u for u, key in enumerate(USES)}
NUSE = len(USES)
LN_VAR = TC + 7
LN1 = LN_VAR + 5
LN2 = LN1 + 1
ZSTEPS = 5
ZACT = 4


def scan_phase(nc, semaphores, x, A_log, w_xproj, w_dt, dt_b, D_row, router_w, router_b, ident_c, nsum_c, bc_dram,
               x1_dram, w_dram, out, nb_run=B):
    with ExitStack() as ctx:
        def sb(name, shape, dt=F32):
            return ctx.enter_context(nc.sbuf_tensor(name, shape, dt))

        def ps(name, shape, dt=F32):
            return ctx.enter_context(nc.psum_tensor(name, shape, dt))

        def sem(name):
            return semaphores.enter_context(nc.semaphore(name))

        decay = ps("decay", [P, 2, L])
        dx = ps("dx", [P, L])
        ps_y = ps("ps_y", [P, HALF])
        aux = ps("aux", [P, HALF])

        ident = sb("ident", [P, P])
        nsum = sb("nsum", [P, CH])
        xproj = sb("xproj", [P, KD, R + 2 * N])
        dtw = sb("dtw", [R, D])
        dtb = sb("dtb", [P, KD])
        drow = sb("drow", [P, D])
        a_neg = sb("a_neg", [P, CHUNKS * GROUPS])
        rw = sb("rw", [P, D])
        rb = sb("rb", [P, 1])

        xr = sb("xr", [P, 2, TC, D])
        xh = sb("xh", [P, 2, D])
        xs = sb("xs", [P, 2, D])
        xhT = sb("xhT", [P, KD, L])
        xpT = sb("xpT", [P, L])
        delT = sb("delT", [P, KD, L])
        dxT = sb("dxT", [P, KD, L])
        te = sb("te", [P, L])
        tu = sb("tu", [P, L])
        bmat = sb("bmat", [P, GROUPS, L])
        cmat = sb("cmat", [P, GROUPS, L])
        junk = sb("junk", [P, D], BF16)
        wcol = sb("wcol", [P, B * TC])
        wrow = xs[:, 0, 0:P]
        st1 = sb("st1", [P, TC, 6])
        mean1 = sb("mean1", [P, TC])
        r1 = sb("r1", [P, 7, TC])
        st2 = sb("st2", [P, TC, 6])
        mean2 = sb("mean2", [P, TC])
        r2 = sb("r2", [P, 9, TC])

        inp = sb("inp", [P, GROUPS, L])
        hid = sb("hid", [P, GROUPS, L])
        ch = sb("ch", [P, 2, L])
        ysb = sb("ysb", [P, 2 * P])
        delr = sb("delr", [P, 2, L])
        dxr = sb("dxr", [P, 2, L])

        consts_in = sem("consts_in")
        x_in = [[sem(f"x_in_{p}{h}") for h in "ab"] for p in ("even", "odd")]
        x1_out = sem("x1_out")
        out_done = [sem("out_done_a"), sem("out_done_b")]
        w_out = sem("w_out")
        bc_out = sem("bc_out")
        b_in = [sem(f"b_in_{g}") for g in range(GROUPS)]
        c_in = [sem(f"c_in_{g}") for g in range(GROUPS)]
        del_rep = [sem("del_rep_even"), sem("del_rep_odd")]
        dx_rep = [sem("dx_rep_even"), sem("dx_rep_odd")]
        repeating = sem("repeating")
        a_exp = sem("a_exp")
        a_ready = sem("a_ready")
        dx_ready = sem("dx_ready")
        decay_ready = sem("decay_ready")
        inp_ready = sem("inp_ready")
        hid_ready = sem("hid_ready")
        ch_ready = sem("ch_ready")
        ch_summed = sem("ch_summed")
        ysb_ready = sem("ysb_ready")
        yt_ready = sem("yt_ready")
        y_added = sem("y_added")
        aux_full = sem("aux_full")
        aux_emptied = sem("aux_emptied")
        z_act = sem("z_act")
        z_dve = sem("z_dve")
        ln1 = sem("ln1")
        ln1_act = sem("ln1_act")
        ln2 = sem("ln2")
        ln2_act = sem("ln2_act")
        xh_ready = sem("xh_ready")
        xs_ready = sem("xs_ready")
        skip_step = sem("skip_step")
        router_sum = sem("router_sum")
        out_made = sem("out_made")
        wt_ready = sem("wt_ready")
        wrow_ready = sem("wrow_ready")
        NCONST = 9

        def tile(b, c, g):
            return b * TILES + c * GROUPS + g

        def has(b, least):
            return not isinstance(b, int) or b >= least

        def batches(eng, body):
            body(0, 0)
            if nb_run > 2:
                with eng.Fori(1, nb_run - 2, 2) as i:
                    body(i, 1)
                    body(i + 1, 0)
            body(nb_run - 1, 1)

        def is_last(b):
            return isinstance(b, int) and b == nb_run - 1

        block = ctx.enter_context(nc.Block())

        @block.sync
        def _(sp):
            HT = TC // 2

            def load_x(b, par, h):
                if has(b, 2):
                    sp.wait_ge(out_done[h], b * 16 - 16)
                sp.dma_start(xr[:, par, h * HT:(h + 1) * HT],
                             x[b].rearrange("(t p) d -> p t d", p=P)[:, h * HT:(h + 1) * HT])\
                    .then_inc(x_in[par][h], 16)

            def store_x1(b, par):
                sp.wait_ge(y_added, b * CHUNKS + CHUNKS)
                sp.dma_start(x1_dram[b].rearrange("(t p) d -> p t d", p=P), xr[:, par]).then_inc(x1_out, 16)

            def store_out(b, par, h):
                sp.wait_ge(out_made, b * TC + (h + 1) * HT)
                sp.dma_start(out[b].rearrange("(t p) d -> p t d", p=P)[:, h * HT:(h + 1) * HT],
                             xr[:, par, h * HT:(h + 1) * HT]).then_inc(out_done[h], 16)

            def repeat(b, c):
                k, r = c // NT, CH * (c % NT)
                if r == 0:
                    sp.wait_ge(z_dve, b * KD * ZSTEPS + ZSTEPS * k + ZSTEPS)
                    sp.sem_inc(repeating, 1)
                if has(b, 1) or c >= 2:
                    sp.wait_ge(dx_ready, b * CHUNKS + c - 1)
                for n in range(NT):
                    sp.dma_start(dxr[n * CH:(n + 1) * CH, c % 2], dxT[r:r + CH, k]).then_inc(dx_rep[c % 2], 16)
                if has(b, 1) or c >= 2:
                    sp.wait_ge(decay_ready, tile(b, c - 1, 0))
                for n in range(NT):
                    sp.dma_start(delr[n * CH:(n + 1) * CH, c % 2], delT[r:r + CH, k]).then_inc(del_rep[c % 2], 16)

            def store_bc(b):
                sp.wait_ge(aux_emptied, b * NUSE + TC + 2)
                if has(b, 1):
                    for s in b_in + c_in:
                        sp.wait_ge(s, b * 16)
                sp.dma_start(bc_dram, xpT[R:R + 2 * N]).then_inc(bc_out, 16)

            def spread(b, g, which):
                if g == 0 and which == 0:
                    sp.wait_ge(bc_out, b * 16 + 16)
                    sp.sem_inc(repeating, 1)
                if has(b, 1):
                    sp.wait_ge((inp_ready, ch_ready)[which], tile(b, 0, 0) - GROUPS + g + 1)
                row = which * N + g * NT
                sp.dma_start((bmat, cmat)[which][:, g],
                             bc_dram[row:row + NT].unsqueeze(1).to_broadcast([NT, CH, L]))\
                    .then_inc((b_in, c_in)[which][g], 16)

            for h in range(2):
                load_x(0, 0, h)
            for dst, src in ((ident[:], ident_c), (nsum[:], nsum_c), (xproj[:], w_xproj), (dtw[:], w_dt),
                             (dtb[:], dt_b), (drow[:], D_row), (a_neg[:], A_log), (rw[:], router_w),
                             (rb[:], router_b)):
                sp.dma_start(dst, src).then_inc(consts_in, 16)
            store_bc(0)
            for g in range(GROUPS):
                spread(0, g, 0)
            for c in range(2):
                repeat(0, c)
            for g in range(GROUPS):
                spread(0, g, 1)

            def body(b, par):
                final = is_last(b)
                for c in range(CHUNKS):
                    if c < CHUNKS - 2:
                        repeat(b, c + 2)
                    elif not final:
                        repeat(b + 1, c + 2 - CHUNKS)
                    if has(b, 1):
                        if c == 0:
                            store_x1(b - 1, 1 - par)
                        if c in (3, 4):
                            store_out(b - 1, 1 - par, c - 3)
                    if final:
                        continue
                    if c in (4, 5):
                        load_x(b + 1, 1 - par, c - 4)
                    if c == PROJECT[1][0][0] + 1:
                        store_bc(b + 1)
                    if c in (14, 15):
                        for g in range(GROUPS):
                            spread(b + 1, g, c - 14)

            batches(sp, body)
            store_x1(nb_run - 1, 1)
            for h in range(2):
                store_out(nb_run - 1, 1, h)
            sp.wait_ge(wrow_ready, 1)
            sp.dma_start(w_dram.rearrange("b (t p) -> (b t) p", p=P)[0:nb_run * TC], wrow[0:nb_run * TC])\
                .then_inc(w_out, 16)
            sp.wait_ge(w_out, 16)
            sp.wait_ge(bc_out, 16 * nb_run)
            sp.wait_ge(x1_out, 16 * nb_run)
            for h in range(2):
                sp.wait_ge(out_done[h], 16 * nb_run)

        @block.tensor
        def _(pe):
            def aux_free(b, key):
                u = USE[key]
                if has(b, 1) or u > 0:
                    pe.wait_ge(aux_emptied, b * NUSE + u)

            def turn_xhat(b, t):
                aux_free(b, ("xhat", t))
                pe.wait_ge(xh_ready, b * TC + t + 1)
                for k in range(KD):
                    last = pe.transpose(aux[:, k * P:(k + 1) * P], xh[:, t % 2, k * P:(k + 1) * P], ident[:])
                last.then_inc(aux_full, 1)

            def project(b, h, ks=range(KD)):
                if 0 in ks:
                    aux_free(b, ("proj", h))
                for k in ks:
                    last = pe.matmul(aux[0:R + 2 * N, :], xproj[:, k, :], xhT[:, k, h * HALF:(h + 1) * HALF],
                                     start=(k == 0), stop=(k == KD - 1))
                if KD - 1 in ks:
                    last.then_inc(aux_full, 1)

            def step_size(b, k, h):
                aux_free(b, ("z", k, h))
                pe.matmul(aux[:], dtw[:, k * P:(k + 1) * P], xpT[0:R, h * HALF:(h + 1) * HALF],
                          start=True, stop=True).then_inc(aux_full, 1)

            def sum_states(b, c, g):
                if g == 0 and (has(b, 1) or c > 0):
                    pe.wait_ge(y_added, b * CHUNKS + c)
                pe.wait_ge(ch_ready, tile(b, c, g) + 1)
                for q in range(4):
                    last = pe.matmul(ps_y[q * CH:(q + 1) * CH, 0:2 * P], nsum[:],
                                     ch[:, g % 2, q * 2 * P:(q + 1) * 2 * P],
                                     start=(g == 0), stop=(g == GROUPS - 1))
                last.then_inc(ch_summed, 1)

            def turn_y(b, c):
                pe.wait_ge(ysb_ready, b * CHUNKS + c + 1)
                for t in range(2):
                    last = pe.transpose(ps_y[:, (2 + t) * P:(3 + t) * P], ysb[:, t * P:(t + 1) * P], ident[:])
                last.then_inc(yt_ready, 1)

            pe.wait_ge(consts_in, 16 * NCONST)
            for t in range(TC):
                turn_xhat(0, t)
            for h in range(2):
                project(0, h)
            for k in range(3):
                for h in range(2):
                    step_size(0, k, h)

            def body(b, par):
                final = is_last(b)
                for c in range(CHUNKS):
                    if c > 0:
                        turn_y(b, c - 1)
                    elif has(b, 1):
                        turn_y(b - 1, CHUNKS - 1)
                    for g in range(GROUPS):
                        sum_states(b, c, g)
                        if c == Z3:
                            for h in range(2):
                                if ZSLOT[h] == g:
                                    step_size(b, 3, h)
                        if final:
                            continue
                        for t in range(TC):
                            if TURN[t] == (c, g):
                                turn_xhat(b + 1, t)
                        for h in range(2):
                            if (c, g) in PROJECT[h]:
                                at = PROJECT[h].index((c, g))
                                per = KD // len(PROJECT[h])
                                project(b + 1, h, range(at * per, at * per + per))
                        if c in Z:
                            for h in range(2):
                                if ZSLOT[h] == g:
                                    step_size(b + 1, Z.index(c), h)

            batches(pe, body)
            turn_y(nb_run - 1, CHUNKS - 1)
            pe.wait_ge(router_sum, 10 * nb_run)
            pe.wait_ge(aux_emptied, nb_run * NUSE)
            pe.transpose(aux[0:nb_run * TC, 0:P], wcol[:, 0:nb_run * TC], ident[:]).then_inc(wt_ready, 1)

        @block.scalar
        def _(act):
            def aux_filled(b, key):
                act.wait_ge(aux_full, b * NUSE + USE[key] + 1)

            def normalise(b, par, t):
                if t == 0:
                    act.wait_ge(ln1, b * LN1 + LN1)
                if t >= 2:
                    act.wait_ge(aux_full, b * NUSE + t - 1)
                elif has(b, 1):
                    act.wait_ge(aux_full, b * NUSE - NUSE + TC - 1 + t)
                nc.scalar.activation(xh[:, t % 2, :], xr[:, par, t, :], ACT.Identity, scale=r1[:, 4, t:t + 1],
                                     bias=r1[:, 6, t:t + 1]).then_inc(xh_ready, 1)

            def normalise_again(b, par, t):
                if t >= 2:
                    act.wait_ge(skip_step, b * 2 * TC + 2 * (t - 1))
                elif has(b, 1):
                    act.wait_ge(skip_step, b * 2 * TC - 2 * TC + 2 * (TC - 1 + t))
                nc.scalar.activation(xs[:, t % 2, :], xr[:, par, t, :], ACT.Identity, scale=r1[:, 4, t:t + 1],
                                     bias=r1[:, 6, t:t + 1]).then_inc(xs_ready, 1)

            def copy_xhat(b, t):
                aux_filled(b, ("xhat", t))
                if t == 0 and has(b, 1):
                    act.wait_ge(z_dve, b * KD * ZSTEPS)
                nc.scalar.activation(xhT[:, :, t * P:(t + 1) * P], aux[:].rearrange("p (k t) -> p k t", k=KD),
                                     ACT.Copy).then_inc(aux_emptied, 1)

            def copy_proj(b, h):
                aux_filled(b, ("proj", h))
                if has(b, 1) and h == 0:
                    act.wait_ge(bc_out, b * 16)
                nc.scalar.activation(xpT[0:R + 2 * N, h * HALF:(h + 1) * HALF], aux[0:R + 2 * N],
                                     ACT.Copy).then_inc(aux_emptied, 1)

            def softplus_a(b, k):
                n = b * KD * ZACT + k * ZACT
                if has(b, 1) or k > 0:
                    act.wait_ge(z_dve, b * KD * ZSTEPS + ZSTEPS * k - 3)
                    act.wait_ge(z_act, n)
                if has(b, 1):
                    for s in dx_rep + del_rep:
                        act.wait_ge(s, (b * (CHUNKS // 2) - CHUNKS // 2 + 2 * k + 2) * 16 * NT)
                for h in range(2):
                    half = slice(h * HALF, (h + 1) * HALF)
                    aux_filled(b, ("z", k, h))
                    nc.scalar.activation(te[:, half], aux[:], ACT.Abs, bias=dtb[:, k:k + 1]).then_inc(z_act, 1)
                    nc.scalar.activation(dxT[:, k, half], aux[:], ACT.Relu, bias=dtb[:, k:k + 1])\
                        .then_inc(aux_emptied, 1)
                act.wait_ge(z_act, n + 2)
                nc.scalar.activation(te[:], te[:], ACT.Exp, scale=-1.0).then_inc(z_act, 1)
                act.wait_ge(z_act, n + 3)
                nc.scalar.activation(delT[:, k, :], te[:], ACT.Ln, bias=1.0).then_inc(z_act, 1)

            def rstd(b, chain, chain_act, r, at, per):
                act.wait_ge(chain, b * per + at)
                nc.scalar.activation(r[:, 1, :], r[:, 0, :], ACT.Ln).then_inc(chain_act, 1)
                act.wait_ge(chain_act, b * 2 + 1)
                nc.scalar.activation(r[:, 2, :], r[:, 1, :], ACT.Exp, scale=-0.5).then_inc(chain_act, 1)

            def make_out(b, par, t):
                if t % 4 == 0:
                    act.wait_ge(ln2, b * LN2 + LN2)
                    act.wait_ge(router_sum, b * 10 + t + 4)
                    act.wait_ge(x1_out, b * 16 + 16)
                nc.scalar.activation(xr[:, par, t, :], xr[:, par, t, :], ACT.Identity, scale=r2[:, 7, t:t + 1],
                                     bias=r2[:, 6, t:t + 1]).then_inc(out_made, 1)

            def exp_decay(b, c, g):
                if has(b, 1) or c * GROUPS + g >= 2:
                    act.wait_ge(hid_ready, tile(b, c, g) - 1)
                if g == 0:
                    act.wait_ge(del_rep[c % 2], (b * (CHUNKS // 2) + c // 2 + 1) * 16 * NT)
                i = c * GROUPS + g
                nc.scalar.activation(decay[:, g % 2, :], delr[:, c % 2, :], ACT.Exp, scale=a_neg[:, i:i + 1])\
                    .then_inc(decay_ready, 1)

            def copy_dx(b, c):
                act.wait_ge(dx_rep[c % 2], (b * (CHUNKS // 2) + c // 2 + 1) * 16 * NT)
                if has(b, 1) or c >= 1:
                    act.wait_ge(inp_ready, tile(b, c, 0))
                nc.scalar.activation(dx[:], dxr[:, c % 2, :], ACT.Copy).then_inc(dx_ready, 1)

            def copy_y(b, c):
                act.wait_ge(ch_summed, tile(b, c, GROUPS - 1) + 1)
                if has(b, 1) or c >= 1:
                    act.wait_ge(yt_ready, b * CHUNKS + c)
                nc.scalar.activation(ysb[:], ps_y[:, 0:2 * P], ACT.Copy).then_inc(ysb_ready, 1)

            nc.scalar.preload_act_table_set("natural_log_exp_and_others")
            act.wait_ge(consts_in, 16 * NCONST)
            nc.scalar.activation(a_neg[:], a_neg[:], ACT.Exp).then_inc(a_exp, 1)
            act.wait_ge(a_exp, 1)
            nc.scalar.mul(a_neg[:], a_neg[:], -1.0).then_inc(a_ready, 1)
            act.wait_ge(a_ready, 1)
            rstd(0, ln1, ln1_act, r1, LN_VAR, LN1)
            for t in range(2):
                normalise(0, 0, t)
            for t in range(TC):
                copy_xhat(0, t)
                if t + 2 < TC:
                    normalise(0, 0, t + 2)
            for h in range(2):
                copy_proj(0, h)
            softplus_a(0, 0)
            for t in range(2):
                normalise_again(0, 0, t)
            for k in (1, 2):
                softplus_a(0, k)
            for t in range(2, TC):
                normalise_again(0, 0, t)
            copy_dx(0, 0)
            for g in range(2):
                exp_decay(0, 0, g)

            def body(b, par):
                final = is_last(b)
                other = 1 - par
                for c in range(CHUNKS):
                    nxt = (b, c + 1) if c < CHUNKS - 1 else (b + 1, 0)
                    exp_decay(b, c, 2)
                    if c > 0:
                        copy_y(b, c - 1)
                    elif has(b, 1):
                        copy_y(b - 1, CHUNKS - 1)
                    exp_decay(b, c, 3)
                    if not (final and c == CHUNKS - 1):
                        copy_dx(*nxt)
                        for g in (0, 1):
                            exp_decay(*nxt, g)
                    if c == Z3:
                        softplus_a(b, 3)
                    if has(b, 1):
                        if c == 1:
                            rstd(b - 1, ln2, ln2_act, r2, LN_VAR, LN2)
                        if c in (2, 3):
                            for t in range(4 * (c - 2), 4 * (c - 1)):
                                make_out(b - 1, other, t)
                    if final:
                        continue
                    if c == NORM1 - 1:
                        rstd(b + 1, ln1, ln1_act, r1, LN_VAR, LN1)
                    if c == NORM1:
                        for t in range(2):
                            normalise(b + 1, other, t)
                    for t in range(TC):
                        if COPY_XHAT[t] == c:
                            copy_xhat(b + 1, t)
                            if t + 2 < TC:
                                normalise(b + 1, other, t + 2)
                    if c == PROJECT[0][0][0] + 1:
                        copy_proj(b + 1, 0)
                    if c in Z:
                        softplus_a(b + 1, Z.index(c))
                    for t in range(TC):
                        if SKIP[t] == c + 1:
                            normalise_again(b + 1, other, t)
                    if c == PROJECT[1][0][0]:
                        copy_proj(b + 1, 1)

            batches(act, body)
            last = nb_run - 1
            copy_y(last, CHUNKS - 1)
            rstd(last, ln2, ln2_act, r2, LN_VAR, LN2)
            for t in range(TC):
                make_out(last, 1, t)

        @block.vector
        def _(dve):
            def stats(par, t, s, chain):
                nc.vector.bn_stats(s[:, t, :], xr[:, par, t, :]).then_inc(chain, 1)

            def moments(b, s, mean, r, chain, per):
                n = b * per + TC
                dve.wait_ge(chain, n)
                nc.vector.tensor_tensor(r[:, 3, :], s[:, :, 1], s[:, :, 4], ALU.add).then_inc(chain, 1)
                nc.vector.tensor_tensor(r[:, 4, :], s[:, :, 1], s[:, :, 4], ALU.subtract).then_inc(chain, 1)
                nc.vector.tensor_tensor(r[:, 5, :], s[:, :, 2], s[:, :, 5], ALU.add).then_inc(chain, 1)
                dve.wait_ge(chain, n + 3)
                nc.vector.tensor_scalar(mean[:], r[:, 3, :], 0.5, None, ALU.mult).then_inc(chain, 1)
                nc.vector.tensor_tensor(r[:, 2, :], r[:, 4, :], r[:, 4, :], ALU.mult).then_inc(chain, 1)
                nc.vector.tensor_scalar(r[:, 1, :], r[:, 5, :], 1.0 / D, EPS, ALU.mult, ALU.add).then_inc(chain, 1)
                dve.wait_ge(chain, n + 6)
                nc.vector.scalar_tensor_tensor(r[:, 0, :], r[:, 2, :], 0.25, r[:, 1, :], ALU.mult, ALU.add)\
                    .then_inc(chain, 1)

            def newton(b, mean, r, chain, chain_act, per):
                dve.wait_ge(chain_act, b * 2 + 2)
                n = b * per + TC + 7
                nc.vector.tensor_tensor(r[:, 3, :], r[:, 2, :], r[:, 2, :], ALU.mult).then_inc(chain, 1)
                dve.wait_ge(chain, n + 1)
                nc.vector.tensor_tensor(r[:, 5, :], r[:, 3, :], r[:, 0, :], ALU.mult).then_inc(chain, 1)
                dve.wait_ge(chain, n + 2)
                nc.vector.tensor_scalar(r[:, 3, :], r[:, 5, :], -0.5, 1.5, ALU.mult, ALU.add).then_inc(chain, 1)
                dve.wait_ge(chain, n + 3)
                nc.vector.tensor_tensor(r[:, 4, :], r[:, 2, :], r[:, 3, :], ALU.mult).then_inc(chain, 1)
                dve.wait_ge(chain, n + 4)
                nc.vector.scalar_tensor_tensor(r[:, 6, :], mean[:], -1.0, r[:, 4, :], ALU.mult, ALU.mult)\
                    .then_inc(chain, 1)

            def ln1_stats(b, par, h):
                dve.wait_ge(x_in[par][h], (b - par) * 8 + 16)
                if h == 0 and has(b, 1):
                    dve.wait_ge(xs_ready, b * TC)
                for t in range(4 * h, 4 * h + 4):
                    stats(par, t, st1, ln1)

            def softplus(b, k, steps):
                na = b * KD * ZACT + ZACT * k
                n = b * KD * ZSTEPS + ZSTEPS * k
                if 0 in steps:
                    dve.wait_ge(z_act, na + 3)
                    if has(b, 1) or k > 0:
                        dve.wait_ge(z_dve, n)
                    nc.vector.tensor_scalar(tu[:], te[:], 1.0, None, ALU.add).then_inc(z_dve, 1)
                    dve.wait_ge(z_dve, n + 1)
                    nc.vector.scalar_tensor_tensor(tu[:], tu[:], 1.0, te[:], ALU.subtract, ALU.subtract)\
                        .then_inc(z_dve, 1)
                if 1 in steps:
                    dve.wait_ge(z_act, na + 4)
                    dve.wait_ge(z_dve, n + 2)
                    nc.vector.tensor_tensor(delT[:, k, :], delT[:, k, :], tu[:], ALU.subtract).then_inc(z_dve, 1)
                    dve.wait_ge(aux_emptied, b * NUSE + USE[("z", k, 1)] + 1)
                    dve.wait_ge(z_dve, n + 3)
                    nc.vector.tensor_tensor(delT[:, k, :], delT[:, k, :], dxT[:, k, :], ALU.add).then_inc(z_dve, 1)
                if 2 in steps:
                    dve.wait_ge(z_dve, n + 4)
                    nc.vector.tensor_tensor(dxT[:, k, :], delT[:, k, :], xhT[:, k, :], ALU.mult).then_inc(z_dve, 1)

            def make_input(b, c, g):
                if g == 0:
                    dve.wait_ge(dx_ready, b * CHUNKS + c + 1)
                if c == 0:
                    dve.wait_ge(b_in[g], b * 16 + 16)
                if has(b, 1) or c > 0:
                    dve.wait_ge(hid_ready, tile(b, c, g) - GROUPS + 1)
                nc.vector.tensor_tensor(inp[:, g, :], dx[:], bmat[:, g, :], ALU.mult).then_inc(inp_ready, 1)

            def scan(b, c, g):
                dve.wait_ge(decay_ready, tile(b, c, g) + 1)
                dve.wait_ge(inp_ready, tile(b, c, g) + 1)
                if has(b, 1) or c > 0:
                    dve.wait_ge(ch_ready, tile(b, c, g) - GROUPS + 1)
                nc.vector.tensor_tensor_scan(hid[:, g, :], decay[:, g % 2, :], inp[:, g, :],
                                             0.0, ALU.mult, ALU.add).then_inc(hid_ready, 1)

            def add_y(b, par, c):
                dve.wait_ge(yt_ready, b * CHUNKS + c + 1)
                if c == 0:
                    dve.wait_ge(skip_step, b * 2 * TC + 2 * TC)
                x1 = xr[:, par, :, c * CH:(c + 1) * CH].rearrange("p (q t) d -> p t q d", t=2)
                y = ps_y[:, 2 * P:4 * P].rearrange("p (t q d) -> p t q d", t=2, q=4)
                nc.vector.tensor_tensor(x1, x1, y, ALU.add).then_inc(y_added, 1)

            def ln2_stats(b, par, h):
                if h == 0:
                    dve.wait_ge(y_added, b * CHUNKS + CHUNKS)
                    if has(b, 1):
                        dve.wait_ge(out_made, b * TC)
                for t in range(4 * h, 4 * h + 4):
                    stats(par, t, st2, ln2)

            def ln2_finish(b):
                newton(b, mean2, r2, ln2, ln2_act, LN2)
                nc.vector.tensor_scalar(r2[:, 7, :], r2[:, 4, :], 1.0, None, ALU.add).then_inc(ln2, 1)

            def router(b, par, h):
                for t in range(4 * h, 4 * h + 4):
                    if has(b, 1) or t > 0:
                        dve.wait_ge(router_sum, b * 10 + t)
                    nc.vector.scalar_tensor_tensor(junk[:], xr[:, par, t, :], mean2[:, t:t + 1], rw[:],
                                                   ALU.subtract, ALU.mult, accum_out=r2[:, 8, t:t + 1])\
                        .then_inc(router_sum, 1)
                if h == 0:
                    return
                dve.wait_ge(router_sum, b * 10 + TC)
                nc.vector.tensor_tensor(r2[:, 3, :], r2[:, 8, :], r2[:, 4, :], ALU.mult).then_inc(router_sum, 1)
                dve.wait_ge(router_sum, b * 10 + TC + 1)
                nc.vector.tensor_scalar(wcol[:, bass.ds(b * TC, TC)], r2[:, 3, :], rb[:, 0:1], None, ALU.add)\
                    .then_inc(router_sum, 1)

            dve.wait_ge(consts_in, 16 * NCONST)
            for h in range(2):
                ln1_stats(0, 0, h)
            moments(0, st1, mean1, r1, ln1, LN1)
            newton(0, mean1, r1, ln1, ln1_act, LN1)
            for k in range(2):
                softplus(0, k, (0, 1, 2))
            softplus(0, 2, (0,))
            for g in range(GROUPS):
                make_input(0, 0, g)

            def body(b, par):
                final = is_last(b)
                other = 1 - par
                for c in range(CHUNKS):
                    for g in range(GROUPS):
                        scan(b, c, g)
                        if g == YADD:
                            if c >= 1:
                                add_y(b, par, c - 1)
                            elif has(b, 1):
                                add_y(b - 1, other, CHUNKS - 1)
                    if has(b, 1):
                        if c in (0, 1):
                            ln2_stats(b - 1, other, c)
                        if c == 1:
                            moments(b - 1, st2, mean2, r2, ln2, LN2)
                        if c == 2:
                            ln2_finish(b - 1)
                        if c in (2, 3):
                            router(b - 1, other, c - 2)
                    if c in SOFTPLUS_NOW:
                        for k, step in SOFTPLUS_NOW[c]:
                            softplus(b, k, (step,))
                    if not final:
                        if c in (NORM1 - 2, NORM1 - 1):
                            ln1_stats(b + 1, other, c - NORM1 + 2)
                        if c == NORM1 - 1:
                            moments(b + 1, st1, mean1, r1, ln1, LN1)
                        if c in SOFTPLUS_NEXT:
                            for k, step in SOFTPLUS_NEXT[c]:
                                softplus(b + 1, k, (step,))
                    for g in range(GROUPS):
                        if c < CHUNKS - 1:
                            make_input(b, c + 1, g)
                        elif not final:
                            make_input(b + 1, 0, g)
                    if c == NORM1 - 1 and not final:
                        newton(b + 1, mean1, r1, ln1, ln1_act, LN1)

            batches(dve, body)
            last = nb_run - 1
            add_y(last, 1, CHUNKS - 1)
            for h in range(2):
                ln2_stats(last, 1, h)
            moments(last, st2, mean2, r2, ln2, LN2)
            ln2_finish(last)
            for h in range(2):
                router(last, 1, h)
            dve.wait_ge(wt_ready, 1)
            nc.vector.tensor_copy(wrow[0:nb_run * TC], aux[0:nb_run * TC, 0:P]).then_inc(wrow_ready, 1)

        @block.gpsimd
        def _(pool):
            def skip_term(b, par, t):
                n = b * 2 * TC + 2 * t
                pool.wait_ge(xs_ready, b * TC + t + 1)
                nc.gpsimd.tensor_tensor(xs[:, t % 2, :], xs[:, t % 2, :], drow[:], ALU.mult).then_inc(skip_step, 1)
                pool.wait_ge(skip_step, n + 1)
                pool.wait_ge(xh_ready, b * TC + t + 1)
                nc.gpsimd.tensor_tensor(xr[:, par, t, :], xr[:, par, t, :], xs[:, t % 2, :], ALU.add)\
                    .then_inc(skip_step, 1)

            def body(b, par):
                for c in range(CHUNKS):
                    for g in range(GROUPS):
                        pool.wait_ge(hid_ready, tile(b, c, g) + 1)
                        if c == 0:
                            pool.wait_ge(c_in[g], b * 16 + 16)
                        if has(b, 1) or c * GROUPS + g >= 2:
                            pool.wait_ge(ch_summed, tile(b, c, g) - 1)
                        nc.gpsimd.tensor_tensor(ch[:, g % 2, :], hid[:, g, :], cmat[:, g, :],
                                                ALU.mult).then_inc(ch_ready, 1)
                        for t in range(TC):
                            if not is_last(b) and SKIP[t] == c and g == 2 * (t % 2):
                                skip_term(b + 1, 1 - par, t)

            pool.wait_ge(consts_in, 16 * NCONST)
            for t in range(TC):
                skip_term(0, 0, t)
            batches(pool, body)


K = 128
KS = K - 1
H, HD, F = 16, 32, 2048
BM, SM = 4, 2048
LOWEST = -3.0e38
MAGIC = 12582912.0
TWO_PI_HI = 6.28125
TWO_PI_LO = 2 * np.pi - TWO_PI_HI

MLP = {"h2T", "up0", "up1", "up2", "up3", "gT0", "gT1", "gT2", "gT3", "down"}
AHEAD = ("hnT", "v")
BANK_USES = {
    "t0": ["up0", "up2", "GT0", "gT0", "gT2", "hnT", "v"],
    "t1": ["h2T", "up1", "up3", "GT1", "gT1", "gT3", "oT"],
    "m0": ["q", "qT", "mask", "o"],
    "m1": ["k", "kT", "down", "attn"],
    "s": ["scores", "aT"],
}
BANK_OF = {use: bank for bank, uses in BANK_USES.items() for use in uses}


def use_number(i, use):
    bank = BANK_OF[use]
    uses = BANK_USES[bank]
    ahead = len(AHEAD) if bank == "t0" else 0
    if isinstance(i, int) and i == -1:
        return AHEAD.index(use)
    if isinstance(i, int) and i == 0:
        return ahead + [u for u in uses if u not in MLP].index(use)
    skipped = sum(u in MLP for u in uses)
    if isinstance(i, int) and i == B:
        return i * len(uses) - skipped + [u for u in uses if u in MLP].index(use)
    return ahead + i * len(uses) - skipped + uses.index(use)


def ffn_phase(nc, semaphores, w_dram, x1_dram, out, mask, pos, wq, wk, wv, wo, w1, w2, ln1, ln2, ident_c, sel16_c, token_c,
              batch_c, inv_c):
    with ExitStack() as ctx:
        def sb(name, shape, dt=F32):
            return ctx.enter_context(nc.sbuf_tensor(name, shape, dt))

        def sem(name):
            return semaphores.enter_context(nc.semaphore(name))

        banks = {name: ctx.enter_context(nc.psum_tensor(f"ps_{name}", [P, n, HALF], F32))
                 for name, n in (("s", 4), ("t0", 1), ("t1", 1), ("m0", 1), ("m1", 1))}
        one = {name: banks[name][:, 0, :] for name in ("t0", "t1", "m0", "m1")}

        ident = sb("identf", [P, P])
        token = sb("token", [P, TC])
        batch = sb("batch", [B, 3])
        inv = sb("inv", [P, HD // 2])
        w_qkv = sb("w_qkv", [P, 3, KD, D])
        w_o = sb("w_o", [P, KD, D])
        w_1 = sb("w_1", [P, KD, F])
        w_2 = sb("w_2", [P, F // P, D])
        g1 = sb("g1", [P, KD])
        g2 = sb("g2", [P, KD])

        top = sb("top", [B, K])
        topi = sb("topi", [B, K], U32)
        rows_f = sb("rows_f", [B, 5, K])
        cols_i = sb("cols_i", [P, 3, B], U32)
        wsel = sb("wsel", [P, B])
        notsel = sb("notsel", [P, B])
        idx_bc = sb("idx_bc", [P, B, K])
        pos_i = sb("pos_i", [P, B], I32)
        pos_f = sb("pos_f", [P, B])
        cos = sb("cos", [P, B, HD // 2])
        sin = sb("sin", [P, B, HD // 2])

        idx_x = sb("idx_x", [P, 2, 1], U32)
        idx_m = sb("idx_m", [P, 2, 1], U32)
        idx_out = sb("idx_out", [P, 2, 1], U32)
        xg = sb("xg", [P, 2, D])
        rows_m = sb("rows_m", [P, L])
        xn = sb("xn", [P, 2, D])
        base = sb("base", [P, 2, D])
        hn = sb("hn", [P, D])
        hnT = sb("hnT", [P, KD, P])
        qk = sb("qk", [P, 2, D])
        rot = sb("rot", [P, D])
        vsb = sb("vsb", [P, 2, D])
        qkT = sb("qkT", [P, 2, KD, P])
        onehot = sb("onehot", [P, TC, K])
        GT = sb("GT", [P, TC, P])
        msel = sb("msel", [P, K])
        prob = sb("prob", [P, H, K])
        probT = sb("probT", [P, H, P])
        osb = sb("osb", [P, D])
        oT = sb("oT", [P, KD, P])
        x1f = sb("x1f", [P, 2, D])
        h2 = sb("h2", [P, 2, D])
        h2T = sb("h2T", [P, KD, P])
        act_up = sb("act_up", [P, F])
        gT = sb("gT", [P, F // P, P])
        row = sb("row", [P, 2, D])
        wts = act_up[0:B].rearrange("p (e t) -> p e t", e=2)
        sel16 = gT[0:B]
        ang = act_up[:, 0:4 * B * HD // 2].rearrange("p (e b f) -> p e b f", e=4, b=B)
        sq = sb("sq", [P, D], BF16)
        sq2 = sb("sq2", [P, D], BF16)
        st = sb("st", [P, 6])
        v1 = sb("v1", [P, 2, 24])
        mx = sb("mx", [P, 3, H])

        loaded = sem("loaded")
        wts_in = sem("wts_in")
        folded = sem("folded")
        topk = sem("topk")
        cols_full = sem("cols_full")
        cols_done = sem("cols_done")
        idxbc_full = sem("idxbc_full")
        pos_in = sem("pos_in")
        angle = sem("angle")
        full = {b: sem(f"full_{b}") for b in banks}
        free = {b: sem(f"free_{b}") for b in banks}
        idx_copied = sem("idx_copied")
        x_in = [sem("xg_even"), sem("xg_odd")]
        m_in = sem("m_in")
        scattered = [sem("scattered_even"), sem("scattered_odd")]
        norm = sem("norm")
        norm_act = sem("norm_act")
        norm2 = sem("norm2")
        norm2_act = sem("norm2_act")
        rope = sem("rope")
        onehot_ready = sem("onehot_ready")
        soft = sem("soft")
        exp_ready = sem("exp_ready")
        o_ready = sem("o_ready")
        row_ready = sem("row_ready")
        based = sem("based")
        gathering = sem("gathering")
        scattering = sem("scattering")

        SETUP_DMAS = 5
        WEIGHT_DMAS = 8

        def steps(eng, body):
            body(0, 0)
            body(1, 1)
            with eng.Fori(2, B - 3, 2) as i:
                body(i, 0)
                body(i + 1, 1)
            body(B - 2, 0)
            body(B - 1, 1)
            body(B, 0)

        def attention(i):
            return not (isinstance(i, int) and i == B)

        def final(i):
            return isinstance(i, int) and i == B - 1

        def mlp(i):
            return not (isinstance(i, int) and i == 0)

        def fill(pe, i, use):
            n = use_number(i, use)
            if not (isinstance(n, int) and n == 0):
                pe.wait_ge(free[BANK_OF[use]], n)

        def filled(eng, i, use):
            eng.wait_ge(full[BANK_OF[use]], use_number(i, use) + 1)
            return BANK_OF[use]

        block = ctx.enter_context(nc.Block())

        @block.sync
        def _(sp):
            sp.dma_start(wts[:, 0, :], w_dram).then_inc(wts_in, 16)
            for dst, src in ((ident[:], ident_c), (sel16[:], sel16_c), (token[:], token_c), (batch[:], batch_c),
                             (inv[:], inv_c)):
                sp.dma_start(dst, src).then_inc(loaded, 16)
            for dst, src in ((w_qkv[:, 0], wq), (w_qkv[:, 1], wk), (w_qkv[:, 2], wv), (g1[:], ln1), (w_o[:], wo),
                             (g2[:], ln2), (w_1[:], w1), (w_2[:], w2)):
                sp.dma_start(dst, src).then_inc(loaded, 16)

        @block.gpsimd
        def _(pool):
            pool.wait_ge(cols_done, 5)
            for b in range(B):
                pool.indirect_dma_start(
                    out=pos_i[:, b:b + 1], out_offset=None, in_=pos,
                    in_offset=bass.IndirectOffsetOnAxis(ap=cols_i[:, 1, b:b + 1], axis=0),
                ).then_inc(pos_in, 16)

            def take_index(a, dst, j):
                nc.gpsimd.tensor_copy(dst, cols_i[:, j, bass.ds(a, 1)]).then_inc(idx_copied, 1)

            def gather_x(a, par):
                if has_batch(a, 2):
                    pool.wait_ge(x_in[par], (a - par) * 8)
                    pool.wait_ge(based, a - 1)
                take_index(a, idx_x[:, par], 0)
                pool.wait_ge(idx_copied, copied_before(a, "x") + 1)
                pool.sem_inc(gathering, 1)
                pool.indirect_dma_start(
                    out=xg[:, par, :], out_offset=None, in_=x1_dram,
                    in_offset=bass.IndirectOffsetOnAxis(ap=idx_x[:, par], axis=0)).then_inc(x_in[par], 16)

            def gather_mask(a, par):
                if has_batch(a, 1):
                    pool.wait_ge(m_in, a * 16)
                    pool.wait_ge(full["t1"], use_number(a - 1, "GT1") + 1)
                take_index(a, idx_m[:, par], 2)
                pool.wait_ge(idx_copied, copied_before(a, "mask") + 1)
                pool.sem_inc(gathering, 1)
                pool.indirect_dma_start(
                    out=rows_m[:], out_offset=None, in_=mask,
                    in_offset=bass.IndirectOffsetOnAxis(ap=idx_m[:, par], axis=0)).then_inc(m_in, 16)

            def scatter(m, pm):
                take_index(m, idx_out[:, pm], 0)
                pool.wait_ge(idx_copied, copied_before(m, "out") + 1)
                pool.wait_ge(row_ready, m + 1)
                pool.sem_inc(scattering, 1)
                pool.indirect_dma_start(
                    out=out, out_offset=bass.IndirectOffsetOnAxis(ap=idx_out[0:KS, pm], axis=0),
                    in_=row[0:KS, pm, :], in_offset=None).then_inc(scattered[pm], 16)
                pool.wait_ge(scattered[pm], (m - pm) * 8 + 16)

            def copied_before(a, which):
                if which == "out":
                    i = a + 1
                    if isinstance(i, int) and i >= B - 1:
                        return 3 * (B - 1) + 1 + i - (B - 1)
                    return 3 * i + 1 + 2
                at = ("x", "mask").index(which)
                if isinstance(a, int) and a <= 1:
                    return 2 * a + at
                return 3 * (a - 1) + 1 + at

            def has_batch(a, least):
                return not isinstance(a, int) or a >= least

            def body(i, par):
                if not (isinstance(i, int) and i >= B - 1):
                    gather_x(i + 1, 1 - par)
                    gather_mask(i + 1, 1 - par)
                if mlp(i):
                    scatter(i - 1, 1 - par)

            gather_x(0, 0)
            gather_mask(0, 0)
            steps(pool, body)

        @block.tensor
        def _(pe):
            pe.wait_ge(loaded, 16 * (SETUP_DMAS + WEIGHT_DMAS))
            pe.wait_ge(topk, TOPK)
            for j in range(4):
                last = pe.transpose(one["t0"][:, j * B:(j + 1) * B], rows_f[:, j, :], ident[0:B, 0:B])
            last = pe.transpose(one["t0"][:, 4 * B:5 * B], top[:], ident[0:B, 0:B])
            last.then_inc(cols_full, 1)
            for b in range(B):
                last = pe.matmul(banks["s"][:, b // 4, (b % 4) * K:(b % 4 + 1) * K], sel16[:, b, :],
                                 rows_f[:, 4, :], start=True, stop=True)
            last.then_inc(idxbc_full, 1)
            def turn(bank, src, n=KD):
                for k in range(n):
                    last = pe.transpose(one[bank][:, k * P:(k + 1) * P], src[:, k * P:(k + 1) * P], ident[:])
                last.then_inc(full[bank], 1)

            def product(bank, xT, w, n):
                for k in range(n):
                    last = pe.matmul(one[bank], xT[:, k, :], w(k), start=(k == 0), stop=(k == n - 1))
                last.then_inc(full[bank], 1)

            def turn_hn(i):
                pe.wait_ge(norm, (i + 1) * NORM + NORM)
                fill(pe, i, "hnT")
                turn("t0", hn)

            def values(i):
                pe.wait_ge(free["t0"], use_number(i, "hnT") + 1)
                fill(pe, i, "v")
                product("t0", hnT, lambda k: w_qkv[:, 2, k, :], KD)

            pe.wait_ge(folded, FOLDED)
            pe.wait_ge(cols_done, 6)
            turn_hn(-1)
            values(-1)

            def body(i, par):
                a, m, pm = i, i - 1, 1 - par
                if attention(i):
                    for j, use in enumerate(("q", "k")):
                        fill(pe, i, use)
                        product(BANK_OF[use], hnT, lambda k, j=j: w_qkv[:, j, k, :], KD)
                if mlp(i):
                    pe.wait_ge(norm2, m * NORM2 + NORM2)
                    fill(pe, i, "h2T")
                    turn("t1", h2[:, pm, :])
                    pe.wait_ge(free["t1"], use_number(i, "h2T") + 1)
                    for j in range(4):
                        fill(pe, i, f"up{j}")
                        product(BANK_OF[f"up{j}"], h2T, lambda k, j=j: w_1[:, k, j * HALF:(j + 1) * HALF], KD)
                if attention(i):
                    pe.wait_ge(m_in, a * 16 + 16)
                    for n in range(2):
                        fill(pe, i, f"GT{n}")
                        turn(BANK_OF[f"GT{n}"], rows_m[:, n * HALF:(n + 1) * HALF])
                    for j, use in enumerate(("qT", "kT")):
                        pe.wait_ge(rope, a * ROPE + 6 * (j + 1))
                        fill(pe, i, use)
                        turn(BANK_OF[use], qk[:, j, :])
                    pe.wait_ge(free["m0"], use_number(i, "qT") + 1)
                    pe.wait_ge(free["m1"], use_number(i, "kT") + 1)
                    fill(pe, i, "scores")
                    for k in range(KD):
                        for j in range(4):
                            last = pe.matmul(banks["s"][:, j, k * K:k * K + KS], qkT[j * HD:(j + 1) * HD, 0, k, :],
                                             qkT[j * HD:(j + 1) * HD, 1, k, 0:KS], start=True, stop=True)
                    last.then_inc(full["s"], 1)
                    for n in range(2):
                        pe.wait_ge(free[BANK_OF[f"GT{n}"]], use_number(i, f"GT{n}") + 1)
                    pe.wait_ge(onehot_ready, a + 1)
                    fill(pe, i, "mask")
                    for t in range(TC):
                        last = pe.matmul(one["m0"][:, 0:K], GT[:, t, :], onehot[:, t, :],
                                         start=(t == 0), stop=(t == TC - 1))
                    last.then_inc(full["m0"], 1)
                if mlp(i):
                    for j in range(4):
                        bank = BANK_OF[f"up{j}"]
                        pe.wait_ge(free[bank], use_number(i, f"up{j}") + 1)
                        fill(pe, i, f"gT{j}")
                        turn(BANK_OF[f"gT{j}"], act_up[:, j * HALF:(j + 1) * HALF])
                    fill(pe, i, "down")
                    for j in range(4):
                        pe.wait_ge(free[BANK_OF[f"gT{j}"]], use_number(i, f"gT{j}") + 1)
                        for k in range(4 * j, 4 * j + 4):
                            last = pe.matmul(one["m1"], gT[:, k, :], w_2[:, k, :], start=(k == 0),
                                             stop=(k == F // P - 1))
                    last.then_inc(full["m1"], 1)
                if attention(i):
                    pe.wait_ge(exp_ready, a + 1)
                    fill(pe, i, "aT")
                    for h in range(H):
                        last = pe.transpose(banks["s"][0:KS, h // 4, (h % 4) * P:(h % 4 + 1) * P], prob[:, h, 0:KS],
                                            ident[:])
                    last.then_inc(full["s"], 1)
                    if not final(i):
                        turn_hn(i)
                    pe.wait_ge(free["s"], use_number(i, "aT") + 1)
                    pe.wait_ge(o_ready, a * 2 + 1)
                    pe.wait_ge(free["t0"], use_number(i - 1, "v") + 1)
                    fill(pe, i, "o")
                    for h in range(H):
                        hd = 4 * (h % 4) + h // 4
                        last = pe.matmul(one["m0"][:, hd * HD:(hd + 1) * HD], probT[0:KS, h, :],
                                         vsb[0:KS, par, hd * HD:(hd + 1) * HD], start=True, stop=True)
                    last.then_inc(full["m0"], 1)
                    if not final(i):
                        values(i)
                    pe.wait_ge(o_ready, a * 2 + 2)
                    fill(pe, i, "oT")
                    turn("t1", osb)
                    pe.wait_ge(free["t1"], use_number(i, "oT") + 1)
                    fill(pe, i, "attn")
                    product("m1", oT, lambda k: w_o[:, k, :], KD)

            steps(pe, body)

        @block.scalar
        def _(act):
            act.wait_ge(loaded, 16 * (SETUP_DMAS + WEIGHT_DMAS))
            for j in range(3):
                for k in range(KD):
                    nc.scalar.activation(w_qkv[:, j, k, :], w_qkv[:, j, k, :], ACT.Copy, scale=g1[:, k:k + 1])\
                        .then_inc(folded, 1)
            for k in range(KD):
                nc.scalar.activation(w_1[:, k, :], w_1[:, k, :], ACT.Copy, scale=g2[:, k:k + 1]).then_inc(folded, 1)

            def copy(i, use, dst, rows=P):
                bank = filled(act, i, use)
                nc.scalar.activation(dst, one[bank][0:rows].rearrange("p (k t) -> p k t", t=P) if dst.ndim == 3
                                     else one[bank][0:rows], ACT.Copy).then_inc(free[bank], 1)

            act.wait_ge(angle, ANGLE)
            nc.scalar.activation(sin[:], ang[:, 0], ACT.Sin).then_inc(angle, 1)
            nc.scalar.activation(cos[:], ang[:, 1], ACT.Sin).then_inc(angle, 1)

            def inverse_root(chain, n, chain_act, na, var, spare, root):
                act.wait_ge(chain, n)
                nc.scalar.activation(spare, var, ACT.Ln).then_inc(chain_act, 1)
                act.wait_ge(chain_act, na + 1)
                nc.scalar.activation(root, spare, ACT.Exp, scale=-0.5).then_inc(chain_act, 1)

            def prepare(a, par):
                v = v1[:, par, :]
                inverse_root(norm, a * NORM + 8, norm_act, a * 5, v[:, 0:1], v[:, 7:8], v[:, 2:3])
                act.wait_ge(norm, a * NORM + 13)
                if not (isinstance(a, int) and a == 0):
                    act.wait_ge(norm_act, a * 5)
                nc.scalar.activation(sq[:], xn[:, par, :], ACT.Square, accum_out=v[:, 8:9]).then_inc(norm_act, 1)
                inverse_root(norm, a * NORM + 14, norm_act, a * 5 + 3, v[:, 9:10], v[:, 10:11], v[:, 11:12])

            nc.scalar.preload_act_table_set("natural_log_exp_and_others")
            prepare(0, 0)

            def copy_ahead(i, par):
                if not (isinstance(i, int) and i == -1):
                    act.wait_ge(full["m1"], use_number(i, "k") + 1)
                copy(i, "hnT", hnT[:])

            def copy_v(i, par):
                if not (isinstance(i, int) and i <= 0):
                    act.wait_ge(full["m0"], use_number(i - 1, "o") + 1)
                copy(i, "v", vsb[:, par, :])

            copy_ahead(-1, 0)
            copy_v(-1, 0)

            def body(i, par):
                a, m, pm = i, i - 1, 1 - par
                if mlp(i):
                    copy(i, "h2T", h2T[:])
                if mlp(i):
                    for j in range(4):
                        bank = filled(act, i, f"up{j}")
                        nc.scalar.activation(act_up[:, j * HALF:(j + 1) * HALF], one[bank],
                                             ACT.Gelu_apprx_tanh).then_inc(free[bank], 1)
                if attention(i):
                    copy(i, "qT", qkT[:, 0])
                    copy(i, "kT", qkT[:, 1])
                if mlp(i):
                    for j in range(4):
                        copy(i, f"gT{j}", gT[:, 4 * j:4 * j + 4, :])
                if attention(i):
                    nc.scalar.preload_act_table_set("natural_log_exp_and_others")
                    act.wait_ge(soft, a * SOFT + 2)
                    nc.scalar.activation(prob[:, :, 0:KS], prob[:, :, 0:KS], ACT.Exp).then_inc(exp_ready, 1)
                    if not final(i):
                        prepare(i + 1, pm)
                    act.wait_ge(full["s"], use_number(i, "aT") + 1)
                    nc.scalar.activation(probT[0:KS, 0:8, :],
                                         banks["s"][0:KS, 0:2, :].rearrange("p j (k t) -> p (j k) t", t=P),
                                         ACT.Copy).then_inc(free["s"], 1)
                    if not final(i):
                        copy_ahead(i, pm)
                        copy_v(i, pm)
                    copy(i, "oT", oT[:])
                    v = v1[:, par, :]
                    act.wait_ge(norm2, a * NORM2 + 1)
                    nc.scalar.activation(sq2[:], x1f[:, par, :], ACT.Square, accum_out=v[:, 16:17])\
                        .then_inc(norm2_act, 1)
                    inverse_root(norm2, a * NORM2 + 2, norm2_act, a * 3 + 1, v[:, 17:18], v[:, 18:19], v[:, 19:20])

            steps(act, body)

        @block.vector
        def _(dve):
            V = nc.vector
            chain = [0]

            def link(ins):
                chain[0] += 1
                ins.then_inc(topk, 1)
                dve.wait_ge(topk, chain[0])

            dve.wait_ge(wts_in, 16)
            for r in range(K // 8):
                now, then = wts[:, r % 2, :], wts[:, 1 - r % 2, :]
                eight = slice(8 * r, 8 * r + 8)
                link(V.max(top[:, eight], now))
                link(V.max_index(topi[:, eight], top[:, eight], now))
                link(V.match_replace(then, top[:, eight], now, LOWEST))
            link(V.tensor_copy(rows_f[:, 4, :], topi[:]))
            dve.wait_ge(loaded, 16 * (SETUP_DMAS + WEIGHT_DMAS))
            for j, scale in enumerate((1.0, 1.0, 2.0)):
                link(V.tensor_scalar(rows_f[:, j, :], rows_f[:, 4, :], scale, batch[:, j:j + 1], ALU.mult, ALU.add))
            link(V.tensor_scalar(rows_f[:, 3, :], top[:], top[:, K - 1:K], None, ALU.is_le))
            assert chain[0] == TOPK
            dve.wait_ge(cols_full, 1)
            t0 = one["t0"]
            for j in range(3):
                V.tensor_copy(cols_i[:, j, :], t0[:, j * B:(j + 1) * B]).then_inc(cols_done, 1)
            V.tensor_copy(notsel[:], t0[:, 3 * B:4 * B]).then_inc(cols_done, 1)
            V.tensor_copy(wsel[:], t0[:, 4 * B:5 * B]).then_inc(cols_done, 1)
            dve.wait_ge(idxbc_full, 1)
            V.tensor_copy(idx_bc[:].rearrange("p b k -> p (b k)"),
                          banks["s"][:].rearrange("p j k -> p (j k)")).then_inc(cols_done, 1)
            n = [0]

            def angle_step(ins):
                n[0] += 1
                ins.then_inc(angle, 1)
                dve.wait_ge(angle, n[0])

            dve.wait_ge(pos_in, 16 * B)
            angle_step(V.tensor_copy(pos_f[:], pos_i[:]))
            f3 = [P, B, HD // 2]
            angle_step(V.tensor_tensor(ang[:, 2], pos_f[:].unsqueeze(2).to_broadcast(f3),
                                       inv[:].unsqueeze(1).to_broadcast(f3), ALU.mult))
            angle_step(V.tensor_scalar(ang[:, 3], ang[:, 2], float(1 / (2 * np.pi)), MAGIC, ALU.mult, ALU.add))
            angle_step(V.tensor_scalar(ang[:, 1], ang[:, 3], MAGIC, None, ALU.subtract))
            angle_step(V.scalar_tensor_tensor(ang[:, 3], ang[:, 1], -TWO_PI_HI, ang[:, 2], ALU.mult, ALU.add))
            angle_step(V.scalar_tensor_tensor(ang[:, 2], ang[:, 1], -TWO_PI_LO, ang[:, 3], ALU.mult, ALU.add))
            angle_step(V.tensor_scalar(ang[:, 0], ang[:, 2], 3.1415925, -3.1415925, ALU.min, ALU.max))
            angle_step(V.scalar_tensor_tensor(ang[:, 3], ang[:, 0], -1.0, ang[:, 0], ALU.mult, ALU.max))
            angle_step(V.tensor_scalar(ang[:, 1], ang[:, 3], -1.0, float(np.pi / 2), ALU.mult, ALU.add))
            assert n[0] == ANGLE

            def newton(sem_, at, r0, v, t, u, r):
                V.tensor_tensor(t, r0, r0, ALU.mult).then_inc(sem_, 1)
                dve.wait_ge(sem_, at + 1)
                V.tensor_tensor(u, t, v, ALU.mult).then_inc(sem_, 1)
                dve.wait_ge(sem_, at + 2)
                V.tensor_scalar(t, u, -0.5, 1.5, ALU.mult, ALU.add).then_inc(sem_, 1)
                dve.wait_ge(sem_, at + 3)
                V.tensor_tensor(r, r0, t, ALU.mult).then_inc(sem_, 1)
                dve.wait_ge(sem_, at + 4)

            def prepare(a, par):
                v = v1[:, par, :]
                at = a * NORM
                c = lambda j: v[:, j:j + 1]
                dve.wait_ge(x_in[par], (a - par) * 8 + 16)
                if not (isinstance(a, int) and a == 0):
                    dve.wait_ge(full["t0"], use_number(a - 2, "hnT") + 1)
                if not (isinstance(a, int) and a <= 1):
                    dve.wait_ge(norm2, (a - 2) * NORM2 + 1)
                V.bn_stats(st[:], xg[:, par, :]).then_inc(norm, 1)
                dve.wait_ge(norm, at + 1)
                V.tensor_tensor(c(3), st[:, 1:2], st[:, 4:5], ALU.add).then_inc(norm, 1)
                V.tensor_tensor(c(4), st[:, 1:2], st[:, 4:5], ALU.subtract).then_inc(norm, 1)
                V.tensor_tensor(c(5), st[:, 2:3], st[:, 5:6], ALU.add).then_inc(norm, 1)
                dve.wait_ge(norm, at + 4)
                V.tensor_scalar(c(1), c(3), 0.5, None, ALU.mult).then_inc(norm, 1)
                V.tensor_tensor(c(6), c(4), c(4), ALU.mult).then_inc(norm, 1)
                V.tensor_scalar(c(5), c(5), 1.0 / D, EPS, ALU.mult, ALU.add).then_inc(norm, 1)
                dve.wait_ge(norm, at + 7)
                V.scalar_tensor_tensor(c(0), c(6), 0.25, c(5), ALU.mult, ALU.add).then_inc(norm, 1)
                dve.wait_ge(norm_act, a * 5 + 2)
                newton(norm, at + 8, c(2), c(0), c(3), c(4), c(6))
                V.tensor_scalar(xn[:, par, :], xg[:, par, :], c(1), c(6), ALU.subtract, ALU.mult).then_inc(norm, 1)
                dve.wait_ge(norm_act, a * 5 + 3)
                V.tensor_scalar(c(9), c(8), 1.0 / D, 1e-6, ALU.mult, ALU.add).then_inc(norm, 1)
                dve.wait_ge(norm_act, a * 5 + 5)
                dve.wait_ge(norm, at + 14)
                newton(norm, at + 14, c(11), c(9), c(12), c(13), c(14))
                V.tensor_scalar(hn[:], xn[:, par, :], c(14), None, ALU.mult).then_inc(norm, 1)

            def make_base(a, par):
                if not (isinstance(a, int) and a <= 1):
                    dve.wait_ge(row_ready, a - 1)
                V.scalar_tensor_tensor(base[:, par, :], xn[:, par, :], notsel[:, bass.ds(a, 1)], xg[:, par, :],
                                       ALU.mult, ALU.add).then_inc(based, 1)

            dve.wait_ge(cols_done, 6)
            prepare(0, 0)
            make_base(0, 0)
            dve.wait_ge(angle, ANGLE + 2)

            def one_hot(a):
                if not (isinstance(a, int) and a == 0):
                    dve.wait_ge(full["m0"], use_number(a - 1, "mask") + 1)
                V.tensor_tensor(onehot[:], idx_bc[:, bass.ds(a, 1), :].to_broadcast([P, TC, K]),
                                token[:].unsqueeze(2).to_broadcast([P, TC, K]), ALU.is_equal)\
                 .then_inc(onehot_ready, 1)

            def rotate(i, j):
                bank = filled(dve, i, ("q", "k")[j])
                at = i * ROPE + 6 * j
                x = one[bank].rearrange("p (h e f) -> p h e f", h=H, e=2)
                r = rot[:].rearrange("p (h e f) -> p h e f", h=H, e=2)
                y = qk[:, j, :].rearrange("p (h e f) -> p h e f", h=H, e=2)
                s3 = [P, H, HD // 2]
                c = cos[:, bass.ds(i, 1), :].to_broadcast(s3)
                s = sin[:, bass.ds(i, 1), :].to_broadcast(s3)
                if not (isinstance(i, int) and i == 0):
                    dve.wait_ge(full[("m0", "m1")[j]], use_number(i - 1, ("qT", "kT")[j]) + 1)
                if not (isinstance(i, int) and i == 0 and j == 0):
                    dve.wait_ge(rope, at)
                V.tensor_tensor(y[:, :, 0, :], x[:, :, 0, :], c, ALU.mult).then_inc(rope, 1)
                V.tensor_tensor(r[:, :, 0, :], x[:, :, 1, :], s, ALU.mult).then_inc(rope, 1)
                V.tensor_tensor(y[:, :, 1, :], x[:, :, 1, :], c, ALU.mult).then_inc(rope, 1)
                V.tensor_tensor(r[:, :, 1, :], x[:, :, 0, :], s, ALU.mult).then_inc(rope, 1)
                dve.wait_ge(rope, at + 4)
                V.tensor_tensor(y[:, :, 0, :], y[:, :, 0, :], r[:, :, 0, :], ALU.subtract).then_inc(rope, 1)
                V.tensor_tensor(y[:, :, 1, :], y[:, :, 1, :], r[:, :, 1, :], ALU.add).then_inc(rope, 1)

            def body(i, par):
                a, m, pm = i, i - 1, 1 - par
                if attention(i):
                    for j, use in enumerate(("q", "k")):
                        rotate(i, j)
                        dve.wait_ge(rope, i * ROPE + 6 * j + 4)
                        dve.sem_inc(free[BANK_OF[use]], 1)
                    one_hot(a)
                    for n in range(2):
                        bank = filled(dve, i, f"GT{n}")
                        V.tensor_scalar(GT[:, 4 * n:4 * n + 4, :], one[bank].rearrange("p (k t) -> p k t", t=P),
                                        LOWEST, None, ALU.max).then_inc(free[bank], 1)
                    bank = filled(dve, i, "mask")
                    if not (isinstance(i, int) and i == 0):
                        dve.wait_ge(soft, a * SOFT)
                    V.tensor_copy(msel[:], one[bank][:, 0:K]).then_inc(free[bank], 1)
                    filled(dve, i, "scores")
                    dve.wait_ge(free[bank], use_number(i, "mask") + 1)
                    if not (isinstance(i, int) and i == 0):
                        dve.wait_ge(full["s"], use_number(i - 1, "aT") + 1)
                    at = a * SOFT
                    p3 = prob[:, :, 0:KS]
                    s3 = banks["s"][:].rearrange("p j (k t) -> p (j k) t", t=K)[:, :, 0:KS]
                    V.scalar_tensor_tensor(p3, s3, float(1 / np.sqrt(np.float32(HD))),
                                           msel[:, 0:KS].unsqueeze(1).to_broadcast([P, H, KS]), ALU.mult, ALU.add)\
                     .then_inc(free["s"], 1)
                    dve.wait_ge(free["s"], use_number(i, "scores") + 1)
                    V.tensor_reduce(mx[:, 0, :], p3, AX.X, ALU.max).then_inc(soft, 1)
                    dve.wait_ge(soft, at + 1)
                    V.tensor_tensor(p3, p3, mx[:, 0, :].unsqueeze(2).to_broadcast([P, H, KS]), ALU.subtract)\
                     .then_inc(soft, 1)
                    if not final(i):
                        prepare(i + 1, pm)
                if mlp(i):
                    bank = filled(dve, i, "down")
                    V.tensor_tensor(x1f[:, pm, :], one[bank], x1f[:, pm, :], ALU.add).then_inc(free[bank], 1)
                    dve.wait_ge(free[bank], use_number(i, "down") + 1)
                    if not (isinstance(i, int) and i < 3):
                        dve.wait_ge(scattered[pm], (m - pm) * 8)
                    dve.wait_ge(based, m + 1)
                    V.scalar_tensor_tensor(row[:, pm, :], x1f[:, pm, :], wsel[:, bass.ds(m, 1)], base[:, pm, :],
                                           ALU.mult, ALU.add).then_inc(row_ready, 1)
                if attention(i):
                    if not final(i):
                        make_base(i + 1, pm)
                    at = a * SOFT
                    dve.wait_ge(full["s"], use_number(i, "aT") + 1)
                    V.tensor_copy(probT[0:KS, 8:16, :],
                                  banks["s"][0:KS, 2:4, :].rearrange("p j (k t) -> p (j k) t", t=P))\
                     .then_inc(o_ready, 1)
                    dve.wait_ge(exp_ready, a + 1)
                    V.tensor_reduce(mx[:, 1, :], prob[:, :, 0:KS], AX.X, ALU.add).then_inc(soft, 1)
                    dve.wait_ge(soft, at + 3)
                    V.reciprocal(mx[:, 2, :], mx[:, 1, :]).then_inc(soft, 1)
                    bank = filled(dve, i, "o")
                    dve.wait_ge(soft, at + 4)
                    V.tensor_tensor(osb[:].rearrange("p (k j e) -> p k j e", k=4, j=4),
                                    one[bank].rearrange("p (k j e) -> p k j e", k=4, j=4),
                                    mx[:, 2, :].rearrange("p (j k) -> p k j", j=4).unsqueeze(3)
                                    .to_broadcast([P, 4, 4, HD]), ALU.mult).then_inc(o_ready, 1)
                    dve.wait_ge(o_ready, a * 2 + 2)
                    dve.sem_inc(free[bank], 1)
                    bank = filled(dve, i, "attn")
                    v = v1[:, par, :]
                    n2 = a * NORM2
                    V.tensor_tensor(x1f[:, par, :], one[bank], xn[:, par, :], ALU.add).then_inc(norm2, 1)
                    dve.wait_ge(norm2, n2 + 1)
                    dve.sem_inc(free[bank], 1)
                    dve.wait_ge(norm2_act, a * 3 + 1)
                    V.tensor_scalar(v[:, 17:18], v[:, 16:17], 1.0 / D, 1e-6, ALU.mult, ALU.add).then_inc(norm2, 1)
                    dve.wait_ge(norm2_act, a * 3 + 3)
                    newton(norm2, n2 + 2, v[:, 19:20], v[:, 17:18], v[:, 20:21], v[:, 21:22], v[:, 22:23])
                    V.tensor_scalar(h2[:, par, :], x1f[:, par, :], v[:, 22:23], None, ALU.mult).then_inc(norm2, 1)

            steps(dve, body)


NORM = 19
NORM2 = 7
ROPE = 12
SOFT = 4
TOPK = 3 * (K // 8) + 5
ANGLE = 9
FOLDED = 3 * KD + KD


def layernorm_scan_and_chosen_tokens(nc, a, out, x1_dram, w_dram, bc_dram):
    with ExitStack() as semaphores:
        scan_phase(nc, semaphores, a["x"], a["A_log"], a["w_xproj"], a["w_dt"], a["dt_b"], a["D_row"],
                   a["router_w"], a["router_b"], a["ident"], a["state_sum"], bc_dram, x1_dram, w_dram, out)
        ffn_phase(nc, semaphores, w_dram, x1_dram.rearrange("b l d -> (b l) d"), out.rearrange("b l d -> (b l) d"),
                  a["mask"], a["pos"], a["wq"], a["wk"], a["wv"], a["wo"], a["w1"], a["w2"], a["ln1"], a["ln2"],
                  a["ident"], a["batch_rows"], a["token"], a["batch_first"], a["inv_freq"])


def shape_constants(np):
    m = np.arange(P)
    batch_rows = np.zeros((B, B, P), np.float32)
    batch_rows[np.arange(B), np.arange(B)] = 1
    b = np.arange(B)
    bm = np.minimum(b, BM - 1)
    inv = 1.0 / np.float32(10000.0) ** (np.arange(0, HD, 2, dtype=np.float32) / np.float32(HD))
    return {
        "ident": np.eye(P, dtype=np.float32),
        "state_sum": (m[:, None] % CH == np.arange(CH)[None]).astype(np.float32),
        "batch_rows": batch_rows,
        "token": (m[:, None] + P * np.arange(TC)[None]).astype(np.float32),
        "batch_first": np.stack([b * L, bm * SM, bm * SM * (SM // L)], 1).astype(np.float32),
        "inv_freq": np.broadcast_to(inv.astype(np.float32), (P, HD // 2)),
    }


def kernel(**inputs):
    import numpy as np
    import concourse.bacc as bacc
    from concourse import mybir
    from concourse.bass_utils import run_bass_kernel_spmd

    i = {k: np.asarray(v) for k, v in inputs.items()}

    def rows(w):
        return w.reshape(-1, P, w.shape[1]).transpose(1, 0, 2)

    arrays = {
        "x": i["L0_attn_x"],
        "A_log": i["L0_attn_A_log"].reshape(CHUNKS, CH, GROUPS, NT).transpose(3, 1, 0, 2).reshape(P, TILES),
        "w_xproj": rows(i["L0_attn_x_proj_w"].T),
        "w_dt": i["L0_attn_dt_proj_w"].T,
        "dt_b": i["L0_attn_dt_proj_b"].reshape(KD, P).T,
        "D_row": np.broadcast_to(i["L0_attn_D"], (P, D)),
        "router_w": np.broadcast_to(i["L0_ffn_router_w"].reshape(1, D), (P, D)),
        "router_b": np.broadcast_to(i["L0_ffn_router_b"].reshape(1, 1), (P, 1)),
        "mask": i["L0_ffn_attention_mask"].reshape(-1, L),
        "pos": i["L0_ffn_position_ids"].reshape(-1, 1),
        "ln1": i["L0_ffn_ln1"].reshape(KD, P).T,
        "ln2": i["L0_ffn_ln2"].reshape(KD, P).T,
    }
    for name in ("wq", "wk", "wv", "wo", "w1", "w2"):
        arrays[name] = rows(i[f"L0_ffn_{name}"])
    arrays.update(shape_constants(np))
    arrays = {k: np.ascontiguousarray(v) for k, v in arrays.items()}

    nc = bacc.Bacc("TRN2", target_bir_lowering=False, num_devices=1)
    a = {k: nc.dram_tensor(f"in_{k}", v.shape, mybir.dt.from_np(v.dtype), kind="ExternalInput").ap()
         for k, v in arrays.items()}
    out = nc.dram_tensor("out_rows", (B, L, D), mybir.dt.float32, kind="ExternalOutput").ap()
    x1 = nc.dram_tensor("x1_rows", (B, L, D), mybir.dt.float32, kind="Internal").ap()
    w = nc.dram_tensor("router_weights", (B, L), mybir.dt.float32, kind="Internal").ap()
    bc = nc.dram_tensor("b_and_c", (2 * N, L), mybir.dt.float32, kind="Internal").ap()
    layernorm_scan_and_chosen_tokens(nc, a, out, x1, w, bc)
    r = run_bass_kernel_spmd(nc, [{f"in_{k}": v for k, v in arrays.items()}], core_ids=[0])
    return r.results[0]["out_rows"]
```

```python
from contextlib import ExitStack

import numpy as np

import concourse.bass as bass
from concourse import mybir

ALU = mybir.AluOpType
ACT = mybir.ActivationFunctionType
F32 = mybir.dt.float32
BF16 = mybir.dt.bfloat16
I32 = mybir.dt.int32
U32 = mybir.dt.uint32
AX = mybir.AxisListType

P = 128
EPS = 1e-5

B, L, D, N, R = 16, 1024, 512, 16, 64
CH = 32
NT = P // CH
CHUNKS = D // CH
GROUPS = N // NT
TILES = CHUNKS * GROUPS
TC = L // P
KD = D // P
HALF = 512
KPE = 2
SKIP_FROM = KPE * P

SOFTPLUS_AFTER = 1
YADD = 2
TURN = ((7, 1), (7, 2), (8, 0), (8, 1), (8, 2), (9, 0), (9, 1), (9, 2))
COPY_XHAT = ((7, 3), (8, 1), (8, 2), (8, 3), (9, 1), (9, 2), (9, 3), (10, 1))
PROJECT = (((10, 0), (10, 0), (10, 1), (10, 1)), ((10, 3), (11, 0), (11, 0), (11, 1)))
COPY_PROJ = ((10, 3), (11, 3))
SUMS1 = {(5, 1): range(0, 2), (5, 2): range(2, 4), (5, 3): range(4, 8), (6, 0): range(8, 10), (6, 1): range(10, 12), (6, 2): range(12, 14), (6, 3): range(14, 17)}
SUMS2 = {(0, 1): range(0, 2), (0, 2): range(2, 4), (0, 3): range(4, 8), (1, 0): range(8, 10), (1, 1): range(10, 12), (1, 2): range(12, 14), (1, 3): range(14, 17)}
MAKE_OUT = ((3, 1), (3, 1), (3, 2), (3, 2), (3, 3), (3, 3), (3, 3), (3, 3))
NORM1 = 7
Z = (12, 13, 14)
SKIP = (10, 12, 13, 13, 14, 14, 15, 15)
Z3 = 2
SOFTPLUS_NEXT = {13: ((0, 0), (0, 1)), 14: ((0, 2), (1, 0)), 15: ((1, 1),)}
SOFTPLUS_NOW = {0: ((2, 0),), 2: ((2, 1),), 4: ((3, 0),), 6: ((3, 1),)}
POOL_DX = {1: (0, 0), 2: (2, 0), 3: (6, 1)}
POOL_INPUT = (3,)
STORE_LOAD = (3, 4)

USES = [("xhat", t) for t in range(TC)] + [("proj", 0), ("proj", 1)] + [("z", k, h) for k in range(KD) for h in range(2)]
USE = {key: u for u, key in enumerate(USES)}
NUSE = len(USES)
LN1 = 5
LN2 = 6
LN_ACT = 20
ZSTEPS = 3
ZACT = 5


def scan_phase(nc, semaphores, x, A_log, w_xproj, w_dt, dt_b, D_row, D_col, router_w, router_b, ident_c, nsum_c, bc_dram,
               x1_dram, w_dram, out, nb_run=B):
    with ExitStack() as ctx:
        def sb(name, shape, dt=F32):
            return ctx.enter_context(nc.sbuf_tensor(name, shape, dt))

        def ps(name, shape, dt=F32):
            return ctx.enter_context(nc.psum_tensor(name, shape, dt))

        def sem(name):
            return semaphores.enter_context(nc.semaphore(name))

        decay = ps("decay", [P, 2, L])
        dx = ps("dx", [P, L])
        ps_y = ps("ps_y", [P, HALF])
        aux = ps("aux", [P, HALF])

        ident = sb("ident", [P, P])
        nsum = sb("nsum", [P, CH])
        xproj = sb("xproj", [P, KD, R + 2 * N])
        dtw = sb("dtw", [R, D])
        dtb = sb("dtb", [P, KD])
        drow = sb("drow", [P, D - SKIP_FROM])
        dcol = sb("dcol", [P, KD])
        dskip = sb("dskip", [P, KPE, P])
        a_neg = sb("a_neg", [P, CHUNKS * GROUPS])
        rw = sb("rw", [P, D])
        rb = sb("rb", [P, 1])

        xr = sb("xr", [P, 2, TC, D])
        xh = sb("xh", [P, 2, D])
        xs = sb("xs", [P, 2, D - SKIP_FROM])
        xhT = sb("xhT", [P, KD, L])
        xpT = sb("xpT", [P, L])
        delT = sb("delT", [P, KD, L])
        dxT = sb("dxT", [P, KD, L])
        te = sb("te", [P, L])
        tu = sb("tu", [P, L])
        bmat = sb("bmat", [P, GROUPS, L])
        cmat = sb("cmat", [P, GROUPS, L])
        junk = sb("junk", [P, D], BF16)
        wcol = sb("wcol", [P, B * TC])
        wrow = xs[:, 0, 0:P]
        eps = sb("eps", [P, 1])
        squares = sb("squares", [P, 2, 2, D], BF16)
        r1 = sb("r1", [P, 9, TC])
        r2 = sb("r2", [P, 9, TC])
        m1 = sb("m1", [P, 3, TC])
        m2 = sb("m2", [P, 3, TC])

        inp = sb("inp", [P, GROUPS, L])
        hid = sb("hid", [P, GROUPS, L])
        ch = sb("ch", [P, 2, L])
        ysb = sb("ysb", [P, 2 * P])
        delr = sb("delr", [P, 2, L])
        dxr = sb("dxr", [P, 2, L])

        consts_in = sem("consts_in")
        x_in = [[sem(f"x_in_{p}{h}") for h in "ab"] for p in ("even", "odd")]
        x1_out = sem("x1_out")
        out_done = [sem("out_done_a"), sem("out_done_b")]
        w_out = sem("w_out")
        bc_out = sem("bc_out")
        b_in = [sem(f"b_in_{g}") for g in range(GROUPS)]
        c_in = [sem(f"c_in_{g}") for g in range(GROUPS)]
        del_rep = [sem("del_rep_even"), sem("del_rep_odd")]
        dx_rep = [sem("dx_rep_even"), sem("dx_rep_odd")]
        repeating = sem("repeating")
        a_exp = sem("a_exp")
        a_ready = sem("a_ready")
        dx_ready = sem("dx_ready")
        decay_ready = sem("decay_ready")
        inp_ready = sem("inp_ready")
        hid_ready = sem("hid_ready")
        ch_ready = sem("ch_ready")
        ch_summed = sem("ch_summed")
        ysb_ready = sem("ysb_ready")
        yt_ready = sem("yt_ready")
        y_added = sem("y_added")
        aux_full = sem("aux_full")
        aux_emptied = sem("aux_emptied")
        z_act = sem("z_act")
        z_dve = sem("z_dve")
        ln1 = sem("ln1")
        ln1_act = sem("ln1_act")
        ln2 = sem("ln2")
        ln2_act = sem("ln2_act")
        xh_ready = sem("xh_ready")
        eps_ready = sem("eps_ready")
        xs_ready = sem("xs_ready")
        dx_made = [sem(f"dx_made_{k}") for k in range(KD)]
        pool_input = sem("pool_input")
        skip_step = sem("skip_step")
        dskip_ready = sem("dskip_ready")
        router_sum = sem("router_sum")
        out_made = sem("out_made")
        wt_ready = sem("wt_ready")
        wrow_ready = sem("wrow_ready")
        NCONST = 10

        def tile(b, c, g):
            return b * TILES + c * GROUPS + g

        def inputs(b, c, g):
            pools = sum((p + 1, GROUPS - 1) < (c, g) for p in POOL_INPUT)
            return b * (TILES - len(POOL_INPUT)) + c * GROUPS + g - pools

        def has(b, least):
            return not isinstance(b, int) or b >= least

        def batches(eng, body):
            body(0, 0)
            if nb_run > 2:
                with eng.Fori(1, nb_run - 2, 2) as i:
                    body(i, 1)
                    body(i + 1, 0)
            body(nb_run - 1, 1)

        def is_last(b):
            return isinstance(b, int) and b == nb_run - 1

        block = ctx.enter_context(nc.Block())

        @block.sync
        def _(sp):
            HT = TC // 2

            def load_x(b, par, h):
                if has(b, 2):
                    sp.wait_ge(out_done[h], b * 16 - 16)
                sp.dma_start(xr[:, par, h * HT:(h + 1) * HT],
                             x[b].rearrange("(t p) d -> p t d", p=P)[:, h * HT:(h + 1) * HT])\
                    .then_inc(x_in[par][h], 16)

            def store_x1(b, par):
                sp.wait_ge(y_added, b * CHUNKS + CHUNKS)
                sp.dma_start(x1_dram[b].rearrange("(t p) d -> p t d", p=P), xr[:, par]).then_inc(x1_out, 16)

            def store_out(b, par, h):
                sp.wait_ge(out_made, b * TC + (h + 1) * HT)
                sp.dma_start(out[b].rearrange("(t p) d -> p t d", p=P)[:, h * HT:(h + 1) * HT],
                             xr[:, par, h * HT:(h + 1) * HT]).then_inc(out_done[h], 16)

            def repeat(b, c):
                k, r = c // NT, CH * (c % NT)
                if r == 0:
                    sp.wait_ge(dx_made[k], b + 1)
                    sp.sem_inc(repeating, 1)
                if has(b, 1) or c >= 2:
                    sp.wait_ge(dx_ready, b * CHUNKS + c - 1)
                    if c - 3 in POOL_INPUT:
                        sp.sem_inc(repeating, 1)
                        sp.wait_ge(pool_input, b * len(POOL_INPUT) + POOL_INPUT.index(c - 3) + 1)
                for n in range(NT):
                    sp.dma_start(dxr[n * CH:(n + 1) * CH, c % 2], dxT[r:r + CH, k]).then_inc(dx_rep[c % 2], 16)
                if has(b, 1) or c >= 2:
                    sp.wait_ge(decay_ready, tile(b, c - 1, 0))
                for n in range(NT):
                    sp.dma_start(delr[n * CH:(n + 1) * CH, c % 2], delT[r:r + CH, k]).then_inc(del_rep[c % 2], 16)

            def store_bc(b):
                sp.wait_ge(aux_emptied, b * NUSE + TC + 2)
                if has(b, 1):
                    for s in b_in + c_in:
                        sp.wait_ge(s, b * 16)
                sp.dma_start(bc_dram, xpT[R:R + 2 * N]).then_inc(bc_out, 16)

            def spread(b, g, which):
                if g == 0 and which == 0:
                    sp.wait_ge(bc_out, b * 16 + 16)
                    sp.sem_inc(repeating, 1)
                if has(b, 1):
                    if which == 0:
                        sp.wait_ge(inp_ready, inputs(b - 1, CHUNKS - 1, g) + 1)
                    else:
                        sp.wait_ge(ch_ready, tile(b - 1, CHUNKS - 1, g) + 1)
                row = which * N + g * NT
                sp.dma_start((bmat, cmat)[which][:, g],
                             bc_dram[row:row + NT].unsqueeze(1).to_broadcast([NT, CH, L]))\
                    .then_inc((b_in, c_in)[which][g], 16)

            for h in range(2):
                load_x(0, 0, h)
            for dst, src in ((ident[:], ident_c), (nsum[:], nsum_c), (xproj[:], w_xproj), (dtw[:], w_dt),
                             (dtb[:], dt_b), (drow[:], D_row[:, SKIP_FROM:D]), (dcol[:], D_col), (a_neg[:], A_log), (rw[:], router_w),
                             (rb[:], router_b)):
                sp.dma_start(dst, src).then_inc(consts_in, 16)
            store_bc(0)
            for g in range(GROUPS):
                spread(0, g, 0)
            for c in range(2):
                repeat(0, c)
            for g in range(GROUPS):
                spread(0, g, 1)

            def body(b, par):
                final = is_last(b)
                for c in range(CHUNKS):
                    if c < CHUNKS - 2:
                        repeat(b, c + 2)
                    elif not final:
                        repeat(b + 1, c + 2 - CHUNKS)
                    if has(b, 1):
                        if c == 0:
                            store_x1(b - 1, 1 - par)
                        if c in STORE_LOAD:
                            store_out(b - 1, 1 - par, STORE_LOAD.index(c))
                    if final:
                        continue
                    if c in STORE_LOAD:
                        load_x(b + 1, 1 - par, STORE_LOAD.index(c))
                    if c == COPY_PROJ[1][0] + 1:
                        store_bc(b + 1)
                    if c in (14, 15):
                        for g in range(GROUPS):
                            spread(b + 1, g, c - 14)

            batches(sp, body)
            store_x1(nb_run - 1, 1)
            for h in range(2):
                store_out(nb_run - 1, 1, h)
            sp.wait_ge(wrow_ready, 1)
            sp.dma_start(w_dram.rearrange("b (t p) -> (b t) p", p=P)[0:nb_run * TC], wrow[0:nb_run * TC])\
                .then_inc(w_out, 16)
            sp.wait_ge(w_out, 16)
            sp.wait_ge(bc_out, 16 * nb_run)
            sp.wait_ge(x1_out, 16 * nb_run)
            for h in range(2):
                sp.wait_ge(out_done[h], 16 * nb_run)

        @block.tensor
        def _(pe):
            def aux_free(b, key):
                u = USE[key]
                if has(b, 1) or u > 0:
                    pe.wait_ge(aux_emptied, b * NUSE + u)

            def turn_xhat(b, t):
                aux_free(b, ("xhat", t))
                pe.wait_ge(xh_ready, b * TC + t + 1)
                for k in range(KD):
                    last = pe.transpose(aux[:, k * P:(k + 1) * P], xh[:, t % 2, k * P:(k + 1) * P], ident[:])
                last.then_inc(aux_full, 1)

            def project(b, h, ks=range(KD)):
                if 0 in ks:
                    aux_free(b, ("proj", h))
                for k in ks:
                    last = pe.matmul(aux[0:R + 2 * N, :], xproj[:, k, :], xhT[:, k, h * HALF:(h + 1) * HALF],
                                     start=(k == 0), stop=(k == KD - 1))
                if KD - 1 in ks:
                    last.then_inc(aux_full, 1)

            def step_size(b, k, h):
                aux_free(b, ("z", k, h))
                pe.matmul(aux[:], dtw[:, k * P:(k + 1) * P], xpT[0:R, h * HALF:(h + 1) * HALF],
                          start=True, stop=True).then_inc(aux_full, 1)

            def sum_states(b, c, g):
                if g == 0 and (has(b, 1) or c > 0):
                    pe.wait_ge(y_added, b * CHUNKS + c)
                k = c // NT
                if g == 0 and k < KPE:
                    for q in range(4):
                        pe.matmul(ps_y[q * CH:(q + 1) * CH, 0:2 * P],
                                  dskip[:, k, c % NT * CH:(c % NT + 1) * CH],
                                  xhT[:, k, q * 2 * P:(q + 1) * 2 * P], start=True, stop=False)
                pe.wait_ge(ch_ready, tile(b, c, g) + 1)
                for q in range(4):
                    last = pe.matmul(ps_y[q * CH:(q + 1) * CH, 0:2 * P], nsum[:],
                                     ch[:, g % 2, q * 2 * P:(q + 1) * 2 * P],
                                     start=(g == 0 and k >= KPE), stop=(g == GROUPS - 1))
                last.then_inc(ch_summed, 1)

            def turn_y(b, c):
                pe.wait_ge(ysb_ready, b * CHUNKS + c + 1)
                for t in range(2):
                    last = pe.transpose(ps_y[:, (2 + t) * P:(3 + t) * P], ysb[:, t * P:(t + 1) * P], ident[:])
                last.then_inc(yt_ready, 1)

            pe.wait_ge(consts_in, 16 * NCONST)
            for t in range(TC):
                turn_xhat(0, t)
            for h in range(2):
                project(0, h)
            for k in range(3):
                for h in range(2):
                    step_size(0, k, h)
            pe.wait_ge(dskip_ready, KPE)

            def body(b, par):
                final = is_last(b)
                for c in range(CHUNKS):
                    if c > 0:
                        turn_y(b, c - 1)
                    elif has(b, 1):
                        turn_y(b - 1, CHUNKS - 1)
                    for g in range(GROUPS):
                        sum_states(b, c, g)
                        for h, at in ((0, (-1, 3)), (1, (0, 0))):
                            if (c, g) == (Z3 + at[0], at[1]):
                                step_size(b, 3, h)
                            for k in range(3):
                                if (c, g) == (Z[k] + at[0], at[1]) and not final:
                                    step_size(b + 1, k, h)
                        if final:
                            continue
                        for t in range(TC):
                            if TURN[t] == (c, g):
                                turn_xhat(b + 1, t)
                        for h in range(2):
                            for k in range(KD):
                                if PROJECT[h][k] == (c, g):
                                    project(b + 1, h, (k,))

            batches(pe, body)
            turn_y(nb_run - 1, CHUNKS - 1)
            pe.wait_ge(router_sum, 10 * nb_run)
            pe.wait_ge(aux_emptied, nb_run * NUSE)
            pe.transpose(aux[0:nb_run * TC, 0:P], wcol[:, 0:nb_run * TC], ident[:]).then_inc(wt_ready, 1)

        @block.scalar
        def _(act):
            def aux_filled(b, key):
                act.wait_ge(aux_full, b * NUSE + USE[key] + 1)

            def normalise(b, par, t):
                if t == 0:
                    act.wait_ge(ln1, b * LN1 + LN1)
                if t >= 2:
                    act.wait_ge(aux_full, b * NUSE + t - 1)
                elif has(b, 1):
                    act.wait_ge(aux_full, b * NUSE - NUSE + TC - 1 + t)
                nc.scalar.activation(xh[:, t % 2, :], xr[:, par, t, :], ACT.Identity, scale=r1[:, 4, t:t + 1],
                                     bias=r1[:, 6, t:t + 1]).then_inc(xh_ready, 1)

            def normalise_again(b, par, t):
                if t >= 2:
                    act.wait_ge(skip_step, b * 2 * TC + 2 * (t - 1))
                elif has(b, 1):
                    act.wait_ge(skip_step, b * 2 * TC - 2 * TC + 2 * (TC - 1 + t))
                nc.scalar.activation(xs[:, t % 2, :], xr[:, par, t, SKIP_FROM:D], ACT.Identity,
                                     scale=r1[:, 4, t:t + 1], bias=r1[:, 6, t:t + 1]).then_inc(xs_ready, 1)

            def copy_xhat(b, t):
                aux_filled(b, ("xhat", t))
                if t == 0 and has(b, 1):
                    for k in range(KD):
                        act.wait_ge(dx_made[k], b)
                nc.scalar.activation(xhT[:, :, t * P:(t + 1) * P], aux[:].rearrange("p (k t) -> p k t", k=KD),
                                     ACT.Copy).then_inc(aux_emptied, 1)

            def copy_proj(b, h):
                aux_filled(b, ("proj", h))
                if has(b, 1) and h == 0:
                    act.wait_ge(bc_out, b * 16)
                nc.scalar.activation(xpT[0:R + 2 * N, h * HALF:(h + 1) * HALF], aux[0:R + 2 * N],
                                     ACT.Copy).then_inc(aux_emptied, 1)

            def z_half(b, k, h):
                if h == 0:
                    if has(b, 1) or k > 0:
                        act.wait_ge(z_dve, b * KD * ZSTEPS + ZSTEPS * (k - 1) + 2)
                        act.wait_ge(z_act, b * KD * ZACT + k * ZACT)
                    if has(b, 1):
                        for s in dx_rep + del_rep:
                            act.wait_ge(s, (b * (CHUNKS // 2) - CHUNKS // 2 + 2 * k + 2) * 16 * NT)
                half = slice(h * HALF, (h + 1) * HALF)
                aux_filled(b, ("z", k, h))
                nc.scalar.activation(te[:, half], aux[:], ACT.Abs, bias=dtb[:, k:k + 1]).then_inc(z_act, 1)
                nc.scalar.activation(dxT[:, k, half], aux[:], ACT.Relu, bias=dtb[:, k:k + 1])\
                    .then_inc(aux_emptied, 1)

            def exp_log(b, k):
                n = b * KD * ZACT + k * ZACT
                act.wait_ge(z_act, n + 2)
                nc.scalar.activation(te[:], te[:], ACT.Exp, scale=-1.0).then_inc(z_act, 1)
                act.wait_ge(z_act, n + 3)
                nc.scalar.activation(tu[:], te[:], ACT.Identity, bias=1.0).then_inc(z_act, 1)
                nc.scalar.activation(delT[:, k, :], te[:], ACT.Ln, bias=1.0).then_inc(z_act, 1)

            def sums(b, par, steps, norm, m, chain_act):
                n = b * LN_ACT
                for i in steps:
                    if i in (8, 9):
                        act.wait_ge(chain_act, n + i)
                    elif has(b, 1) or i >= 2:
                        act.wait_ge(chain_act, n + max(i - 1, 0))
                    if i < 8:
                        nc.scalar.activation(squares[:, norm, i % 2], xr[:, par, i, :], ACT.Identity,
                                             accum_out=m[:, 0, i:i + 1]).then_inc(chain_act, 1)
                    elif i == 8:
                        nc.scalar.activation(m[:, 1, :], m[:, 0, :], ACT.Copy, scale=-1.0 / D).then_inc(chain_act, 1)
                    else:
                        t = i - 9
                        nc.scalar.activation(squares[:, norm, i % 2], xr[:, par, t, :], ACT.Square,
                                             bias=m[:, 1, t:t + 1], accum_out=m[:, 2, t:t + 1])\
                            .then_inc(chain_act, 1)

            def ln1_sums(b, par, steps):
                if 0 in steps:
                    for h in range(2):
                        act.wait_ge(x_in[par][h], (b - par) * 8 + 16)
                    if has(b, 1):
                        act.wait_ge(ln1, b * LN1)
                        act.wait_ge(skip_step, b * 2 * TC)
                sums(b, par, steps, 0, m1, ln1_act)
                if 16 in steps:
                    rstd(b, ln1_act, r1, m1)

            def ln2_sums(b, par, steps):
                if 0 in steps:
                    act.wait_ge(y_added, b * CHUNKS + CHUNKS)
                    if has(b, 1):
                        act.wait_ge(ln2, b * LN2)
                        act.wait_ge(router_sum, b * 10)
                sums(b, par, steps, 1, m2, ln2_act)
                if 16 in steps:
                    rstd(b, ln2_act, r2, m2)

            def rstd(b, chain_act, r, m):
                n = b * LN_ACT + 17
                act.wait_ge(chain_act, n)
                nc.scalar.activation(r[:, 0, :], m[:, 2, :], ACT.Identity, scale=1.0 / D, bias=eps[:])\
                    .then_inc(chain_act, 1)
                act.wait_ge(chain_act, n + 1)
                nc.scalar.activation(r[:, 1, :], r[:, 0, :], ACT.Ln).then_inc(chain_act, 1)
                act.wait_ge(chain_act, n + 2)
                nc.scalar.activation(r[:, 2, :], r[:, 1, :], ACT.Exp, scale=-0.5).then_inc(chain_act, 1)

            def make_out(b, par, t):
                if t % 4 == 0:
                    act.wait_ge(ln2, b * LN2 + LN2)
                    act.wait_ge(router_sum, b * 10 + t + 4)
                    act.wait_ge(x1_out, b * 16 + 16)
                nc.scalar.activation(xr[:, par, t, :], xr[:, par, t, :], ACT.Identity, scale=r2[:, 7, t:t + 1],
                                     bias=r2[:, 6, t:t + 1]).then_inc(out_made, 1)

            def exp_decay(b, c, g):
                if has(b, 1) or c * GROUPS + g >= 2:
                    act.wait_ge(hid_ready, tile(b, c, g) - 1)
                if g == 0:
                    act.wait_ge(del_rep[c % 2], (b * (CHUNKS // 2) + c // 2 + 1) * 16 * NT)
                i = c * GROUPS + g
                nc.scalar.activation(decay[:, g % 2, :], delr[:, c % 2, :], ACT.Exp, scale=a_neg[:, i:i + 1])\
                    .then_inc(decay_ready, 1)

            def copy_dx(b, c):
                act.wait_ge(dx_rep[c % 2], (b * (CHUNKS // 2) + c // 2 + 1) * 16 * NT)
                if has(b, 1) or c >= 1:
                    act.wait_ge(inp_ready, inputs(b, c, 0))
                nc.scalar.activation(dx[:], dxr[:, c % 2, :], ACT.Copy).then_inc(dx_ready, 1)

            def copy_y(b, c):
                act.wait_ge(ch_summed, tile(b, c, GROUPS - 1) + 1)
                if has(b, 1) or c >= 1:
                    act.wait_ge(yt_ready, b * CHUNKS + c)
                nc.scalar.activation(ysb[:], ps_y[:, 0:2 * P], ACT.Copy).then_inc(ysb_ready, 1)

            nc.scalar.preload_act_table_set("natural_log_exp_and_others")
            act.wait_ge(consts_in, 16 * NCONST)
            nc.scalar.activation(a_neg[:], a_neg[:], ACT.Exp).then_inc(a_exp, 1)
            act.wait_ge(a_exp, 1)
            nc.scalar.mul(a_neg[:], a_neg[:], -1.0).then_inc(a_ready, 1)
            act.wait_ge(a_ready, 1)
            act.wait_ge(eps_ready, 1)
            ln1_sums(0, 0, range(17))
            for t in range(2):
                normalise(0, 0, t)
            for t in range(TC):
                copy_xhat(0, t)
                if t + 2 < TC:
                    normalise(0, 0, t + 2)
                normalise_again(0, 0, t)
            for h in range(2):
                copy_proj(0, h)
            for k in range(3):
                if k == 2:
                    copy_dx(0, 0)
                    for g in range(2):
                        exp_decay(0, 0, g)
                for h in range(2):
                    z_half(0, k, h)
                exp_log(0, k)

            def beside(b, par, c, place):
                at = (c, place)
                if c == Z3 and place == 1:
                    z_half(b, 3, 0)
                if c == Z3 and place == 3:
                    z_half(b, 3, 1)
                    exp_log(b, 3)
                if has(b, 1):
                    if at in SUMS2:
                        ln2_sums(b - 1, 1 - par, SUMS2[at])
                    for t in range(TC):
                        if MAKE_OUT[t] == at:
                            make_out(b - 1, 1 - par, t)
                if is_last(b):
                    return
                if at in SUMS1:
                    ln1_sums(b + 1, 1 - par, SUMS1[at])
                if at == (NORM1, 2):
                    for t in range(2):
                        normalise(b + 1, 1 - par, t)
                for t in range(TC):
                    if COPY_XHAT[t] == at:
                        copy_xhat(b + 1, t)
                        if t + 2 < TC:
                            normalise(b + 1, 1 - par, t + 2)
                for h in range(2):
                    if COPY_PROJ[h] == at:
                        copy_proj(b + 1, h)
                if c in Z and place == 1:
                    z_half(b + 1, Z.index(c), 0)
                if c in Z and place == 3:
                    z_half(b + 1, Z.index(c), 1)
                    exp_log(b + 1, Z.index(c))
                for t in range(TC):
                    if at == (SKIP[t] - 1, 3):
                        normalise_again(b + 1, 1 - par, t)

            def body(b, par):
                final = is_last(b)
                for c in range(CHUNKS):
                    nxt = (b, c + 1) if c < CHUNKS - 1 else (b + 1, 0)
                    beside(b, par, c, 0)
                    exp_decay(b, c, 2)
                    if c > 0:
                        copy_y(b, c - 1)
                    elif has(b, 1):
                        copy_y(b - 1, CHUNKS - 1)
                    exp_decay(b, c, 3)
                    if not (final and c == CHUNKS - 1):
                        copy_dx(*nxt)
                    beside(b, par, c, 1)
                    for g in (0, 1):
                        if not (final and c == CHUNKS - 1):
                            exp_decay(*nxt, g)
                        beside(b, par, c, 2 + g)

            batches(act, body)
            last = nb_run - 1
            copy_y(last, CHUNKS - 1)
            ln2_sums(last, 1, range(17))
            for t in range(TC):
                make_out(last, 1, t)

        @block.vector
        def _(dve):
            def newton(b, m, r, chain, chain_act, per):
                dve.wait_ge(chain_act, b * LN_ACT + LN_ACT)
                n = b * per
                nc.vector.tensor_tensor(r[:, 3, :], r[:, 2, :], r[:, 2, :], ALU.mult).then_inc(chain, 1)
                dve.wait_ge(chain, n + 1)
                nc.vector.tensor_tensor(r[:, 5, :], r[:, 3, :], r[:, 0, :], ALU.mult).then_inc(chain, 1)
                dve.wait_ge(chain, n + 2)
                nc.vector.tensor_scalar(r[:, 3, :], r[:, 5, :], -0.5, 1.5, ALU.mult, ALU.add).then_inc(chain, 1)
                dve.wait_ge(chain, n + 3)
                nc.vector.tensor_tensor(r[:, 4, :], r[:, 2, :], r[:, 3, :], ALU.mult).then_inc(chain, 1)
                dve.wait_ge(chain, n + 4)
                nc.vector.tensor_tensor(r[:, 6, :], m[:, 1, :], r[:, 4, :], ALU.mult).then_inc(chain, 1)

            def ln1_finish(b):
                if has(b, 1):
                    dve.wait_ge(xh_ready, b * TC)
                    dve.wait_ge(skip_step, b * 2 * TC)
                newton(b, m1, r1, ln1, ln1_act, LN1)

            def softplus(b, k, step):
                na = b * KD * ZACT + ZACT * k
                n = b * KD * ZSTEPS + ZSTEPS * k
                if step == 0:
                    dve.wait_ge(z_act, na + 4)
                    nc.vector.scalar_tensor_tensor(tu[:], tu[:], 1.0, te[:], ALU.subtract, ALU.subtract)\
                        .then_inc(z_dve, 1)
                    dve.wait_ge(z_act, na + 5)
                    dve.wait_ge(z_dve, n + 1)
                    nc.vector.tensor_tensor(delT[:, k, :], delT[:, k, :], tu[:], ALU.subtract).then_inc(z_dve, 1)
                elif step == 1:
                    dve.wait_ge(aux_emptied, b * NUSE + USE[("z", k, 1)] + 1)
                    dve.wait_ge(z_dve, n + 2)
                    nc.vector.tensor_tensor(delT[:, k, :], delT[:, k, :], dxT[:, k, :], ALU.add).then_inc(z_dve, 1)
                else:
                    dve.wait_ge(z_dve, n + 3)
                    nc.vector.tensor_tensor(dxT[:, k, :], delT[:, k, :], xhT[:, k, :], ALU.mult)\
                        .then_inc(dx_made[k], 1)

            def make_input(b, c, g):
                if g == 0:
                    dve.wait_ge(dx_ready, b * CHUNKS + c + 1)
                if c == 0:
                    dve.wait_ge(b_in[g], b * 16 + 16)
                if has(b, 1) or c > 0:
                    dve.wait_ge(hid_ready, tile(b, c, g) - GROUPS + 1)
                nc.vector.tensor_tensor(inp[:, g, :], dx[:], bmat[:, g, :], ALU.mult).then_inc(inp_ready, 1)

            def scan(b, c, g):
                dve.wait_ge(decay_ready, tile(b, c, g) + 1)
                if c - 1 in POOL_INPUT and g == GROUPS - 1:
                    dve.wait_ge(pool_input, b * len(POOL_INPUT) + POOL_INPUT.index(c - 1) + 1)
                else:
                    dve.wait_ge(inp_ready, inputs(b, c, g) + 1)
                if has(b, 1) or c > 0:
                    dve.wait_ge(ch_ready, tile(b, c, g) - GROUPS + 1)
                nc.vector.tensor_tensor_scan(hid[:, g, :], decay[:, g % 2, :], inp[:, g, :],
                                             0.0, ALU.mult, ALU.add).then_inc(hid_ready, 1)

            def add_y(b, par, c):
                dve.wait_ge(yt_ready, b * CHUNKS + c + 1)
                if c == 0:
                    dve.wait_ge(skip_step, b * 2 * TC + 2 * TC)
                x1 = xr[:, par, :, c * CH:(c + 1) * CH].rearrange("p (q t) d -> p t q d", t=2)
                y = ps_y[:, 2 * P:4 * P].rearrange("p (t q d) -> p t q d", t=2, q=4)
                nc.vector.tensor_tensor(x1, x1, y, ALU.add).then_inc(y_added, 1)

            def ln2_finish(b):
                if has(b, 1):
                    dve.wait_ge(out_made, b * TC)
                newton(b, m2, r2, ln2, ln2_act, LN2)
                nc.vector.tensor_scalar(r2[:, 7, :], r2[:, 4, :], 1.0, None, ALU.add).then_inc(ln2, 1)

            def router(b, par, h):
                for t in range(4 * h, 4 * h + 4):
                    if has(b, 1) or t > 0:
                        dve.wait_ge(router_sum, b * 10 + t)
                    nc.vector.scalar_tensor_tensor(junk[:], xr[:, par, t, :], m2[:, 1, t:t + 1], rw[:],
                                                   ALU.add, ALU.mult, accum_out=r2[:, 8, t:t + 1])\
                        .then_inc(router_sum, 1)
                if h == 0:
                    return
                dve.wait_ge(router_sum, b * 10 + TC)
                nc.vector.tensor_tensor(r2[:, 3, :], r2[:, 8, :], r2[:, 4, :], ALU.mult).then_inc(router_sum, 1)
                dve.wait_ge(router_sum, b * 10 + TC + 1)
                nc.vector.tensor_scalar(wcol[:, bass.ds(b * TC, TC)], r2[:, 3, :], rb[:, 0:1], None, ALU.add)\
                    .then_inc(router_sum, 1)

            nc.vector.memset(eps[:], EPS).then_inc(eps_ready, 1)
            dve.wait_ge(consts_in, 16 * NCONST)
            for k in range(KPE):
                nc.vector.tensor_scalar(dskip[:, k, :], ident[:], dcol[:, k:k + 1], None, ALU.mult)\
                    .then_inc(dskip_ready, 1)
            ln1_finish(0)
            for k in range(3):
                if k == 2:
                    for g in range(GROUPS):
                        make_input(0, 0, g)
                for step in range(3):
                    if k not in POOL_DX or step < 2:
                        if all((k, step) not in steps for steps in SOFTPLUS_NOW.values()):
                            softplus(0, k, step)

            def body(b, par):
                final = is_last(b)
                other = 1 - par
                for c in range(CHUNKS):
                    for g in range(GROUPS):
                        scan(b, c, g)
                        if g == SOFTPLUS_AFTER:
                            for k, step in SOFTPLUS_NOW.get(c, ()):
                                softplus(b, k, step)
                            for k, step in SOFTPLUS_NEXT.get(c, ()):
                                if not final:
                                    softplus(b + 1, k, step)
                        if g == YADD:
                            if c >= 1:
                                add_y(b, par, c - 1)
                            elif has(b, 1):
                                add_y(b - 1, other, CHUNKS - 1)
                    if has(b, 1):
                        if c == 2:
                            ln2_finish(b - 1)
                        if c in (2, 3):
                            router(b - 1, other, c - 2)
                    if not final:
                        if c == NORM1:
                            ln1_finish(b + 1)
                    for g in range(GROUPS):
                        if c in POOL_INPUT and g == GROUPS - 1:
                            continue
                        if c < CHUNKS - 1:
                            make_input(b, c + 1, g)
                        elif not final:
                            make_input(b + 1, 0, g)

            batches(dve, body)
            last = nb_run - 1
            add_y(last, 1, CHUNKS - 1)
            ln2_finish(last)
            for h in range(2):
                router(last, 1, h)
            dve.wait_ge(wt_ready, 1)
            nc.vector.tensor_copy(wrow[0:nb_run * TC], aux[0:nb_run * TC, 0:P]).then_inc(wrow_ready, 1)

        @block.gpsimd
        def _(pool):
            def skip_term(b, par, t):
                n = b * 2 * TC + 2 * t
                pool.wait_ge(xs_ready, b * TC + t + 1)
                nc.gpsimd.tensor_tensor(xs[:, t % 2, :], xs[:, t % 2, :], drow[:], ALU.mult).then_inc(skip_step, 1)
                pool.wait_ge(skip_step, n + 1)
                pool.wait_ge(xh_ready, b * TC + t + 1)
                nc.gpsimd.tensor_tensor(xr[:, par, t, SKIP_FROM:D], xr[:, par, t, SKIP_FROM:D], xs[:, t % 2, :], ALU.add)\
                    .then_inc(skip_step, 1)

            def make_input(b, c):
                pool.wait_ge(dx_rep[c % 2], (b * (CHUNKS // 2) + c // 2 + 1) * 16 * NT)
                pool.wait_ge(hid_ready, tile(b, c, 0))
                nc.gpsimd.tensor_tensor(inp[:, GROUPS - 1, :], dxr[:, c % 2, :], bmat[:, GROUPS - 1, :], ALU.mult)\
                    .then_inc(pool_input, 1)

            def multiply_dx(b, k):
                pool.wait_ge(z_dve, b * KD * ZSTEPS + ZSTEPS * k + 3)
                nc.gpsimd.tensor_tensor(dxT[:, k, :], delT[:, k, :], xhT[:, k, :], ALU.mult)\
                    .then_inc(dx_made[k], 1)

            def body(b, par):
                for c in range(CHUNKS):
                    for g in range(GROUPS):
                        pool.wait_ge(hid_ready, tile(b, c, g) + 1)
                        if c == 0:
                            pool.wait_ge(c_in[g], b * 16 + 16)
                        if has(b, 1) or c * GROUPS + g >= 2:
                            pool.wait_ge(ch_summed, tile(b, c, g) - 1)
                        nc.gpsimd.tensor_tensor(ch[:, g % 2, :], hid[:, g, :], cmat[:, g, :],
                                                ALU.mult).then_inc(ch_ready, 1)
                        for k, at in POOL_DX.items():
                            if at == (c, g):
                                multiply_dx(b, k)
                        if c in POOL_INPUT and g == 1:
                            make_input(b, c + 1)
                        for t in range(TC):
                            if not is_last(b) and SKIP[t] == c and g == 2 * (t % 2):
                                skip_term(b + 1, 1 - par, t)

            pool.wait_ge(consts_in, 16 * NCONST)
            for t in range(TC):
                skip_term(0, 0, t)
            batches(pool, body)


K = 128
KS = K - 1
H, HD, F = 16, 32, 2048
BM, SM = 4, 2048
LOWEST = -3.0e38
MAGIC = 12582912.0
TWO_PI_HI = 6.28125
TWO_PI_LO = 2 * np.pi - TWO_PI_HI

MLP = {"h2T", "up0", "up1", "up2", "up3", "gT0", "gT1", "gT2", "gT3", "down"}
AHEAD = ("hnT", "v")
BANK_USES = {
    "t0": ["up0", "up2", "GT0", "gT0", "gT2", "hnT", "v"],
    "t1": ["h2T", "up1", "up3", "GT1", "gT1", "gT3", "oT"],
    "m0": ["q", "qT", "mask", "o"],
    "m1": ["k", "kT", "down", "attn"],
    "s": ["scores", "aT"],
}
BANK_OF = {use: bank for bank, uses in BANK_USES.items() for use in uses}


def use_number(i, use):
    bank = BANK_OF[use]
    uses = BANK_USES[bank]
    ahead = len(AHEAD) if bank == "t0" else 0
    if isinstance(i, int) and i == -1:
        return AHEAD.index(use)
    if isinstance(i, int) and i == 0:
        return ahead + [u for u in uses if u not in MLP].index(use)
    skipped = sum(u in MLP for u in uses)
    if isinstance(i, int) and i == B:
        return i * len(uses) - skipped + [u for u in uses if u in MLP].index(use)
    return ahead + i * len(uses) - skipped + uses.index(use)


def ffn_phase(nc, semaphores, w_dram, x1_dram, out, mask, pos, wq, wk, wv, wo, w1, w2, ln1, ln2, ident_c, sel16_c, token_c,
              batch_c, inv_c):
    with ExitStack() as ctx:
        def sb(name, shape, dt=F32):
            return ctx.enter_context(nc.sbuf_tensor(name, shape, dt))

        def sem(name):
            return semaphores.enter_context(nc.semaphore(name))

        banks = {name: ctx.enter_context(nc.psum_tensor(f"ps_{name}", [P, n, HALF], F32))
                 for name, n in (("s", 4), ("t0", 1), ("t1", 1), ("m0", 1), ("m1", 1))}
        one = {name: banks[name][:, 0, :] for name in ("t0", "t1", "m0", "m1")}

        ident = sb("identf", [P, P])
        token = sb("token", [P, TC])
        batch = sb("batch", [B, 3])
        inv = sb("inv", [P, HD // 2])
        w_qkv = sb("w_qkv", [P, 3, KD, D])
        w_o = sb("w_o", [P, KD, D])
        w_1 = sb("w_1", [P, KD, F])
        w_2 = sb("w_2", [P, F // P, D])
        g1 = sb("g1", [P, KD])
        g2 = sb("g2", [P, KD])

        top = sb("top", [B, K])
        topi = sb("topi", [B, K], U32)
        rows_f = sb("rows_f", [B, 5, K])
        cols_i = sb("cols_i", [P, 3, B], U32)
        wsel = sb("wsel", [P, B])
        notsel = sb("notsel", [P, B])
        idx_bc = sb("idx_bc", [P, B, K])
        pos_i = sb("pos_i", [P, B], I32)
        pos_f = sb("pos_f", [P, B])
        cos = sb("cos", [P, B, HD // 2])
        sin = sb("sin", [P, B, HD // 2])

        idx_x = sb("idx_x", [P, 2, 1], U32)
        idx_m = sb("idx_m", [P, 2, 1], U32)
        idx_out = sb("idx_out", [P, 2, 1], U32)
        xg = sb("xg", [P, 2, D])
        rows_m = sb("rows_m", [P, L])
        xn = sb("xn", [P, 2, D])
        base = sb("base", [P, 2, D])
        hn = sb("hn", [P, D])
        hnT = sb("hnT", [P, KD, P])
        qk = sb("qk", [P, 2, D])
        rot = sb("rot", [P, D])
        vsb = sb("vsb", [P, 2, D])
        qkT = sb("qkT", [P, 2, KD, P])
        onehot = sb("onehot", [P, TC, K])
        GT = sb("GT", [P, TC, P])
        msel = sb("msel", [P, K])
        prob = sb("prob", [P, H, K])
        probT = sb("probT", [P, H, P])
        osb = sb("osb", [P, D])
        oT = sb("oT", [P, KD, P])
        x1f = sb("x1f", [P, 2, D])
        h2 = sb("h2", [P, 2, D])
        h2T = sb("h2T", [P, KD, P])
        act_up = sb("act_up", [P, F])
        gT = sb("gT", [P, F // P, P])
        row = sb("row", [P, 2, D])
        wts = act_up[0:B].rearrange("p (e t) -> p e t", e=2)
        sel16 = gT[0:B]
        ang = act_up[:, 0:4 * B * HD // 2].rearrange("p (e b f) -> p e b f", e=4, b=B)
        sq = sb("sq", [P, D], BF16)
        sq2 = sb("sq2", [P, D], BF16)
        st = sb("st", [P, 6])
        v1 = sb("v1", [P, 2, 24])
        mx = sb("mx", [P, 3, H])

        loaded = sem("loaded")
        wts_in = sem("wts_in")
        folded = sem("folded")
        topk = sem("topk")
        cols_full = sem("cols_full")
        cols_done = sem("cols_done")
        idxbc_full = sem("idxbc_full")
        pos_in = sem("pos_in")
        angle = sem("angle")
        full = {b: sem(f"full_{b}") for b in banks}
        free = {b: sem(f"free_{b}") for b in banks}
        idx_copied = sem("idx_copied")
        x_in = [sem("xg_even"), sem("xg_odd")]
        m_in = sem("m_in")
        scattered = [sem("scattered_even"), sem("scattered_odd")]
        norm = sem("norm")
        norm_act = sem("norm_act")
        norm2 = sem("norm2")
        norm2_act = sem("norm2_act")
        rope = sem("rope")
        onehot_ready = sem("onehot_ready")
        soft = sem("soft")
        exp_ready = sem("exp_ready")
        o_ready = sem("o_ready")
        row_ready = sem("row_ready")
        based = sem("based")
        gathering = sem("gathering")
        scattering = sem("scattering")

        SETUP_DMAS = 5
        WEIGHT_DMAS = 8

        def steps(eng, body):
            body(0, 0)
            body(1, 1)
            with eng.Fori(2, B - 3, 2) as i:
                body(i, 0)
                body(i + 1, 1)
            body(B - 2, 0)
            body(B - 1, 1)
            body(B, 0)

        def attention(i):
            return not (isinstance(i, int) and i == B)

        def final(i):
            return isinstance(i, int) and i == B - 1

        def mlp(i):
            return not (isinstance(i, int) and i == 0)

        def fill(pe, i, use):
            n = use_number(i, use)
            if not (isinstance(n, int) and n == 0):
                pe.wait_ge(free[BANK_OF[use]], n)

        def filled(eng, i, use):
            eng.wait_ge(full[BANK_OF[use]], use_number(i, use) + 1)
            return BANK_OF[use]

        block = ctx.enter_context(nc.Block())

        @block.sync
        def _(sp):
            sp.dma_start(wts[:, 0, :], w_dram).then_inc(wts_in, 16)
            for dst, src in ((ident[:], ident_c), (sel16[:], sel16_c), (token[:], token_c), (batch[:], batch_c),
                             (inv[:], inv_c)):
                sp.dma_start(dst, src).then_inc(loaded, 16)
            for dst, src in ((w_qkv[:, 0], wq), (w_qkv[:, 1], wk), (w_qkv[:, 2], wv), (g1[:], ln1), (w_o[:], wo),
                             (g2[:], ln2), (w_1[:], w1), (w_2[:], w2)):
                sp.dma_start(dst, src).then_inc(loaded, 16)

        @block.gpsimd
        def _(pool):
            def take_index(a, dst, j):
                nc.gpsimd.tensor_copy(dst, cols_i[:, j, bass.ds(a, 1)]).then_inc(idx_copied, 1)

            def gather_x(a, par):
                if has_batch(a, 2):
                    pool.wait_ge(x_in[par], (a - par) * 8)
                    pool.wait_ge(based, a - 1)
                take_index(a, idx_x[:, par], 0)
                pool.wait_ge(idx_copied, copied_before(a, "x") + 1)
                pool.sem_inc(gathering, 1)
                pool.indirect_dma_start(
                    out=xg[:, par, :], out_offset=None, in_=x1_dram,
                    in_offset=bass.IndirectOffsetOnAxis(ap=idx_x[:, par], axis=0)).then_inc(x_in[par], 16)

            def gather_mask(a, par):
                if has_batch(a, 1):
                    pool.wait_ge(m_in, a * 16)
                    pool.wait_ge(full["t1"], use_number(a - 1, "GT1") + 1)
                take_index(a, idx_m[:, par], 2)
                pool.wait_ge(idx_copied, copied_before(a, "mask") + 1)
                pool.sem_inc(gathering, 1)
                pool.indirect_dma_start(
                    out=rows_m[:], out_offset=None, in_=mask,
                    in_offset=bass.IndirectOffsetOnAxis(ap=idx_m[:, par], axis=0)).then_inc(m_in, 16)

            def scatter(m, pm):
                take_index(m, idx_out[:, pm], 0)
                pool.wait_ge(idx_copied, copied_before(m, "out") + 1)
                pool.wait_ge(row_ready, m + 1)
                pool.sem_inc(scattering, 1)
                pool.indirect_dma_start(
                    out=out, out_offset=bass.IndirectOffsetOnAxis(ap=idx_out[0:KS, pm], axis=0),
                    in_=row[0:KS, pm, :], in_offset=None).then_inc(scattered[pm], 16)
                pool.wait_ge(scattered[pm], (m - pm) * 8 + 16)

            def copied_before(a, which):
                if which == "out":
                    i = a + 1
                    if isinstance(i, int) and i >= B - 1:
                        return 3 * (B - 1) + 1 + i - (B - 1)
                    return 3 * i + 1 + 2
                at = ("x", "mask").index(which)
                if isinstance(a, int) and a <= 1:
                    return 2 * a + at
                return 3 * (a - 1) + 1 + at

            def has_batch(a, least):
                return not isinstance(a, int) or a >= least

            def body(i, par):
                if not (isinstance(i, int) and i >= B - 1):
                    gather_x(i + 1, 1 - par)
                    gather_mask(i + 1, 1 - par)
                if mlp(i):
                    scatter(i - 1, 1 - par)

            pool.wait_ge(cols_done, 5)
            gather_x(0, 0)
            gather_mask(0, 0)
            for b in range(B):
                pool.indirect_dma_start(
                    out=pos_i[:, b:b + 1], out_offset=None, in_=pos,
                    in_offset=bass.IndirectOffsetOnAxis(ap=cols_i[:, 1, b:b + 1], axis=0),
                ).then_inc(pos_in, 16)
            steps(pool, body)

        @block.tensor
        def _(pe):
            pe.wait_ge(loaded, 16 * (SETUP_DMAS + WEIGHT_DMAS))
            pe.wait_ge(topk, TOPK)
            for j in range(4):
                last = pe.transpose(one["t0"][:, j * B:(j + 1) * B], rows_f[:, j, :], ident[0:B, 0:B])
            last = pe.transpose(one["t0"][:, 4 * B:5 * B], top[:], ident[0:B, 0:B])
            last.then_inc(cols_full, 1)
            for b in range(B):
                last = pe.matmul(banks["s"][:, b // 4, (b % 4) * K:(b % 4 + 1) * K], sel16[:, b, :],
                                 rows_f[:, 4, :], start=True, stop=True)
            last.then_inc(idxbc_full, 1)
            def turn(bank, src, n=KD):
                for k in range(n):
                    last = pe.transpose(one[bank][:, k * P:(k + 1) * P], src[:, k * P:(k + 1) * P], ident[:])
                last.then_inc(full[bank], 1)

            def product(bank, xT, w, n):
                for k in range(n):
                    last = pe.matmul(one[bank], xT[:, k, :], w(k), start=(k == 0), stop=(k == n - 1))
                last.then_inc(full[bank], 1)

            def turn_hn(i):
                pe.wait_ge(norm, (i + 1) * NORM + NORM)
                fill(pe, i, "hnT")
                turn("t0", hn)

            def values(i, ks=range(KD)):
                if 0 in ks:
                    pe.wait_ge(free["t0"], use_number(i, "hnT") + 1)
                    fill(pe, i, "v")
                for k in ks:
                    last = pe.matmul(one["t0"], hnT[:, k, :], w_qkv[:, 2, k, :], start=(k == 0), stop=(k == KD - 1))
                if KD - 1 in ks:
                    last.then_inc(full["t0"], 1)

            def down(i, j):
                pe.wait_ge(free[BANK_OF[f"gT{j}"]], use_number(i, f"gT{j}") + 1)
                for k in range(4 * j, 4 * j + 4):
                    last = pe.matmul(one["m1"], gT[:, k, :], w_2[:, k, :], start=(k == 0), stop=(k == F // P - 1))
                if j == 3:
                    last.then_inc(full["m1"], 1)

            pe.wait_ge(folded, FOLDED)
            pe.wait_ge(cols_done, 5)
            turn_hn(-1)
            values(-1)
            pe.wait_ge(cols_done, 6)

            def body(i, par):
                a, m, pm = i, i - 1, 1 - par
                if attention(i):
                    for j, use in enumerate(("q", "k")):
                        fill(pe, i, use)
                        product(BANK_OF[use], hnT, lambda k, j=j: w_qkv[:, j, k, :], KD)
                if mlp(i):
                    pe.wait_ge(norm2, m * NORM2 + NORM2)
                    fill(pe, i, "h2T")
                    turn("t1", h2[:, pm, :])
                    pe.wait_ge(free["t1"], use_number(i, "h2T") + 1)
                    for j in range(4):
                        fill(pe, i, f"up{j}")
                        product(BANK_OF[f"up{j}"], h2T, lambda k, j=j: w_1[:, k, j * HALF:(j + 1) * HALF], KD)
                if attention(i):
                    pe.wait_ge(m_in, a * 16 + 16)
                    for n in range(2):
                        fill(pe, i, f"GT{n}")
                        turn(BANK_OF[f"GT{n}"], rows_m[:, n * HALF:(n + 1) * HALF])
                    for j, use in enumerate(("qT", "kT")):
                        pe.wait_ge(rope, a * ROPE + 6 * (j + 1))
                        fill(pe, i, use)
                        turn(BANK_OF[use], qk[:, j, :])
                    for n in range(2):
                        pe.wait_ge(free[BANK_OF[f"GT{n}"]], use_number(i, f"GT{n}") + 1)
                    pe.wait_ge(onehot_ready, a + 1)
                    fill(pe, i, "mask")
                    for t in range(TC):
                        last = pe.matmul(one["m0"][:, 0:K], GT[:, t, :], onehot[:, t, :],
                                         start=(t == 0), stop=(t == TC - 1))
                    last.then_inc(full["m0"], 1)
                    pe.wait_ge(free["m0"], use_number(i, "qT") + 1)
                    pe.wait_ge(free["m1"], use_number(i, "kT") + 1)
                    fill(pe, i, "scores")
                    for k in range(KD):
                        for j in range(4):
                            last = pe.matmul(banks["s"][:, j, k * K:k * K + KS], qkT[j * HD:(j + 1) * HD, 0, k, :],
                                             qkT[j * HD:(j + 1) * HD, 1, k, 0:KS], start=True, stop=True)
                    last.then_inc(full["s"], 1)
                if mlp(i):
                    for j in range(4):
                        bank = BANK_OF[f"up{j}"]
                        pe.wait_ge(free[bank], use_number(i, f"up{j}") + 1)
                        fill(pe, i, f"gT{j}")
                        turn(BANK_OF[f"gT{j}"], act_up[:, j * HALF:(j + 1) * HALF])
                    fill(pe, i, "down")
                    for j in range(3):
                        down(i, j)
                if attention(i):
                    pe.wait_ge(exp_ready, a + 1)
                    fill(pe, i, "aT")
                    for h in range(H):
                        last = pe.transpose(banks["s"][0:KS, h // 4, (h % 4) * P:(h % 4 + 1) * P], prob[:, h, 0:KS],
                                            ident[:])
                    last.then_inc(full["s"], 1)
                    if not final(i):
                        turn_hn(i)
                if mlp(i):
                    down(i, 3)
                if attention(i):
                    pe.wait_ge(free["s"], use_number(i, "aT") + 1)
                    pe.wait_ge(o_ready, a * 2 + 1)
                    pe.wait_ge(free["t0"], use_number(i - 1, "v") + 1)
                    fill(pe, i, "o")
                    for h in range(H):
                        hd = 4 * (h % 4) + h // 4
                        last = pe.matmul(one["m0"][:, hd * HD:(hd + 1) * HD], probT[0:KS, h, :],
                                         vsb[0:KS, par, hd * HD:(hd + 1) * HD], start=True, stop=True)
                    last.then_inc(full["m0"], 1)
                    if not final(i):
                        values(i, range(0, 2))
                    pe.wait_ge(o_ready, a * 2 + 2)
                    fill(pe, i, "oT")
                    turn("t1", osb)
                    if not final(i):
                        values(i, range(2, KD))
                    pe.wait_ge(free["t1"], use_number(i, "oT") + 1)
                    fill(pe, i, "attn")
                    product("m1", oT, lambda k: w_o[:, k, :], KD)

            steps(pe, body)

        @block.scalar
        def _(act):
            act.wait_ge(loaded, 16 * (SETUP_DMAS + WEIGHT_DMAS))
            for j in range(3):
                for k in range(KD):
                    nc.scalar.activation(w_qkv[:, j, k, :], w_qkv[:, j, k, :], ACT.Copy, scale=g1[:, k:k + 1])\
                        .then_inc(folded, 1)
            for k in range(KD):
                nc.scalar.activation(w_1[:, k, :], w_1[:, k, :], ACT.Copy, scale=g2[:, k:k + 1]).then_inc(folded, 1)

            def copy(i, use, dst, rows=P):
                bank = filled(act, i, use)
                nc.scalar.activation(dst, one[bank][0:rows].rearrange("p (k t) -> p k t", t=P) if dst.ndim == 3
                                     else one[bank][0:rows], ACT.Copy).then_inc(free[bank], 1)

            def inverse_root(chain, n, chain_act, na, var, spare, root):
                act.wait_ge(chain, n)
                nc.scalar.activation(spare, var, ACT.Ln).then_inc(chain_act, 1)
                act.wait_ge(chain_act, na + 1)
                nc.scalar.activation(root, spare, ACT.Exp, scale=-0.5).then_inc(chain_act, 1)

            def prepare(a, par):
                v = v1[:, par, :]
                inverse_root(norm, a * NORM + 8, norm_act, a * 5, v[:, 0:1], v[:, 7:8], v[:, 2:3])
                act.wait_ge(norm, a * NORM + 13)
                if not (isinstance(a, int) and a == 0):
                    act.wait_ge(norm_act, a * 5)
                nc.scalar.activation(sq[:], xn[:, par, :], ACT.Square, accum_out=v[:, 8:9]).then_inc(norm_act, 1)
                inverse_root(norm, a * NORM + 14, norm_act, a * 5 + 3, v[:, 9:10], v[:, 10:11], v[:, 11:12])

            nc.scalar.preload_act_table_set("natural_log_exp_and_others")
            prepare(0, 0)

            def copy_ahead(i, par):
                if not (isinstance(i, int) and i == -1):
                    act.wait_ge(full["m1"], use_number(i, "k") + 1)
                copy(i, "hnT", hnT[:])

            def copy_v(i, par):
                if not (isinstance(i, int) and i <= 0):
                    act.wait_ge(full["m0"], use_number(i - 1, "o") + 1)
                copy(i, "v", vsb[:, par, :])

            copy_ahead(-1, 0)
            copy_v(-1, 0)
            act.wait_ge(angle, ANGLE)
            nc.scalar.activation(sin[:], ang[:, 0], ACT.Sin).then_inc(angle, 1)
            nc.scalar.activation(cos[:], ang[:, 1], ACT.Sin).then_inc(angle, 1)

            def body(i, par):
                a, m, pm = i, i - 1, 1 - par
                if mlp(i):
                    copy(i, "h2T", h2T[:])
                if mlp(i):
                    for j in range(4):
                        bank = filled(act, i, f"up{j}")
                        nc.scalar.activation(act_up[:, j * HALF:(j + 1) * HALF], one[bank],
                                             ACT.Gelu_apprx_tanh).then_inc(free[bank], 1)
                if attention(i):
                    copy(i, "qT", qkT[:, 0])
                    copy(i, "kT", qkT[:, 1])
                if mlp(i):
                    for j in range(4):
                        copy(i, f"gT{j}", gT[:, 4 * j:4 * j + 4, :])
                if attention(i):
                    nc.scalar.preload_act_table_set("natural_log_exp_and_others")
                    act.wait_ge(soft, a * SOFT + 2)
                    nc.scalar.activation(prob[:, :, 0:KS], prob[:, :, 0:KS], ACT.Exp).then_inc(exp_ready, 1)
                    if not final(i):
                        prepare(i + 1, pm)
                    act.wait_ge(full["s"], use_number(i, "aT") + 1)
                    nc.scalar.activation(probT[0:KS, 0:8, :],
                                         banks["s"][0:KS, 0:2, :].rearrange("p j (k t) -> p (j k) t", t=P),
                                         ACT.Copy).then_inc(free["s"], 1)
                    if not final(i):
                        copy_ahead(i, pm)
                        copy_v(i, pm)
                    copy(i, "oT", oT[:])
                    v = v1[:, par, :]
                    act.wait_ge(norm2, a * NORM2 + 1)
                    nc.scalar.activation(sq2[:], x1f[:, par, :], ACT.Square, accum_out=v[:, 16:17])\
                        .then_inc(norm2_act, 1)
                    inverse_root(norm2, a * NORM2 + 2, norm2_act, a * 3 + 1, v[:, 17:18], v[:, 18:19], v[:, 19:20])

            steps(act, body)

        @block.vector
        def _(dve):
            V = nc.vector
            chain = [0]

            def link(ins):
                chain[0] += 1
                ins.then_inc(topk, 1)
                dve.wait_ge(topk, chain[0])

            dve.wait_ge(wts_in, 16)
            for r in range(K // 8):
                now, then = wts[:, r % 2, :], wts[:, 1 - r % 2, :]
                eight = slice(8 * r, 8 * r + 8)
                link(V.max(top[:, eight], now))
                link(V.max_index(topi[:, eight], top[:, eight], now))
                link(V.match_replace(then, top[:, eight], now, LOWEST))
            link(V.tensor_copy(rows_f[:, 4, :], topi[:]))
            dve.wait_ge(loaded, 16 * (SETUP_DMAS + WEIGHT_DMAS))
            for j, scale in enumerate((1.0, 1.0, 2.0)):
                link(V.tensor_scalar(rows_f[:, j, :], rows_f[:, 4, :], scale, batch[:, j:j + 1], ALU.mult, ALU.add))
            link(V.tensor_scalar(rows_f[:, 3, :], top[:], top[:, K - 1:K], None, ALU.is_le))
            assert chain[0] == TOPK
            dve.wait_ge(cols_full, 1)
            t0 = one["t0"]
            for j in range(3):
                V.tensor_copy(cols_i[:, j, :], t0[:, j * B:(j + 1) * B]).then_inc(cols_done, 1)
            V.tensor_copy(notsel[:], t0[:, 3 * B:4 * B]).then_inc(cols_done, 1)
            V.tensor_copy(wsel[:], t0[:, 4 * B:5 * B]).then_inc(cols_done, 1)
            def newton(sem_, at, r0, v, t, u, r):
                V.tensor_tensor(t, r0, r0, ALU.mult).then_inc(sem_, 1)
                dve.wait_ge(sem_, at + 1)
                V.tensor_tensor(u, t, v, ALU.mult).then_inc(sem_, 1)
                dve.wait_ge(sem_, at + 2)
                V.tensor_scalar(t, u, -0.5, 1.5, ALU.mult, ALU.add).then_inc(sem_, 1)
                dve.wait_ge(sem_, at + 3)
                V.tensor_tensor(r, r0, t, ALU.mult).then_inc(sem_, 1)
                dve.wait_ge(sem_, at + 4)

            def prepare(a, par):
                v = v1[:, par, :]
                at = a * NORM
                c = lambda j: v[:, j:j + 1]
                dve.wait_ge(x_in[par], (a - par) * 8 + 16)
                if not (isinstance(a, int) and a == 0):
                    dve.wait_ge(full["t0"], use_number(a - 2, "hnT") + 1)
                if not (isinstance(a, int) and a <= 1):
                    dve.wait_ge(norm2, (a - 2) * NORM2 + 1)
                V.bn_stats(st[:], xg[:, par, :]).then_inc(norm, 1)
                dve.wait_ge(norm, at + 1)
                V.tensor_tensor(c(3), st[:, 1:2], st[:, 4:5], ALU.add).then_inc(norm, 1)
                V.tensor_tensor(c(4), st[:, 1:2], st[:, 4:5], ALU.subtract).then_inc(norm, 1)
                V.tensor_tensor(c(5), st[:, 2:3], st[:, 5:6], ALU.add).then_inc(norm, 1)
                dve.wait_ge(norm, at + 4)
                V.tensor_scalar(c(1), c(3), 0.5, None, ALU.mult).then_inc(norm, 1)
                V.tensor_tensor(c(6), c(4), c(4), ALU.mult).then_inc(norm, 1)
                V.tensor_scalar(c(5), c(5), 1.0 / D, EPS, ALU.mult, ALU.add).then_inc(norm, 1)
                dve.wait_ge(norm, at + 7)
                V.scalar_tensor_tensor(c(0), c(6), 0.25, c(5), ALU.mult, ALU.add).then_inc(norm, 1)
                dve.wait_ge(norm_act, a * 5 + 2)
                newton(norm, at + 8, c(2), c(0), c(3), c(4), c(6))
                V.tensor_scalar(xn[:, par, :], xg[:, par, :], c(1), c(6), ALU.subtract, ALU.mult).then_inc(norm, 1)
                dve.wait_ge(norm_act, a * 5 + 3)
                V.tensor_scalar(c(9), c(8), 1.0 / D, 1e-6, ALU.mult, ALU.add).then_inc(norm, 1)
                dve.wait_ge(norm_act, a * 5 + 5)
                dve.wait_ge(norm, at + 14)
                newton(norm, at + 14, c(11), c(9), c(12), c(13), c(14))
                V.tensor_scalar(hn[:], xn[:, par, :], c(14), None, ALU.mult).then_inc(norm, 1)

            def make_base(a, par):
                if not (isinstance(a, int) and a <= 1):
                    dve.wait_ge(row_ready, a - 1)
                V.scalar_tensor_tensor(base[:, par, :], xn[:, par, :], notsel[:, bass.ds(a, 1)], xg[:, par, :],
                                       ALU.mult, ALU.add).then_inc(based, 1)

            dve.wait_ge(cols_done, 5)
            prepare(0, 0)
            make_base(0, 0)
            dve.wait_ge(idxbc_full, 1)
            V.tensor_copy(idx_bc[:].rearrange("p b k -> p (b k)"),
                          banks["s"][:].rearrange("p j k -> p (j k)")).then_inc(cols_done, 1)
            dve.wait_ge(cols_done, 6)
            n = [0]

            def angle_step(ins):
                n[0] += 1
                ins.then_inc(angle, 1)
                dve.wait_ge(angle, n[0])

            dve.wait_ge(pos_in, 16 * B)
            angle_step(V.tensor_copy(pos_f[:], pos_i[:]))
            f3 = [P, B, HD // 2]
            angle_step(V.tensor_tensor(ang[:, 2], pos_f[:].unsqueeze(2).to_broadcast(f3),
                                       inv[:].unsqueeze(1).to_broadcast(f3), ALU.mult))
            angle_step(V.tensor_scalar(ang[:, 3], ang[:, 2], float(1 / (2 * np.pi)), MAGIC, ALU.mult, ALU.add))
            angle_step(V.tensor_scalar(ang[:, 1], ang[:, 3], MAGIC, None, ALU.subtract))
            angle_step(V.scalar_tensor_tensor(ang[:, 3], ang[:, 1], -TWO_PI_HI, ang[:, 2], ALU.mult, ALU.add))
            angle_step(V.scalar_tensor_tensor(ang[:, 2], ang[:, 1], -TWO_PI_LO, ang[:, 3], ALU.mult, ALU.add))
            angle_step(V.tensor_scalar(ang[:, 0], ang[:, 2], 3.1415925, -3.1415925, ALU.min, ALU.max))
            angle_step(V.scalar_tensor_tensor(ang[:, 3], ang[:, 0], -1.0, ang[:, 0], ALU.mult, ALU.max))
            angle_step(V.tensor_scalar(ang[:, 1], ang[:, 3], -1.0, float(np.pi / 2), ALU.mult, ALU.add))
            assert n[0] == ANGLE

            dve.wait_ge(angle, ANGLE + 2)

            def one_hot(a):
                if not (isinstance(a, int) and a == 0):
                    dve.wait_ge(full["m0"], use_number(a - 1, "mask") + 1)
                V.tensor_tensor(onehot[:], idx_bc[:, bass.ds(a, 1), :].to_broadcast([P, TC, K]),
                                token[:].unsqueeze(2).to_broadcast([P, TC, K]), ALU.is_equal)\
                 .then_inc(onehot_ready, 1)

            def rotate(i, j):
                bank = filled(dve, i, ("q", "k")[j])
                at = i * ROPE + 6 * j
                x = one[bank].rearrange("p (h e f) -> p h e f", h=H, e=2)
                r = rot[:].rearrange("p (h e f) -> p h e f", h=H, e=2)
                y = qk[:, j, :].rearrange("p (h e f) -> p h e f", h=H, e=2)
                s3 = [P, H, HD // 2]
                c = cos[:, bass.ds(i, 1), :].to_broadcast(s3)
                s = sin[:, bass.ds(i, 1), :].to_broadcast(s3)
                if not (isinstance(i, int) and i == 0):
                    dve.wait_ge(full[("m0", "m1")[j]], use_number(i - 1, ("qT", "kT")[j]) + 1)
                if not (isinstance(i, int) and i == 0 and j == 0):
                    dve.wait_ge(rope, at)
                V.tensor_tensor(y[:, :, 0, :], x[:, :, 0, :], c, ALU.mult).then_inc(rope, 1)
                V.tensor_tensor(r[:, :, 0, :], x[:, :, 1, :], s, ALU.mult).then_inc(rope, 1)
                V.tensor_tensor(y[:, :, 1, :], x[:, :, 1, :], c, ALU.mult).then_inc(rope, 1)
                V.tensor_tensor(r[:, :, 1, :], x[:, :, 0, :], s, ALU.mult).then_inc(rope, 1)
                dve.wait_ge(rope, at + 4)
                V.tensor_tensor(y[:, :, 0, :], y[:, :, 0, :], r[:, :, 0, :], ALU.subtract).then_inc(rope, 1)
                V.tensor_tensor(y[:, :, 1, :], y[:, :, 1, :], r[:, :, 1, :], ALU.add).then_inc(rope, 1)

            def body(i, par):
                a, m, pm = i, i - 1, 1 - par
                if attention(i):
                    for j, use in enumerate(("q", "k")):
                        rotate(i, j)
                        dve.wait_ge(rope, i * ROPE + 6 * j + 4)
                        dve.sem_inc(free[BANK_OF[use]], 1)
                    one_hot(a)
                    for n in range(2):
                        bank = filled(dve, i, f"GT{n}")
                        V.tensor_scalar(GT[:, 4 * n:4 * n + 4, :], one[bank].rearrange("p (k t) -> p k t", t=P),
                                        LOWEST, None, ALU.max).then_inc(free[bank], 1)
                    bank = filled(dve, i, "mask")
                    if not (isinstance(i, int) and i == 0):
                        dve.wait_ge(soft, a * SOFT)
                    V.tensor_copy(msel[:], one[bank][:, 0:K]).then_inc(free[bank], 1)
                    filled(dve, i, "scores")
                    dve.wait_ge(free[bank], use_number(i, "mask") + 1)
                    if not (isinstance(i, int) and i == 0):
                        dve.wait_ge(full["s"], use_number(i - 1, "aT") + 1)
                    at = a * SOFT
                    p3 = prob[:, :, 0:KS]
                    s3 = banks["s"][:].rearrange("p j (k t) -> p (j k) t", t=K)[:, :, 0:KS]
                    V.scalar_tensor_tensor(p3, s3, float(1 / np.sqrt(np.float32(HD))),
                                           msel[:, 0:KS].unsqueeze(1).to_broadcast([P, H, KS]), ALU.mult, ALU.add)\
                     .then_inc(free["s"], 1)
                    dve.wait_ge(free["s"], use_number(i, "scores") + 1)
                    V.tensor_reduce(mx[:, 0, :], p3, AX.X, ALU.max).then_inc(soft, 1)
                    dve.wait_ge(soft, at + 1)
                    V.tensor_tensor(p3, p3, mx[:, 0, :].unsqueeze(2).to_broadcast([P, H, KS]), ALU.subtract)\
                     .then_inc(soft, 1)
                    if not final(i):
                        prepare(i + 1, pm)
                if attention(i):
                    at = a * SOFT
                    dve.wait_ge(full["s"], use_number(i, "aT") + 1)
                    V.tensor_copy(probT[0:KS, 8:16, :],
                                  banks["s"][0:KS, 2:4, :].rearrange("p j (k t) -> p (j k) t", t=P))\
                     .then_inc(o_ready, 1)
                    dve.wait_ge(exp_ready, a + 1)
                    V.tensor_reduce(mx[:, 1, :], prob[:, :, 0:KS], AX.X, ALU.add).then_inc(soft, 1)
                    dve.wait_ge(soft, at + 3)
                    V.reciprocal(mx[:, 2, :], mx[:, 1, :]).then_inc(soft, 1)
                    bank = filled(dve, i, "o")
                    dve.wait_ge(soft, at + 4)
                    V.tensor_tensor(osb[:].rearrange("p (k j e) -> p k j e", k=4, j=4),
                                    one[bank].rearrange("p (k j e) -> p k j e", k=4, j=4),
                                    mx[:, 2, :].rearrange("p (j k) -> p k j", j=4).unsqueeze(3)
                                    .to_broadcast([P, 4, 4, HD]), ALU.mult).then_inc(o_ready, 1)
                    dve.wait_ge(o_ready, a * 2 + 2)
                    dve.sem_inc(free[bank], 1)
                if mlp(i):
                    bank = filled(dve, i, "down")
                    V.tensor_tensor(x1f[:, pm, :], one[bank], x1f[:, pm, :], ALU.add).then_inc(free[bank], 1)
                    dve.wait_ge(free[bank], use_number(i, "down") + 1)
                    if not (isinstance(i, int) and i < 3):
                        dve.wait_ge(scattered[pm], (m - pm) * 8)
                    dve.wait_ge(based, m + 1)
                    V.scalar_tensor_tensor(row[:, pm, :], x1f[:, pm, :], wsel[:, bass.ds(m, 1)], base[:, pm, :],
                                           ALU.mult, ALU.add).then_inc(row_ready, 1)
                if attention(i):
                    if not final(i):
                        make_base(i + 1, pm)
                    bank = filled(dve, i, "attn")
                    v = v1[:, par, :]
                    n2 = a * NORM2
                    V.tensor_tensor(x1f[:, par, :], one[bank], xn[:, par, :], ALU.add).then_inc(norm2, 1)
                    dve.wait_ge(norm2, n2 + 1)
                    dve.sem_inc(free[bank], 1)
                    dve.wait_ge(norm2_act, a * 3 + 1)
                    V.tensor_scalar(v[:, 17:18], v[:, 16:17], 1.0 / D, 1e-6, ALU.mult, ALU.add).then_inc(norm2, 1)
                    dve.wait_ge(norm2_act, a * 3 + 3)
                    newton(norm2, n2 + 2, v[:, 19:20], v[:, 17:18], v[:, 20:21], v[:, 21:22], v[:, 22:23])
                    V.tensor_scalar(h2[:, par, :], x1f[:, par, :], v[:, 22:23], None, ALU.mult).then_inc(norm2, 1)

            steps(dve, body)


NORM = 19
NORM2 = 7
ROPE = 12
SOFT = 4
TOPK = 3 * (K // 8) + 5
ANGLE = 9
FOLDED = 3 * KD + KD


def layernorm_scan_and_chosen_tokens(nc, a, out, x1_dram, w_dram, bc_dram):
    with ExitStack() as semaphores:
        scan_phase(nc, semaphores, a["x"], a["A_log"], a["w_xproj"], a["w_dt"], a["dt_b"], a["D_row"], a["D_col"],
                   a["router_w"], a["router_b"], a["ident"], a["state_sum"], bc_dram, x1_dram, w_dram, out)
        ffn_phase(nc, semaphores, w_dram, x1_dram.rearrange("b l d -> (b l) d"), out.rearrange("b l d -> (b l) d"),
                  a["mask"], a["pos"], a["wq"], a["wk"], a["wv"], a["wo"], a["w1"], a["w2"], a["ln1"], a["ln2"],
                  a["ident"], a["batch_rows"], a["token"], a["batch_first"], a["inv_freq"])


def shape_constants(np):
    m = np.arange(P)
    batch_rows = np.zeros((B, B, P), np.float32)
    batch_rows[np.arange(B), np.arange(B)] = 1
    b = np.arange(B)
    bm = np.minimum(b, BM - 1)
    inv = 1.0 / np.float32(10000.0) ** (np.arange(0, HD, 2, dtype=np.float32) / np.float32(HD))
    return {
        "ident": np.eye(P, dtype=np.float32),
        "state_sum": (m[:, None] % CH == np.arange(CH)[None]).astype(np.float32),
        "batch_rows": batch_rows,
        "token": (m[:, None] + P * np.arange(TC)[None]).astype(np.float32),
        "batch_first": np.stack([b * L, bm * SM, bm * SM * (SM // L)], 1).astype(np.float32),
        "inv_freq": np.broadcast_to(inv.astype(np.float32), (P, HD // 2)),
    }


def kernel(**inputs):
    import numpy as np
    import concourse.bacc as bacc
    from concourse import mybir
    from concourse.bass_utils import run_bass_kernel_spmd

    i = {k: np.asarray(v) for k, v in inputs.items()}

    def rows(w):
        return w.reshape(-1, P, w.shape[1]).transpose(1, 0, 2)

    arrays = {
        "x": i["L0_attn_x"],
        "A_log": i["L0_attn_A_log"].reshape(CHUNKS, CH, GROUPS, NT).transpose(3, 1, 0, 2).reshape(P, TILES),
        "w_xproj": rows(i["L0_attn_x_proj_w"].T),
        "w_dt": i["L0_attn_dt_proj_w"].T,
        "dt_b": i["L0_attn_dt_proj_b"].reshape(KD, P).T,
        "D_row": np.broadcast_to(i["L0_attn_D"], (P, D)),
        "D_col": i["L0_attn_D"].reshape(KD, P).T,
        "router_w": np.broadcast_to(i["L0_ffn_router_w"].reshape(1, D), (P, D)),
        "router_b": np.broadcast_to(i["L0_ffn_router_b"].reshape(1, 1), (P, 1)),
        "mask": i["L0_ffn_attention_mask"].reshape(-1, L),
        "pos": i["L0_ffn_position_ids"].reshape(-1, 1),
        "ln1": i["L0_ffn_ln1"].reshape(KD, P).T,
        "ln2": i["L0_ffn_ln2"].reshape(KD, P).T,
    }
    for name in ("wq", "wk", "wv", "wo", "w1", "w2"):
        arrays[name] = rows(i[f"L0_ffn_{name}"])
    arrays.update(shape_constants(np))
    arrays = {k: np.ascontiguousarray(v) for k, v in arrays.items()}

    nc = bacc.Bacc("TRN2", target_bir_lowering=False, num_devices=1)
    a = {k: nc.dram_tensor(f"in_{k}", v.shape, mybir.dt.from_np(v.dtype), kind="ExternalInput").ap()
         for k, v in arrays.items()}
    out = nc.dram_tensor("out_rows", (B, L, D), mybir.dt.float32, kind="ExternalOutput").ap()
    x1 = nc.dram_tensor("x1_rows", (B, L, D), mybir.dt.float32, kind="Internal").ap()
    w = nc.dram_tensor("router_weights", (B, L), mybir.dt.float32, kind="Internal").ap()
    bc = nc.dram_tensor("b_and_c", (2 * N, L), mybir.dt.float32, kind="Internal").ap()
    layernorm_scan_and_chosen_tokens(nc, a, out, x1, w, bc)
    r = run_bass_kernel_spmd(nc, [{f"in_{k}": v for k, v in arrays.items()}], core_ids=[0])
    return r.results[0]["out_rows"]
```
